# Optimizing a Trainium2 kernel written in Bass

```python
import numpy as np
import jax
import jax.numpy as jnp

def _softmax(x, axis=-1):
    return jax.nn.softmax(x, axis=axis)

def _gelu(x):
    return jax.nn.gelu(x, approximate=True)

def _silu(x):
    return jax.nn.silu(x)

def _sigmoid(x):
    return jax.nn.sigmoid(x)

def _layernorm(x, axis=-1, eps=1e-05):
    m = jnp.mean(x, axis=axis, keepdims=True)
    v = jnp.var(x, axis=axis, keepdims=True)
    return (x - m) / jnp.sqrt(v + eps)

def _scatter_add(tgt, idx, src, axis=0):
    return tgt.at[idx].add(src)

def _segment_sum(src, seg, n):
    return jax.ops.segment_sum(src, seg, n)
kernel_name = 'mk_sandwich_d2_jaxref_r8_1a3faf'

def setup_inputs(seed: int=0):
    np.random.seed(seed)
    _w = jnp.asarray

    def _L0_attn_setup():
        import jax, jax.numpy as jnp
        import numpy as np
        D_MODEL = 128
        NUM_HEADS = 16
        D_K = D_MODEL // NUM_HEADS
        BATCH, SEQ = (2, 256)
        key = jax.random.key(seed)
        k = jax.random.split(key, 5)
        std = np.sqrt(2.0 / (D_MODEL + D_MODEL)).astype(np.float32)
        return {'x': jax.random.normal(k[0], (BATCH, SEQ, D_MODEL), dtype=jnp.float32), 'WQ': jax.random.normal(k[1], (D_MODEL, D_MODEL), dtype=jnp.float32) * std, 'WK': jax.random.normal(k[2], (D_MODEL, D_MODEL), dtype=jnp.float32) * std, 'WV': jax.random.normal(k[3], (D_MODEL, D_MODEL), dtype=jnp.float32) * std, 'WO': jax.random.normal(k[4], (D_MODEL, D_MODEL), dtype=jnp.float32) * std}
    _L0_attn_in = _L0_attn_setup()

    def _L0_ffn_setup():
        import jax, jax.numpy as jnp
        import numpy as np

        def _bitlinear(x, w_latent):
            scale = jax.lax.stop_gradient(jnp.clip(jnp.mean(jnp.abs(w_latent), axis=1, keepdims=True), 1e-05, None))
            tern = jnp.clip(jnp.round(w_latent / scale), -1.0, 1.0)
            w = w_latent + jax.lax.stop_gradient(tern - w_latent)
            return x @ (w * scale).T
        key = jax.random.key(seed)
        ks = jax.random.split(key, 6)
        dim, hidden, rank = (128, 512, 16)
        B, S = (4, 512)
        x = jax.random.normal(ks[0], (B, S, dim), dtype=jnp.float32)
        w_fc = 0.02 * jax.random.normal(ks[1], (hidden, dim), dtype=jnp.float32)
        w_proj = 0.02 * jax.random.normal(ks[2], (dim, hidden), dtype=jnp.float32)
        u = 0.02 * jax.random.normal(ks[3], (hidden, rank), dtype=jnp.float32)
        v = 0.02 * jax.random.normal(ks[4], (rank, dim), dtype=jnp.float32)
        fast_b = jax.random.normal(ks[5], (rank, rank), dtype=jnp.float32)
        gate = jnp.float32(0.05)
        return {'x': x, 'fast_b': fast_b, 'w_fc': w_fc, 'w_proj': w_proj, 'u': u, 'v': v, 'gate': gate}
    _L0_ffn_in = _L0_ffn_setup()

    def _L1_attn_setup():
        import jax, jax.numpy as jnp
        import numpy as np
        D_MODEL = 128
        D_STATE = 16
        D_CONV = 4
        EXPAND = 2
        D_INNER = EXPAND * D_MODEL
        DT_RANK = 64

        def _silu(v):
            return v * jax.nn.sigmoid(v)

        def _mamba_forward(x, W_in, conv_w, conv_b, W_x, W_dt, b_dt, A_log, D_param, W_out):
            B, L, _ = x.shape
            xz = jnp.einsum('bld,ed->ble', x, W_in)
            x_path, z_path = jnp.split(xz, 2, axis=-1)
            xc = jnp.transpose(x_path, (0, 2, 1))
            xc = jax.lax.conv_general_dilated(xc, conv_w, window_strides=(1,), padding=[(D_CONV - 1, 0)], dimension_numbers=('NCH', 'OIH', 'NCH'), feature_group_count=D_INNER)
            xc = jnp.transpose(xc, (0, 2, 1)) + conv_b
            xc = _silu(xc)
            x_dbl = jnp.einsum('bld,ed->ble', xc, W_x)
            dt_low = x_dbl[..., :DT_RANK]
            Bmat = x_dbl[..., DT_RANK:DT_RANK + D_STATE]
            Cmat = x_dbl[..., DT_RANK + D_STATE:]
            dt = jnp.einsum('blr,dr->bld', dt_low, W_dt) + b_dt
            A = -jnp.exp(A_log)
            delta = jnp.minimum(jax.nn.softplus(dt) + 0.0001, 10.0)
            deltaA = jnp.minimum(jnp.exp(delta[..., None] * A[None, None]), 10.0)
            deltaB_u = jnp.clip(delta[..., None] * Bmat[:, :, None, :] * xc[..., None], -10.0, 10.0)
            h0 = jnp.zeros((B, D_INNER, D_STATE), dtype=x.dtype)

            def step(h, inp):
                a_t, bu_t = inp
                h = jnp.clip(a_t * h + bu_t, -20.0, 20.0)
                return (h, h)
            _, hs = jax.lax.scan(step, h0, (jnp.swapaxes(deltaA, 0, 1), jnp.swapaxes(deltaB_u, 0, 1)))
            hs = jnp.swapaxes(hs, 0, 1)
            y = jnp.einsum('bldn,bln->bld', hs, Cmat)
            y = jnp.clip(y + xc * D_param, -50.0, 50.0)
            y = y * _silu(z_path)
            return jnp.einsum('bld,ed->ble', y, W_out)
        key = jax.random.key(seed)
        ks = jax.random.split(key, 8)
        B, L = (2, 128)
        x = jax.random.normal(ks[0], (B, L, D_MODEL), dtype=jnp.float32)
        W_in = jax.random.normal(ks[1], (2 * D_INNER, D_MODEL), dtype=jnp.float32) / np.sqrt(D_MODEL)
        conv_w = jax.random.normal(ks[2], (D_INNER, 1, D_CONV), dtype=jnp.float32) * (1.0 / np.sqrt(D_CONV))
        conv_b = jnp.zeros((D_INNER,), dtype=jnp.float32)
        W_x = jax.random.normal(ks[3], (DT_RANK + 2 * D_STATE, D_INNER), dtype=jnp.float32) / np.sqrt(D_INNER)
        dt_std = DT_RANK ** (-0.5)
        W_dt = jax.random.uniform(ks[4], (D_INNER, DT_RANK), dtype=jnp.float32, minval=-dt_std, maxval=dt_std)
        b_dt = jnp.zeros((D_INNER,), dtype=jnp.float32)
        A_log = jnp.zeros((D_INNER, D_STATE), dtype=jnp.float32)
        D_param = jnp.full((D_INNER,), 0.1, dtype=jnp.float32)
        W_out = jax.random.normal(ks[5], (D_MODEL, D_INNER), dtype=jnp.float32) * (0.1 / np.sqrt(D_INNER))
        return {'x': x, 'W_in': W_in, 'conv_w': conv_w, 'conv_b': conv_b, 'W_x': W_x, 'W_dt': W_dt, 'b_dt': b_dt, 'A_log': A_log, 'D_param': D_param, 'W_out': W_out}
    _L1_attn_in = _L1_attn_setup()

    def _L1_ffn_setup():
        import jax, jax.numpy as jnp
        import numpy as np
        ALPHA = 1.0
        key = jax.random.key(seed)
        ks = jax.random.split(key, 7)
        B, S, IN, OUT = (8, 1024, 128, 128)
        RANK, DDIM, UDIM = (4, 100, 50)
        return {'hidden_states': jax.random.normal(ks[0], (B, S, IN), dtype=jnp.float32), 'W': jax.random.normal(ks[1], (OUT, IN), dtype=jnp.float32) * 0.02, 'b': jax.random.normal(ks[2], (OUT,), dtype=jnp.float32) * 0.02, 'lora_down': jax.random.normal(ks[3], (RANK, DDIM), dtype=jnp.float32) * 0.1, 'lora_up': jax.random.normal(ks[4], (UDIM, RANK), dtype=jnp.float32) * 0.1, 'down_aux': jax.random.normal(ks[5], (DDIM, IN), dtype=jnp.float32) * 0.03, 'up_aux': jax.random.normal(ks[6], (OUT, UDIM), dtype=jnp.float32) * 0.03}
    _L1_ffn_in = _L1_ffn_setup()
    _d = {'L0_attn_x': _L0_attn_in['x'], 'L0_attn_WQ': _L0_attn_in['WQ'], 'L0_attn_WK': _L0_attn_in['WK'], 'L0_attn_WV': _L0_attn_in['WV'], 'L0_attn_WO': _L0_attn_in['WO'], 'L0_ffn_fast_b': _L0_ffn_in['fast_b'], 'L0_ffn_w_fc': _L0_ffn_in['w_fc'], 'L0_ffn_w_proj': _L0_ffn_in['w_proj'], 'L0_ffn_u': _L0_ffn_in['u'], 'L0_ffn_v': _L0_ffn_in['v'], 'L0_ffn_gate': _L0_ffn_in['gate'], 'L1_attn_W_in': _L1_attn_in['W_in'], 'L1_attn_conv_w': _L1_attn_in['conv_w'], 'L1_attn_conv_b': _L1_attn_in['conv_b'], 'L1_attn_W_x': _L1_attn_in['W_x'], 'L1_attn_W_dt': _L1_attn_in['W_dt'], 'L1_attn_b_dt': _L1_attn_in['b_dt'], 'L1_attn_A_log': _L1_attn_in['A_log'], 'L1_attn_D_param': _L1_attn_in['D_param'], 'L1_attn_W_out': _L1_attn_in['W_out'], 'L1_ffn_W': _L1_ffn_in['W'], 'L1_ffn_b': _L1_ffn_in['b'], 'L1_ffn_lora_down': _L1_ffn_in['lora_down'], 'L1_ffn_lora_up': _L1_ffn_in['lora_up'], 'L1_ffn_down_aux': _L1_ffn_in['down_aux'], 'L1_ffn_up_aux': _L1_ffn_in['up_aux']}
    _x0 = _d['L0_attn_x']
    _d['L0_attn_x'] = jax.random.normal(jax.random.fold_in(jax.random.key(seed), 1), (1, 2048, 128), dtype=_x0.dtype)
    del _x0
    return _d

def reference(L0_attn_x, L0_attn_WQ, L0_attn_WK, L0_attn_WV, L0_attn_WO, L0_ffn_fast_b, L0_ffn_w_fc, L0_ffn_w_proj, L0_ffn_u, L0_ffn_v, L0_ffn_gate, L1_attn_W_in, L1_attn_conv_w, L1_attn_conv_b, L1_attn_W_x, L1_attn_W_dt, L1_attn_b_dt, L1_attn_A_log, L1_attn_D_param, L1_attn_W_out, L1_ffn_W, L1_ffn_b, L1_ffn_lora_down, L1_ffn_lora_up, L1_ffn_down_aux, L1_ffn_up_aux):

    def _L0_attn_ref(x, WQ, WK, WV, WO):
        import jax, jax.numpy as jnp
        import numpy as np
        D_MODEL = 128
        NUM_HEADS = 16
        D_K = D_MODEL // NUM_HEADS
        BATCH, SEQ = (2, 256)
        B, S, E = x.shape
        mask = jnp.where(jnp.triu(jnp.ones((S, S), dtype=bool), k=1), -jnp.inf, 0.0).astype(x.dtype)

        def heads(W):
            return (x @ W).reshape(B, S, NUM_HEADS, D_K).transpose(0, 2, 1, 3)
        Q, K, V = (heads(WQ), heads(WK), heads(WV))
        score = jnp.einsum('bhqd,bhkd->bhqk', Q, K) / jnp.sqrt(jnp.asarray(D_K, x.dtype))
        score = score + mask
        score = score - jnp.max(score, axis=-1, keepdims=True)
        score = jnp.exp(score)
        score = score / jnp.sum(score, axis=-1, keepdims=True)
        out = jnp.einsum('bhqk,bhkd->bhqd', score, V)
        out = out.transpose(0, 2, 1, 3).reshape(B, S, E)
        return out @ WO

    def _L0_ffn_ref(x, fast_b, w_fc, w_proj, u, v, gate):
        import jax, jax.numpy as jnp
        import numpy as np

        def _bitlinear(x, w_latent):
            scale = jax.lax.stop_gradient(jnp.clip(jnp.mean(jnp.abs(w_latent), axis=1, keepdims=True), 1e-05, None))
            tern = jnp.clip(jnp.round(w_latent / scale), -1.0, 1.0)
            w = w_latent + jax.lax.stop_gradient(tern - w_latent)
            return x @ (w * scale).T
        h = _bitlinear(x, w_fc) + gate * (x @ v.T @ fast_b.T @ u.T)
        r = jnp.maximum(h, 0.0)
        return _bitlinear(r * r, w_proj)

    def _L1_attn_ref(x, W_in, conv_w, conv_b, W_x, W_dt, b_dt, A_log, D_param, W_out):
        import jax, jax.numpy as jnp
        import numpy as np
        D_MODEL = 128
        D_STATE = 16
        D_CONV = 4
        EXPAND = 2
        D_INNER = EXPAND * D_MODEL
        DT_RANK = 64

        def _silu(v):
            return v * jax.nn.sigmoid(v)

        def _mamba_forward(x, W_in, conv_w, conv_b, W_x, W_dt, b_dt, A_log, D_param, W_out):
            B, L, _ = x.shape
            xz = jnp.einsum('bld,ed->ble', x, W_in)
            x_path, z_path = jnp.split(xz, 2, axis=-1)
            xc = jnp.transpose(x_path, (0, 2, 1))
            xc = jax.lax.conv_general_dilated(xc, conv_w, window_strides=(1,), padding=[(D_CONV - 1, 0)], dimension_numbers=('NCH', 'OIH', 'NCH'), feature_group_count=D_INNER)
            xc = jnp.transpose(xc, (0, 2, 1)) + conv_b
            xc = _silu(xc)
            x_dbl = jnp.einsum('bld,ed->ble', xc, W_x)
            dt_low = x_dbl[..., :DT_RANK]
            Bmat = x_dbl[..., DT_RANK:DT_RANK + D_STATE]
            Cmat = x_dbl[..., DT_RANK + D_STATE:]
            dt = jnp.einsum('blr,dr->bld', dt_low, W_dt) + b_dt
            A = -jnp.exp(A_log)
            delta = jnp.minimum(jax.nn.softplus(dt) + 0.0001, 10.0)
            deltaA = jnp.minimum(jnp.exp(delta[..., None] * A[None, None]), 10.0)
            deltaB_u = jnp.clip(delta[..., None] * Bmat[:, :, None, :] * xc[..., None], -10.0, 10.0)
            h0 = jnp.zeros((B, D_INNER, D_STATE), dtype=x.dtype)

            def step(h, inp):
                a_t, bu_t = inp
                h = jnp.clip(a_t * h + bu_t, -20.0, 20.0)
                return (h, h)
            _, hs = jax.lax.scan(step, h0, (jnp.swapaxes(deltaA, 0, 1), jnp.swapaxes(deltaB_u, 0, 1)))
            hs = jnp.swapaxes(hs, 0, 1)
            y = jnp.einsum('bldn,bln->bld', hs, Cmat)
            y = jnp.clip(y + xc * D_param, -50.0, 50.0)
            y = y * _silu(z_path)
            return jnp.einsum('bld,ed->ble', y, W_out)
        return _mamba_forward(x, W_in, conv_w, conv_b, W_x, W_dt, b_dt, A_log, D_param, W_out)

    def _L1_ffn_ref(hidden_states, W, b, lora_down, lora_up, down_aux, up_aux):
        import jax, jax.numpy as jnp
        import numpy as np
        ALPHA = 1.0
        lilora_weight = up_aux @ (lora_up @ (lora_down @ down_aux))
        base = jnp.einsum('bsi,oi->bso', hidden_states, W) + b
        delta = jnp.einsum('bsi,oi->bso', hidden_states, lilora_weight)
        return base + ALPHA * delta
    x = L0_attn_x
    x = x + _layernorm(_L0_attn_ref(_layernorm(x, axis=-1), L0_attn_WQ, L0_attn_WK, L0_attn_WV, L0_attn_WO), axis=-1)
    x = x + _layernorm(_L0_ffn_ref(_layernorm(x, axis=-1), L0_ffn_fast_b, L0_ffn_w_fc, L0_ffn_w_proj, L0_ffn_u, L0_ffn_v, L0_ffn_gate), axis=-1)
    x = x + _layernorm(_L1_attn_ref(_layernorm(x, axis=-1), L1_attn_W_in, L1_attn_conv_w, L1_attn_conv_b, L1_attn_W_x, L1_attn_W_dt, L1_attn_b_dt, L1_attn_A_log, L1_attn_D_param, L1_attn_W_out), axis=-1)
    x = x + _layernorm(_L1_ffn_ref(_layernorm(x, axis=-1), L1_ffn_W, L1_ffn_b, L1_ffn_lora_down, L1_ffn_lora_up, L1_ffn_down_aux, L1_ffn_up_aux), axis=-1)
    return x

_drawn_inputs = setup_inputs


def setup_inputs(seed=0):
    import zlib

    import numpy as np

    out = dict(_drawn_inputs(seed))
    spreads = {'L1_attn_conv_b': (0.0, 0.1),
     'L1_attn_b_dt': (0.0, 0.289),
     'L1_attn_A_log': (0.0, 0.1),
     'L1_attn_D_param': (0.10000000149011612, 0.6)}
    factors = {}
    for name, (base, spread) in spreads.items():
        noise = np.random.default_rng([zlib.crc32(name.encode()), seed]).standard_normal(out[name].shape)
        drawn = base * np.exp(spread * noise) if base else spread * noise
        out[name] = jnp.asarray(drawn.astype(out[name].dtype))
    for name, factor in factors.items():
        out[name] = (out[name] * factor).astype(out[name].dtype)
    return out
```

```python
from contextlib import ExitStack

import concourse.bass as bass
from concourse import mybir

ALU = mybir.AluOpType
ACT = mybir.ActivationFunctionType
AX = mybir.AxisListType
F32 = mybir.dt.float32
BF16 = mybir.dt.bfloat16
I32 = mybir.dt.int32

P = 128
S = 2048
D = 128
HEADS, DK = 16, 8
TILES = S // P
CW = 512
CHUNKS = S // CW
TPC = CW // P
QUADS = HEADS // 4
UNITS = CHUNKS * QUADS
HIDDEN, RANK = 512, 16
HT = HIDDEN // P
DI, NST, DTR, CONV = 256, 16, 64, 4
HALVES = DI // P
LR, DDIM, UDIM = 4, 100, 50
EPS = 1e-5
MASKED = -1.0e30
LOWEST = -3.0e38
ROUND = 6
SPLIT_Q = (0, 0, 1, 1, 0, 2)
SPLIT_K = (0, 1, 0, 1, 2, 0)
ROWS = ROUND * DK
PAIR = 2 * ROWS
AUG = PAIR + 3
NORMS = 8
H_BOUND = 19.99


def build(nc, a):
    ctx = ExitStack()
    with ctx:
        def sb(name, shape, dt=F32):
            return ctx.enter_context(nc.sbuf_tensor(name, shape, dt))

        def sem(name):
            return ctx.enter_context(nc.semaphore(name))

        st_ps = ctx.enter_context(nc.psum_tensor("st_ps", [P, 4, CW], F32))
        bank = [st_ps[:, i, :] for i in range(4)] + [
            ctx.enter_context(nc.psum_tensor(f"bank{i}", [P, CW], F32))[:, :] for i in range(4, 8)]
        qk_ps = [bank[4], bank[5]]
        pv_ps = bank[6]
        misc = bank[7]

        x = sb("x", [P, TILES, D])
        xn = sb("xn", [P, 2, TPC, D])
        xT = sb("xT", [P, 4 + S])
        xTc = [xT[:, 4 + CW * c:4 + CW * (c + 1)] for c in range(CHUNKS)]
        stats = sb("stats", [P, 2 * TILES, 6])
        moments = sb("moments", [P, NORMS * TILES, 2])
        lnvar = sb("lnvar", [P, NORMS * TILES])
        rstd = sb("rstd", [P, NORMS * TILES])
        nrm = sb("nrm", [P, 2, TPC, D])
        arena_q = sb("arena_q", [P, 8192])
        arena_k = sb("arena_k", [P, 8192])
        arena_v = sb("arena_v", [P, 8192])
        qs = arena_q[:, :].bitcast(BF16).rearrange("p (b h t) -> p b h t", b=2, h=HEADS)
        ks = arena_k[:, :].bitcast(BF16).rearrange("p (h t) -> p h t", h=8)
        vaug = arena_v[:, :].rearrange("p (j h e) -> p j h e", j=TILES, h=HEADS)
        parts = sb("parts", [P, 2, 2, 3, CW], BF16)
        probs = sb("probs", [P, 3, 4, CW])
        junk = sb("junk", [P, 2, CW], BF16)
        maxcol = sb("maxcol", [P, 2, TPC, 4, CHUNKS])
        rowmax = sb("rowmax", [P, 2, TPC, 4])
        maxres = sb("maxres", [P, 2, TPC, 4])
        maxparts = sb("maxparts", [P, 2, TPC, 4, 3], BF16)
        maxT = sb("maxT", [12, 2, CW], BF16)
        oT = sb("oT", [P, 2, CW])
        resid = oT
        rsum = sb("rsum", [P, 2, TPC, 4])
        attn = sb("attn", [P, 2, TPC, D])
        attnT = sb("attnT", [P, CW])
        sub = xT[:, 4:].rearrange("p (i e) -> p i e", e=D)
        xc = arena_q[:, 0:4096].rearrange("p (h t) -> p h t", h=2)
        sz = arena_q[:, 4096:8192].rearrange("p (h t) -> p h t", h=2)
        delta = arena_k[:, 0:4096].rearrange("p (h t) -> p h t", h=2)
        dxc = arena_k[:, 4096:8192].rearrange("p (h t) -> p h t", h=2)
        ring = arena_v[:, :].rearrange("p (r t) -> p r t", t=CW)
        NA, NB, NC_RING = 4, 3, 3
        a_ring = [ring[:, i, :] for i in range(0, 4)]
        bu_ring = [ring[:, i, :] for i in range(4, 7)]
        h_ring = [ring[:, i, :] for i in range(7, 10)]
        hc_ring = [ring[:, i, :] for i in range(10, 13)]
        c_ring = [ring[:, i, :] for i in range(13, 16)]
        flat = parts[:, :, :, :, :].rearrange("p a m s t -> p (a m s t)")
        bcs = flat[0:96, 0:S]
        bc_hi = flat[0:96, S:S + CW]
        bc_mid = flat[0:96, S + CW:S + 2 * CW]
        bc_r = flat[0:96, S + 2 * CW:S + 4 * CW].bitcast(F32)
        dtl = flat[0:DTR, S + 4 * CW:S + 8 * CW].bitcast(F32).rearrange("p (a t) -> p a t", a=2)
        sp_a, sp_b = probs[:, 0, 0:2, :], probs[:, 0, 2:4, :]
        carry = sb("carry", [P, HALVES, NST])
        relu = probs[:, 0, :, :]
        relu2 = probs[:, 1:3, :, :]
        ident = sb("ident", [P, P])
        ident_b = sb("ident_b", [P, P], BF16)
        ones = sb("ones", [P, P])
        mask_kq = sb("mask_kq", [P, P], BF16)
        mask_qk = sb("mask_qk", [P, CW])
        pick = sb("pick", [96, 2 * NST, P], BF16)
        w_qkvo = sb("w_qkvo", [P, 4, D])
        w_fc = probs[:, 0, 0, :].rearrange("p (m e) -> p m e", m=HT)
        w_pj = probs[:, 0, 1, :]
        fb = sb("fb", [RANK, RANK])
        w_u = sb("w_u", [P, HT, RANK])
        w_v = sb("w_v", [RANK, D])
        gate = sb("gate", [P, 1])
        w_in = probs[:, 0, 2, :].rearrange("p (m e) -> p m e", m=4)
        conv_w = sb("conv_w", [P, HALVES, CONV])
        conv_b = sb("conv_b", [P, HALVES])
        w_x = probs[0:96, 0, 3, 0:DI]
        w_dt = sb("w_dt", [P, HALVES, DTR])
        b_dt = sb("b_dt", [P, HALVES])
        a_log = sb("a_log", [P, HALVES, NST])
        d_par = sb("d_par", [P, HALVES])
        w_out = probs[:, 0, 3, DI:]
        w_l = probs[:, 1, 0, 0:D]
        b_l = sb("b_l", [P, D])
        l_down = sb("l_down", [LR, DDIM])
        l_up = sb("l_up", [UDIM, LR])
        d_aux = probs[0:DDIM, 1, 0, D:2 * D]
        u_aux = probs[:, 1, 0, 2 * D:2 * D + UDIM]
        tern_fc = attn[:, 0, :, :]
        tern_pj = attn[:, 1, :, :].rearrange("p i e -> p (i e)")
        tmp_w = nrm[:, :, :, :].rearrange("p a i e -> p a (i e)")
        scl = sb("scl", [P, 3, HT + 1])
        fcT = sb("fcT", [P, HIDDEN])
        pjT = sb("pjT", [P, HT, D])
        uT = probs[0:RANK, 1, 1, :]
        fbT = probs[0:RANK, 1, 2, 0:RANK]
        q1 = probs[0:RANK, 1, 2, D:2 * D]
        w_tap = oT[:, :, :].rearrange("p a t -> p (a t)").rearrange("p (k h e) -> p k h e", k=CONV, h=HALVES)
        tapT = sb("tapT", [P, CONV, DI])
        zT = sb("zT", [P, DI])
        wxT = sb("wxT", [P, HALVES, 96])
        wbcT = sb("wbcT", [P, HALVES, 96])
        wdtT = sb("wdtT", [DTR, DI])
        woutT = sb("woutT", [P, HALVES, D])
        neg_a = sb("neg_a", [P, HALVES, NST])
        a_max = sb("a_max", [P, HALVES])
        ldT = probs[0:DDIM, 1, 2, 16:16 + LR]
        luT = probs[0:LR, 1, 2, 32:32 + UDIM]
        uaT = probs[0:UDIM, 1, 2, 2 * D:3 * D]
        r1 = probs[0:LR, 1, 2, 3 * D:4 * D]
        r2 = probs[0:UDIM, 1, 3, 0:D]
        wlT = sb("wlT", [P, D])
        bmax = sb("bmax", [P, CHUNKS, TPC])
        diag = probs[:, 2, 2, :].rearrange("p (i t) -> p i t", i=TPC)
        bnd_a, bnd_b, bnd_h = probs[:, 1, 0:2, :], probs[:, 1, 2:4, :], probs[:, 2, 0:2, :]
        bnd_c = sb("bnd_c", [P, HALVES])
        bnd_m = sb("bnd_m", [P, CHUNKS, HALVES])
        over = sb("over", [P, 1])
        over_i = sb("over_i", [1, 1], I32)
        eps_col = sb("eps_col", [P, 1])
        h_last, h_next = sb("h_last", [P, 1]), sb("h_next", [P, 1])

        def prep_bank(n):
            return bank[6 + n % 2]

        def y_bank(c, hf):
            return bank[hf if c % 2 == 0 else 6 + hf]

        scratch = nc.dram_tensor("split_parts", (2, 3, P, S), BF16, kind="Internal").ap()

        x_in = [sem(f"x_in{c}") for c in range(CHUNKS)]
        wqkv_in, weights_in = sem("wqkv_in"), sem("weights_in")
        N_WEIGHTS = 21
        PREP_SLOTS = 11
        consts, consts_b = sem("consts"), sem("consts_b")
        stats_of = [sem(f"stats{k}") for k in range(8)]
        moments_of = [sem(f"moments{k}") for k in range(8)]
        lnvar_of = [sem(f"lnvar{k}") for k in range(8)]
        rstd_of = [sem(f"rstd{k}") for k in range(8)]
        dve_step = sem("dve_step")
        act_step = sem("act_step")
        xn_done = [sem(f"xn_done{k}") for k in range(4)]
        xT_ps = [sem(f"xT_ps{k}") for k in range(4)]
        xT_done = [sem(f"xT_done{k}") for k in range(4)]
        prep_dve, prep_pe, prep_act = sem("prep_dve"), sem("prep_pe"), sem("prep_act")
        qkv_ps, v_taken, parts_done = sem("qkv_ps"), sem("v_taken"), sem("parts_done")
        k_hi, q_hi = sem("k_hi"), sem("q_hi")
        parts_stored = [sem(f"parts_stored{c}") for c in range(CHUNKS)]
        stacked = [sem(f"stacked{c}") for c in range(CHUNKS)]
        pads = sem("pads")
        scores_ps, scores_max = sem("scores_ps"), sem("scores_max")
        max_parts, maxT_ps, maxT_done = sem("max_parts"), sem("maxT_ps"), sem("maxT_done")
        max_rows = [sem(f"max_rows{i}") for i in range(2)]
        sT_ps, exp_done, pv_done, pv_taken = sem("sT_ps"), sem("exp_done"), sem("pv_done"), sem("pv_taken")
        oT_ps, attn_done, attnT_ps, attnT_done = sem("oT_ps"), sem("attn_done"), sem("attnT_ps"), sem("attnT_done")
        wo_ps, sub_done = sem("wo_ps"), sem("sub_done")
        x1_done, x2_done, x3_done, x4_done = (sem(f"x{i}_done") for i in range(1, 5))
        fc_ps, relu_done, relu2_done, pj_ps = sem("fc_ps"), sem("relu_done"), sem("relu2_done"), sem("pj_ps")
        pad_done, pre_ps, silu_done = sem("pad_done"), sem("pre_ps"), sem("silu_done")
        dtl_ps, dtl_done, bc_ps, bcs_done, bmax_done = sem("dtl_ps"), sem("dtl_done"), sem("bc_ps"), sem("bcs_done"), sem("bmax_done")
        dt_ps, sp_a_done, sp_exp, sp_ln, delta_done, dxc_done = (sem(n) for n in ("dt_ps", "sp_a_done", "sp_exp", "sp_ln", "delta_done", "dxc_done"))
        bt_ps, diag_done, bm_ps, bnd_b_done, bnd_abs, bnd_exp, bnd_done = (sem(n) for n in ("bt_ps", "diag_done", "bm_ps", "bnd_b_done", "bnd_abs", "bnd_exp", "bnd_done"))
        over_done, over_ps, flag_done = sem("over_done"), sem("over_ps"), sem("flag_done")
        b_ps, c_ps, c_done, decay_done, bu_done, h_done, hc_done, y_ps, hc_used = (
            sem(n) for n in ("b_ps", "c_ps", "c_done", "decay_done", "bu_done", "h_done", "hc_done", "y_ps", "hc_used"))
        y_done, yout_ps, fin_ps, stored = (sem(n) for n in ("y_done", "yout_ps", "fin_ps", "stored"))
        clip_done, carry_set, y_sum, y_clip = (sem(n) for n in ("clip_done", "carry_set", "y_sum", "y_clip"))
        eps_set = sem("eps_set")

        unit = [(u // QUADS, u % QUADS) for u in range(UNITS)]
        pieces = [[(i, n, g) for g in range(c + 1) for i in range(TPC) for n in range(4)] for c, _ in unit]
        steps = [TPC * (c + 1) for c, _ in unit]
        piece_base = [sum(len(p) for p in pieces[:u]) for u in range(UNITS + 1)]
        step_base = [sum(steps[:u]) for u in range(UNITS + 1)]
        FIRST = 2
        LEAD = 3
        STEPS = step_base[UNITS]

        def deal_pieces():
            order = [(v, p) for v in range(FIRST, UNITS) for p in range(len(pieces[v]))]
            due = {max(step_base[v] - LEAD, 1): piece_base[v + 1] - piece_base[FIRST] for v in range(FIRST, UNITS)}
            at, done = [], 0
            for s in range(STEPS):
                need = [-(-(n - done) // (t - s)) for t, n in due.items() if t > s]
                upto = min(done + max(need + [0]), len(order))
                at.append(order[done:upto])
                done = upto
            return at

        pieces_at = deal_pieces()
        turn_at = [[v for v in range(FIRST, UNITS) if s and (v, len(pieces[v]) - 1) in pieces_at[s - 1]]
                   for s in range(STEPS)]
        misc_order = [("max", v) for v in range(FIRST)]
        for u in range(UNITS):
            for j in range(steps[u]):
                misc_order += [("max", v) for v in turn_at[step_base[u] + j]]
                misc_order += [("out", u - 1)] * (j == 2 and u > 0)
                misc_order += [("project", u // QUADS - 1)] * (j == 3 and u > 0 and u % QUADS == 0)
        misc_order += [("out", UNITS - 1), ("project", CHUNKS - 1)]

        block = ctx.enter_context(nc.Block())

        @block.sync
        def _(sp):
            xr = a["L0_attn_x"][0].rearrange("(i p) e -> p i e", p=P)
            for c in range(CHUNKS):
                sp.dma_start(x[:, TPC * c:TPC * (c + 1), :], xr[:, TPC * c:TPC * (c + 1), :]).then_inc(x_in[c], 16)
                if c == 0:
                    for n, w in enumerate(("WQ", "WK", "WV", "WO")):
                        sp.dma_start(w_qkvo[:, n, :], a[f"L0_attn_{w}"]).then_inc(wqkv_in, 16)

            def stack_q(c):
                for par in range(2):
                    for t in range(ROUND):
                        src = scratch[0, SPLIT_Q[t]].rearrange("(hp par d) t -> par d hp t", par=2, d=DK)[par]
                        row = ROWS * par + DK * t
                        sp.dma_start(qs[row:row + DK, c % 2, par::2, :], src[:, :, CW * c:CW * (c + 1)]).then_inc(stacked[c], 16)

            sp.wait_ge(pads, 2)
            for c in range(CHUNKS):
                for m in range(2):
                    sp.wait_ge(parts_done, 2 * c + m + 1)
                    sp.dma_start(scratch[m, :, :, CW * c:CW * (c + 1)].rearrange("s p t -> p s t"),
                                 parts[:, c % 2, m, :, :]).then_inc(parts_stored[c], 16)
                sp.wait_ge(parts_stored[c], 32)
                if c < 2:
                    stack_q(c)
                for par in range(2):
                    for t in range(ROUND):
                        src = scratch[1, SPLIT_K[t]].rearrange("(hp par d) t -> par d hp t", par=2, d=DK)[par]
                        row = ROWS * par + DK * t
                        sp.dma_start(ks[row:row + DK, :, CW * c:CW * (c + 1)],
                                     src[:, :, CW * c:CW * (c + 1)]).then_inc(stacked[c], 16)
            for u, (c, quad) in enumerate(unit):
                for c2 in range(2, CHUNKS):
                    if u in next(t for t in turn_at[step_base[QUADS * (c2 - 1)]:] if t)[:1]:
                        sp.wait_ge(sT_ps, 2 * step_base[QUADS * (c2 - 1)])
                        stack_q(c2)
                sp.wait_ge(maxT_done, u + 1)
                for n in range(4):
                    sp.dma_start(qs[PAIR:AUG, c % 2, 4 * quad + n, :],
                                 maxT[3 * n:3 * n + 3, u % 2, :]).then_inc(max_rows[u % 2], 16)
            outr = a["out"][0].rearrange("(i p) e -> p i e", p=P)
            for c in range(CHUNKS):
                sp.wait_ge(x4_done, c + 1)
                sp.dma_start(outr[:, TPC * c:TPC * (c + 1), :], x[:, TPC * c:TPC * (c + 1), :]).then_inc(stored, 16)
            sp.wait_ge(stored, 16 * CHUNKS)

        @block.gpsimd
        def _(pool):
            def chained(ins, n):
                ins.then_inc(consts, 1)
                pool.wait_ge(consts, n)

            chained(nc.gpsimd.memset(ident[:], 1.0), 1)
            chained(nc.gpsimd.affine_select(out=ident[:], in_=ident[:], compare_op=ALU.is_equal, fill=0.0, base=0,
                                            pattern=[[-1, P]], channel_multiplier=1), 2)
            nc.gpsimd.memset(ones[:], 1.0).then_inc(consts, 1)
            nc.gpsimd.memset(xT[:, 0:4], 0.0).then_inc(consts, 1)
            nc.gpsimd.tensor_copy(ident_b[:], ident[:]).then_inc(consts, 1)
            nc.gpsimd.memset(mask_kq[:], 0.0).then_inc(consts, 1)
            chained(nc.gpsimd.memset(mask_qk[:], 0.0), 7)
            nc.gpsimd.affine_select(out=mask_kq[:], in_=mask_kq[:], compare_op=ALU.is_ge, fill=MASKED, base=0,
                                    pattern=[[1, P]], channel_multiplier=-1).then_inc(consts, 1)
            nc.gpsimd.affine_select(out=mask_qk[:, CW - P:], in_=mask_qk[:, CW - P:], compare_op=ALU.is_ge,
                                    fill=MASKED, base=0, pattern=[[-1, P]], channel_multiplier=1).then_inc(consts, 1)
            nc.gpsimd.memset(vaug[:, :, :, DK:], 1.0).then_inc(consts, 1)
            chained(nc.gpsimd.memset(pick[:], 0.0), 11)
            for g in range(3):
                chained(nc.gpsimd.affine_select(out=pick[:], in_=pick[:], compare_op=ALU.not_equal, fill=1.0,
                                                base=-32 * g, pattern=[[-1, 2 * NST], [0, P]],
                                                channel_multiplier=1), 12 + g)
            for c in range(CHUNKS):
                for hf in range(HALVES):
                    pool.wait_ge(delta_done, 2 * c + hf + 1)
                    pool.wait_ge(silu_done, 4 * c + hf + 1)
                    nc.gpsimd.tensor_tensor(dxc[:, hf, CW * c:CW * (c + 1)], delta[:, hf, CW * c:CW * (c + 1)],
                                            xc[:, hf, CW * c:CW * (c + 1)], ALU.mult).then_inc(dxc_done, 1)
            for m in range(CHUNKS * NST * HALVES):
                pool.wait_ge(c_done, m // 2 + 1)
                pool.wait_ge(h_done, m + 1)
                if m >= NB:
                    pool.wait_ge(hc_used, m - NB + 1)
                c, n, hf = m // (2 * NST), (m // 2) % NST, m % 2
                if m == 0:
                    pool.wait_ge(carry_set, 1)
                if c < CHUNKS - 1:
                    nc.gpsimd.tensor_copy(carry[:, hf, n:n + 1], h_ring[m % NB][:, CW - 1:CW])
                nc.gpsimd.tensor_tensor(hc_ring[m % NB], h_ring[m % NB], c_ring[(m // 2) % NC_RING],
                                        ALU.mult).then_inc(hc_done, 1)

        @block.tensor
        def _(pe):
            mm, tr = pe.matmul, pe.transpose

            def transposed_chunk(k, c, src, dst):
                for i in range(TPC):
                    ins = tr(dst[:, P * i:P * (i + 1)], src[:, c % 2, i, :], ident[:, :])
                ins.then_inc(xT_ps[k], 1)

            pe.wait_ge(consts, 2)
            for c in range(CHUNKS):
                pe.wait_ge(xn_done[0], c + 1)
                if c:
                    pe.wait_ge(xT_done[0], c)
                transposed_chunk(0, c, xn, bank[0])
                pe.wait_ge(xT_done[0], c + 1)
                if c == 0:
                    pe.wait_ge(wqkv_in, 64)
                else:
                    pe.wait_ge(parts_done, 2 * c)
                    pe.wait_ge(v_taken, c)
                mm(bank[1], w_qkvo[:, 0, :], xTc[c], start=True, stop=True).then_inc(qkv_ps, 1)
                mm(bank[2], w_qkvo[:, 1, :], xTc[c], start=True, stop=True).then_inc(qkv_ps, 1)
                for i in range(TPC):
                    ins = mm(bank[3][:, P * i:P * (i + 1)], xTc[c][:, P * i:P * (i + 1)], w_qkvo[:, 2, :],
                             start=(i == 0), stop=(i == TPC - 1), skip_group_check=True)
                ins.then_inc(qkv_ps, 1)

            def slot(n):
                if n >= 2:
                    pe.wait_ge(prep_act, n - 1)
                return prep_bank(n)

            pe.wait_ge(weights_in, 16 * N_WEIGHTS)
            b0 = slot(0)
            for m in range(HT):
                ins = tr(b0[0:RANK, P * m:P * (m + 1)], w_u[:, m, :], ident[:, :])
            ins.then_inc(prep_pe, 1)
            b1 = slot(1)
            tr(b1[0:RANK, 0:RANK], fb[:, :], ident[0:RANK, 0:RANK])
            tr(b1[0:DDIM, 32:32 + LR], l_down[:, :], ident[0:LR, 0:LR])
            tr(b1[0:LR, 64:64 + UDIM], l_up[:, :], ident[0:UDIM, 0:UDIM])
            tr(b1[0:UDIM, P:2 * P], u_aux[:, :], ident[:, :]).then_inc(prep_pe, 1)
            b2 = slot(2)
            for i in range(2):
                tr(b2[:, P * i:P * (i + 1)], w_in[:, 2 + i, :], ident[:, :])
            for i in range(2):
                ins = tr(b2[:, 2 * P + P * i:3 * P + P * i], w_out[:, P * i:P * (i + 1)], ident[:, :])
            ins.then_inc(prep_pe, 1)
            b3 = slot(3)
            for i in range(2):
                tr(b3[:, P * i:P * i + 96], w_x[:, P * i:P * (i + 1)], ident[0:96, 0:96])
            for i in range(2):
                ins = tr(b3[0:DTR, 2 * P + P * i:3 * P + P * i], w_dt[:, i, :], ident[:, :])
            ins.then_inc(prep_pe, 1)
            for g in range(2):
                b = slot(4 + g)
                if g == 0:
                    pe.wait_ge(prep_dve, 1)
                for k in range(2):
                    for hf in range(HALVES):
                        o = 2 * P * k + P * hf
                        ins = tr(b[:, o:o + P], w_tap[:, 2 * g + k, hf, :], ident[:, :])
                ins.then_inc(prep_pe, 1)
            b6 = slot(6)
            pe.wait_ge(prep_dve, 2)
            for m in range(HT):
                ins = tr(b6[:, P * m:P * (m + 1)], tern_pj[:, P * m:P * (m + 1)], ident[:, :])
            ins.then_inc(prep_pe, 1)
            b7 = slot(7)
            mm(b7[0:RANK, 0:D], fbT[:, :], w_v[:, :], start=True, stop=True)
            mm(b7[0:LR, P:2 * P], ldT[:, :], d_aux[:, :], start=True, stop=True,
               skip_group_check=True).then_inc(prep_pe, 1)
            b8 = slot(8)
            pe.wait_ge(prep_act, 8)
            mm(b8[0:UDIM, 0:D], luT[:, :], r1[:, :], start=True, stop=True).then_inc(prep_pe, 1)
            b9 = slot(9)
            pe.wait_ge(prep_dve, 3)
            for m in range(HT):
                mm(b9[:, P * m:P * (m + 1)], tern_fc[:, m, :], ident[:, :], start=(m == 0), stop=False,
                   skip_group_check=True)
                ins = mm(b9[:, P * m:P * (m + 1)], q1[:, :], uT[:, P * m:P * (m + 1)], start=False,
                         stop=(m == HT - 1), skip_group_check=True)
            ins.then_inc(prep_pe, 1)
            b10 = slot(10)
            pe.wait_ge(prep_act, 9)
            mm(b10[:, 0:D], w_l[:, :], ident[:, :], start=True, stop=False)
            mm(b10[:, 0:D], r2[:, :], uaT[:, :], start=False, stop=True).then_inc(prep_pe, 1)

            pe.wait_ge(xT_done[0], CHUNKS)
            pe.wait_ge(parts_done, 2 * CHUNKS)
            pe.wait_ge(v_taken, CHUNKS)
            pe.wait_ge(prep_act, PREP_SLOTS)
            pe.wait_ge(consts, 10)
            pe.wait_ge(pads, 2)

            def scores(v, p):
                c, quad = unit[v]
                i, n, g = pieces[v][p]
                h, gp = 4 * quad + n, piece_base[v] + p
                if p == 0 and quad == 0:
                    pe.wait_ge(stacked[c], 16 * 4 * ROUND)
                if gp >= 2:
                    pe.wait_ge(scores_max, gp - 1)
                w = CW if g < c else P * (i + 1)
                mm(qk_ps[gp % 2][:, 0:w], qs[0:PAIR, c % 2, h, P * i:P * (i + 1)],
                   ks[0:PAIR, h // 2, CW * g:CW * g + w], start=True, stop=True).then_inc(scores_ps, 1)

            def scores_T(u, j, pair):
                c, quad = unit[u]
                s = step_base[u] + j
                if s >= 1:
                    pe.wait_ge(exp_done, 2 * (s - 1) + pair + 1)
                q0 = max(0, P * (j - TPC * c))
                for n in (2 * pair, 2 * pair + 1):
                    h = 4 * quad + n
                    on_diag = j >= TPC * c
                    ins = mm(st_ps[:, n, q0:CW], ks[0:AUG, h // 2, P * j:P * (j + 1)],
                             qs[0:AUG, c % 2, h, q0:CW], start=True, stop=not on_diag)
                if on_diag:
                    for n in (2 * pair, 2 * pair + 1):
                        ins = mm(st_ps[:, n, q0:q0 + P], ident_b[:, :], mask_kq[:, :], start=False, stop=True)
                ins.then_inc(sT_ps, 1)

            def weigh(u, j, part):
                c, quad = unit[u]
                s = step_base[u] + j
                q0 = max(0, P * (j - TPC * c))
                cut = q0 + (CW - q0 + 1) // 2
                lo, hi = (q0, cut) if part == 0 else (cut, CW)
                if part == 0:
                    if j == 0 and u:
                        pe.wait_ge(pv_taken, u)
                    pe.wait_ge(exp_done, 2 * (s + 1))
                for n in range(4):
                    ins = mm(pv_ps[32 * n:32 * n + 32, lo:hi], vaug[:, j, 4 * quad + n, :],
                             probs[:, s % 3, n, lo:hi], start=(j == 0 and part == 0),
                             stop=(j == steps[u] - 1 and part == 1), tile_position=(0, 32 * n),
                             skip_group_check=True)
                if part == 1:
                    ins.then_inc(pv_done, 1)

            def misc_free(job):
                k = misc_order.index(job)
                if k:
                    kind, n = misc_order[k - 1]
                    pe.wait_ge({"max": maxT_done, "out": attn_done, "project": sub_done}[kind], n + 1)

            def turn_max(v):
                pe.wait_ge(max_parts, v + 1)
                misc_free(("max", v))
                m16 = misc.bitcast(BF16)
                for i in range(TPC):
                    ins = tr(m16[0:12, P * i:P * (i + 1)], maxparts[:, v % 2, i, :, :].rearrange("p n s -> p (n s)"),
                             ident_b[:, :])
                ins.then_inc(maxT_ps, 1)

            def turn_out(u):
                pe.wait_ge(pv_taken, u + 1)
                misc_free(("out", u))
                for i in range(TPC):
                    ins = tr(misc[:, P * i:P * (i + 1)], oT[:, u % 2, P * i:P * (i + 1)], ident[:, :])
                ins.then_inc(oT_ps, 1)

            def project_out(c):
                pe.wait_ge(attn_done, QUADS * (c + 1))
                misc_free(("project", c))
                for i in range(TPC):
                    ins = tr(misc[:, P * i:P * (i + 1)], attn[:, c % 2, i, :], ident[:, :])
                ins.then_inc(attnT_ps, 1)
                pe.wait_ge(attnT_done, c + 1)
                for i in range(TPC):
                    ins = mm(misc[:, P * i:P * (i + 1)], attnT[:, P * i:P * (i + 1)], w_qkvo[:, 3, :],
                             start=(i == 0), stop=(i == TPC - 1), skip_group_check=True)
                ins.then_inc(wo_ps, 1)

            for u in range(FIRST):
                for p in range(len(pieces[u])):
                    scores(u, p)
                turn_max(u)
            last = None
            for u in range(UNITS):
                pe.wait_ge(max_rows[u % 2], 64 * (u // 2 + 1))
                for j in range(steps[u]):
                    s_ = step_base[u] + j
                    todo = pieces_at[s_]
                    cut = [len(todo) * k // 4 for k in range(5)]
                    for k in range(4):
                        if k % 2 == 0:
                            scores_T(u, j, k // 2)
                        elif last is not None:
                            weigh(*last, k // 2)
                        for v, p in todo[cut[k]:cut[k + 1]]:
                            scores(v, p)
                    last = (u, j)
                    for v in turn_at[s_]:
                        turn_max(v)
                    if j == 2 and u:
                        turn_out(u - 1)
                    if j == 3 and u and u % QUADS == 0:
                        project_out(u // QUADS - 1)
            weigh(*last, 0)
            weigh(*last, 1)
            turn_out(UNITS - 1)
            project_out(CHUNKS - 1)

            pe.wait_ge(sub_done, CHUNKS)
            for c in range(CHUNKS):
                pe.wait_ge(xn_done[1], c + 1)
                if c:
                    pe.wait_ge(xT_done[1], c)
                transposed_chunk(1, c, xn, bank[0])
                pe.wait_ge(xT_done[1], c + 1)
                for m in range(HT):
                    if c:
                        pe.wait_ge(relu_done, HT * (c - 1) + m + 1)
                    mm(bank[1 + m], fcT[:, P * m:P * (m + 1)], xTc[c], start=True, stop=True).then_inc(fc_ps, 1)
                pe.wait_ge(relu2_done, HT * (c + 1))
                if c >= 2:
                    pe.wait_ge(x2_done, c - 1)
                dst = bank[5 + c % 2]
                for i in range(TPC):
                    for m in range(HT):
                        ins = mm(dst[:, P * i:P * (i + 1)], relu2[:, c % 2, m, P * i:P * (i + 1)], pjT[:, m, :],
                                 start=(i == 0 and m == 0), stop=(m == HT - 1), skip_group_check=True)
                ins.then_inc(pj_ps, 1)

            for c in range(CHUNKS):
                pe.wait_ge(xn_done[2], c + 1)
                if c:
                    pe.wait_ge(xT_done[2], c)
                else:
                    pe.wait_ge(xT_done[1], CHUNKS)
                    pe.wait_ge(relu_done, HT * CHUNKS)
                    pe.wait_ge(x2_done, CHUNKS)
                transposed_chunk(2, c, xn, bank[0])
                pe.wait_ge(xT_done[2], c + 1)
                t0 = 4 + CW * c - (CONV - 1)
                for hf in range(HALVES):
                    if c:
                        pe.wait_ge(silu_done, 4 * (c - 1) + hf + 1)
                    for k in range(CONV):
                        ins = mm(bank[1 + hf], tapT[:, k, P * hf:P * (hf + 1)], xT[:, t0 + k:t0 + k + CW],
                                 start=(k == 0), stop=(k == CONV - 1))
                    ins.then_inc(pre_ps, 1)
                for hf in range(HALVES):
                    if c:
                        pe.wait_ge(silu_done, 4 * (c - 1) + 3 + hf)
                    mm(bank[3 + hf], zT[:, P * hf:P * (hf + 1)], xTc[c], start=True, stop=True).then_inc(pre_ps, 1)
                pe.wait_ge(silu_done, 4 * c + 2)
                for hf in range(HALVES):
                    ins = mm(bank[5][0:DTR, :], wxT[:, hf, 0:DTR], xc[:, hf, CW * c:CW * (c + 1)],
                             start=(hf == 0), stop=(hf == HALVES - 1))
                ins.then_inc(dtl_ps, 1)
                if c:
                    pe.wait_ge(bcs_done, c)
                for hf in range(HALVES):
                    ins = mm(bank[6][0:96, :], wbcT[:, hf, :], xc[:, hf, CW * c:CW * (c + 1)],
                             start=(hf == 0), stop=(hf == HALVES - 1))
                ins.then_inc(bc_ps, 1)
                if c:
                    pe.wait_ge(bnd_b_done, 2 * c)
                for i in range(TPC):
                    for hf in range(HALVES):
                        t1 = CW * c + P * i
                        ins = mm(bank[7][:, NST * i:NST * (i + 1)], xc[:, hf, t1:t1 + P], wxT[:, hf, DTR:DTR + NST],
                                 start=(i == 0 and hf == 0), stop=(hf == HALVES - 1), skip_group_check=True)
                ins.then_inc(bt_ps, 1)
                pe.wait_ge(dtl_done, c + 1)
                for hf in range(HALVES):
                    if hf == 0:
                        pe.wait_ge(silu_done, 4 * c + 4)
                    mm(bank[1 + hf], wdtT[:, P * hf:P * (hf + 1)], dtl[:, c % 2, :], start=True,
                       stop=True).then_inc(dt_ps, 1)
                pe.wait_ge(sp_a_done, 2 * (c + 1))
                pe.wait_ge(diag_done, c + 1)
                for i in range(TPC):
                    ins = mm(bank[7][:, P * i:P * (i + 1)], ones[:, :], diag[:, i, :], start=(i == 0),
                             stop=(i == TPC - 1), skip_group_check=True)
                ins.then_inc(bm_ps, 1)
            pe.wait_ge(over_done, 1)
            mm(bank[5][0:1, 0:1], over[:, :], ones[:, 0:1], start=True, stop=True).then_inc(over_ps, 1)

            pe.wait_ge(consts, 14)
            pe.wait_ge(bcs_done, CHUNKS)
            pe.wait_ge(bnd_b_done, 2 * CHUNKS)
            pe.wait_ge(flag_done, 1)
            pe.wait_ge(silu_done, 4 * CHUNKS)

            def spread(n_):
                c, n = divmod(n_, NST)
                if n_ >= 2:
                    pe.wait_ge(bu_done, 2 * (n_ - 2) + 2)
                mm(bank[2 + n_ % 2], pick[:, n, :], bcs[:, CW * c:CW * (c + 1)], start=True,
                   stop=True).then_inc(b_ps, 1)
                if n_ >= 2:
                    pe.wait_ge(c_done, n_ - 1)
                mm(bank[4 + n_ % 2], pick[:, NST + n, :], bcs[:, CW * c:CW * (c + 1)], start=True,
                   stop=True).then_inc(c_ps, 1)

            spread(0)
            spread(1)
            for n_ in range(CHUNKS * NST):
                c, n = divmod(n_, NST)
                if n_ + 2 < CHUNKS * NST:
                    spread(n_ + 2)
                for hf in range(HALVES):
                    m = 2 * n_ + hf
                    if n == 0 and c >= 2:
                        pe.wait_ge(y_done, 2 * (c - 2) + hf + 1)
                    pe.wait_ge(hc_done, m + 1)
                    mm(y_bank(c, hf), ident[:, :], hc_ring[m % NB], start=(n == 0),
                       stop=(n == NST - 1)).then_inc(hc_used, 1)

            for c in range(CHUNKS):
                pe.wait_ge(y_done, 2 * (c + 1))
                if c == 0:
                    pe.wait_ge(bu_done, 2 * CHUNKS * NST)
                if c >= 2:
                    pe.wait_ge(x3_done, c - 1)
                dst = bank[2 + c % 2]
                for i in range(TPC):
                    t1 = CW * c + P * i
                    for hf in range(HALVES):
                        ins = mm(dst[:, P * i:P * (i + 1)], sz[:, hf, t1:t1 + P], woutT[:, hf, :],
                                 start=(i == 0 and hf == 0), stop=(hf == HALVES - 1), skip_group_check=True)
                ins.then_inc(yout_ps, 1)
            pe.wait_ge(c_done, CHUNKS * NST)
            for c in range(CHUNKS):
                pe.wait_ge(xn_done[3], c + 1)
                if c:
                    pe.wait_ge(xT_done[3], c)
                transposed_chunk(3, c, xn, bank[0])
                pe.wait_ge(xT_done[3], c + 1)
                if c >= 2:
                    pe.wait_ge(x4_done, c - 1)
                dst = bank[4 + c % 2]
                for i in range(TPC):
                    mm(dst[:, P * i:P * (i + 1)], xTc[c][:, P * i:P * (i + 1)], wlT[:, :],
                       start=(i == 0), stop=False, skip_group_check=True)
                    ins = mm(dst[:, P * i:P * (i + 1)], ones[0:1, :], b_l[0:1, :],
                             start=False, stop=(i == TPC - 1), skip_group_check=True)
                ins.then_inc(fin_ps, 1)

        @block.scalar
        def _(act):
            f = nc.scalar.activation

            def ln_rstd(k, c):
                t = TILES * k + TPC * c
                act.wait_ge(moments_of[k], c + 1)
                f(lnvar[:, t:t + TPC], moments[:, t:t + TPC, 1], ACT.Ln, bias=eps_col[:, 0:1]).then_inc(lnvar_of[k], 1)
                act.wait_ge(lnvar_of[k], c + 1)
                f(rstd[:, t:t + TPC], lnvar[:, t:t + TPC], ACT.Exp, scale=-0.5).then_inc(rstd_of[k], 1)

            def take_xT(k, c, src):
                act.wait_ge(xT_ps[k], c + 1)
                f(xTc[c], src, ACT.Copy).then_inc(xT_done[k], 1)

            nc.scalar.preload_act_table_set("natural_log_exp_and_others")
            d = lambda dst, src, **k: act.dma_start(dst, src, **k).then_inc(weights_in, 16)
            d(w_fc[:], a["L0_ffn_w_fc"].rearrange("(m p) e -> p m e", p=P))
            d(w_pj[:], a["L0_ffn_w_proj"])
            d(w_in[:], a["L1_attn_W_in"].rearrange("(m p) e -> p m e", p=P))
            d(conv_w[:], a["L1_attn_conv_w"].rearrange("(h p) o k -> p h (o k)", p=P))
            d(conv_b[:], a["L1_attn_conv_b"].rearrange("(h p) -> p h", p=P), allow_slow_non_contiguous=True)
            d(a_log[:], a["L1_attn_A_log"].rearrange("(h p) n -> p h n", p=P))
            d(w_u[:], a["L0_ffn_u"].rearrange("(m p) r -> p m r", p=P))
            d(fb[:], a["L0_ffn_fast_b"])
            d(w_v[:], a["L0_ffn_v"])
            d(gate[0:RANK, :], a["L0_ffn_gate"].to_broadcast([RANK, 1]))
            d(w_x[:], a["L1_attn_W_x"])
            d(w_dt[:], a["L1_attn_W_dt"].rearrange("(h p) r -> p h r", p=P))
            d(b_dt[:], a["L1_attn_b_dt"].rearrange("(h p) -> p h", p=P), allow_slow_non_contiguous=True)
            d(d_par[:], a["L1_attn_D_param"].rearrange("(h p) -> p h", p=P), allow_slow_non_contiguous=True)
            d(w_out[:], a["L1_attn_W_out"])
            d(w_l[:], a["L1_ffn_W"])
            d(b_l[0:1, :], a["L1_ffn_b"].rearrange("(a o) -> a o", a=1))
            d(l_down[:], a["L1_ffn_lora_down"])
            d(l_up[:], a["L1_ffn_lora_up"])
            d(d_aux[:], a["L1_ffn_down_aux"])
            d(u_aux[:], a["L1_ffn_up_aux"])

            act.wait_ge(eps_set, 1)
            for c in range(CHUNKS):
                ln_rstd(0, c)
                take_xT(0, c, bank[0])
                act.wait_ge(qkv_ps, 3 * c + 3)
                act.wait_ge(consts, 10)
                f(vaug[:, TPC * c:TPC * (c + 1), :, 0:DK],
                  bank[3].rearrange("p (i h d) -> p i h d", i=TPC, h=HEADS), ACT.Copy).then_inc(v_taken, 1)

            def took(ins):
                ins.then_inc(prep_act, 1)

            act.wait_ge(weights_in, 16 * N_WEIGHTS)
            f(neg_a[:, :, :], a_log[:, :, :], ACT.Exp).then_inc(act_step, 1)
            act.wait_ge(prep_pe, 1)
            took(f(uT[:, :], prep_bank(0)[0:RANK, :], ACT.Copy))
            act.wait_ge(prep_pe, 2)
            b1 = prep_bank(1)
            f(fbT[:, :], b1[0:RANK, 0:RANK], ACT.Copy)
            f(ldT[:, :], b1[0:DDIM, 32:32 + LR], ACT.Copy)
            f(luT[:, :], b1[0:LR, 64:64 + UDIM], ACT.Copy)
            took(f(uaT[:, :], b1[0:UDIM, P:2 * P], ACT.Copy))
            act.wait_ge(prep_pe, 3)
            b2 = prep_bank(2)
            f(zT[:, :], b2[:, 0:2 * P], ACT.Copy)
            took(f(woutT[:, :, :].rearrange("p h e -> p (h e)"), b2[:, 2 * P:4 * P], ACT.Copy))
            act.wait_ge(prep_pe, 4)
            b3 = prep_bank(3)
            wx_ps = b3[:, 0:2 * P].rearrange("p (h e) -> p h e", h=2)
            f(wxT[:, :, :], wx_ps[:, :, 0:96], ACT.Copy)
            for g in range(3):
                f(wbcT[:, :, 32 * g:32 * (g + 1)], wx_ps[:, :, DTR:96], ACT.Copy)
            took(f(wdtT[:, :], b3[0:DTR, 2 * P:4 * P], ACT.Copy))
            for g in range(2):
                act.wait_ge(prep_pe, 5 + g)
                took(f(tapT[:, 2 * g:2 * g + 2, :].rearrange("p k d -> p (k d)"), prep_bank(4 + g), ACT.Copy))
            act.wait_ge(prep_pe, 7)
            took(f(pjT[:, :, :].rearrange("p m e -> p (m e)"), prep_bank(6), ACT.Copy))
            act.wait_ge(prep_pe, 8)
            f(q1[:, :], prep_bank(7)[0:RANK, 0:D], ACT.Copy, scale=gate[0:RANK, 0:1])
            took(f(r1[:, :], prep_bank(7)[0:LR, P:2 * P], ACT.Copy))
            act.wait_ge(prep_pe, 9)
            took(f(r2[:, :], prep_bank(8)[0:UDIM, 0:D], ACT.Copy))
            act.wait_ge(prep_pe, 10)
            took(f(fcT[:, :], prep_bank(9), ACT.Copy))
            act.wait_ge(prep_pe, 11)
            took(f(wlT[:, :], prep_bank(10)[:, 0:D], ACT.Copy))

            def take_max(u):
                act.wait_ge(maxT_ps, u + 1)
                if u >= 2:
                    act.wait_ge(max_rows[u % 2], 64 * (u // 2))
                f(maxT[:, u % 2, :], misc.bitcast(BF16)[0:12, 0:CW], ACT.Copy).then_inc(maxT_done, 1)

            def take_out(u):
                act.wait_ge(pv_done, step_base[u + 1])
                if u >= 2:
                    act.wait_ge(oT_ps, u - 1)
                f(oT[:, u % 2, :], pv_ps, ACT.Copy).then_inc(pv_taken, 1)

            def take_projection(c):
                act.wait_ge(attnT_ps, c + 1)
                if c:
                    act.wait_ge(wo_ps, c)
                f(attnT[:, :], misc, ACT.Copy).then_inc(attnT_done, 1)
                act.wait_ge(wo_ps, c + 1)
                f(sub[:, TPC * c:TPC * (c + 1), :].rearrange("p i e -> p (i e)"), misc,
                  ACT.Copy).then_inc(sub_done, 1)

            for u in range(FIRST):
                take_max(u)
            for u, (c, _) in enumerate(unit):
                for j in range(steps[u]):
                    s_ = step_base[u] + j
                    q0 = max(0, P * (j - TPC * c))
                    for pair in range(2):
                        act.wait_ge(sT_ps, 2 * s_ + pair + 1)
                        if s_ >= 3:
                            act.wait_ge(pv_done, s_ - 2)
                        f(probs[:, s_ % 3, 2 * pair:2 * pair + 2, q0:CW], st_ps[:, 2 * pair:2 * pair + 2, q0:CW],
                          ACT.Exp, scale=DK ** -0.5).then_inc(exp_done, 1)
                    if j == 0 and u:
                        take_out(u - 1)
                    for v in turn_at[s_]:
                        take_max(v)
                    if j == 3 and u and u % QUADS == 0:
                        take_projection(u // QUADS - 1)
            take_out(UNITS - 1)
            take_projection(CHUNKS - 1)

            for c in range(CHUNKS):
                ln_rstd(1, c)
            for c in range(CHUNKS):
                ln_rstd(2, c)
                take_xT(1, c, bank[0])
                for m in range(HT):
                    act.wait_ge(fc_ps, HT * c + m + 1)
                    if c:
                        act.wait_ge(relu2_done, HT * (c - 1) + m + 1)
                    f(relu[:, m, :], bank[1 + m], ACT.Relu).then_inc(relu_done, 1)
                if c:
                    ln_rstd(3, c - 1)
            ln_rstd(3, CHUNKS - 1)

            for c in range(CHUNKS):
                t = slice(CW * c, CW * (c + 1))
                ln_rstd(4, c)
                take_xT(2, c, bank[0])
                for hf in range(HALVES):
                    act.wait_ge(pre_ps, 4 * c + hf + 1)
                    f(xc[:, hf, t], bank[1 + hf], ACT.Silu, bias=conv_b[:, hf:hf + 1]).then_inc(silu_done, 1)
                for hf in range(HALVES):
                    act.wait_ge(pre_ps, 4 * c + hf + 3)
                    f(sz[:, hf, t], bank[3 + hf], ACT.Silu).then_inc(silu_done, 1)
                act.wait_ge(dtl_ps, c + 1)
                if c >= 2:
                    act.wait_ge(dt_ps, 2 * (c - 1))
                f(dtl[:, c % 2, :], bank[5][0:DTR, :], ACT.Copy).then_inc(dtl_done, 1)
                for hf in range(HALVES):
                    act.wait_ge(sp_a_done, 2 * c + hf + 1)
                    f(sp_b[:, hf, :], sp_a[:, hf, :], ACT.Exp).then_inc(sp_exp, 1)
                for hf in range(HALVES):
                    act.wait_ge(sp_exp, 2 * c + hf + 1)
                    f(sp_a[:, hf, :], sp_b[:, hf, :], ACT.Ln, bias=1.0).then_inc(sp_ln, 1)
                for hf in range(HALVES):
                    act.wait_ge(delta_done, 2 * c + hf + 1)
                    if c:
                        act.wait_ge(bnd_done, 2 * (c - 1) + hf + 1)
                    act.wait_ge(prep_dve, 4)
                    f(bnd_a[:, hf, :], delta[:, hf, t], ACT.Exp, scale=a_max[:, hf:hf + 1]).then_inc(bnd_exp, 1)
                for hf in range(HALVES):
                    act.wait_ge(bnd_b_done, 2 * c + hf + 1)
                    f(bnd_h[:, hf, :], bnd_b[:, hf, :], ACT.Abs).then_inc(bnd_abs, 1)

            for n_ in range(CHUNKS * NST):
                c, n = divmod(n_, NST)
                act.wait_ge(c_ps, n_ + 1)
                if n_ >= NC_RING:
                    act.wait_ge(hc_done, 2 * (n_ - NC_RING) + 2)
                f(c_ring[n_ % NC_RING], bank[4 + n_ % 2], ACT.Copy).then_inc(c_done, 1)
                for hf in range(HALVES):
                    m = 2 * n_ + hf
                    if m >= NA:
                        act.wait_ge(h_done, m - NA + 1)
                    f(a_ring[m % NA], delta[:, hf, CW * c:CW * (c + 1)], ACT.Exp,
                      scale=neg_a[:, hf, n:n + 1]).then_inc(decay_done, 1)

            for c in range(CHUNKS):
                ln_rstd(5, c)
            for c in range(CHUNKS):
                ln_rstd(6, c)
                take_xT(3, c, bank[0])
                if c:
                    ln_rstd(7, c - 1)
            ln_rstd(7, CHUNKS - 1)

        @block.vector
        def _(dve):
            v = nc.vector
            step = [0]

            def chained(ins):
                ins.then_inc(dve_step, 1)
                step[0] += 1
                dve.wait_ge(dve_step, step[0])

            def ln_stats(k, c, tile_of):
                t = TILES * k + TPC * c
                for i in range(TPC):
                    ins = v.bn_stats(stats[:, t % (2 * TILES) + i, :], tile_of(i))
                ins.then_inc(stats_of[k], 1)
                dve.wait_ge(stats_of[k], c + 1)
                for i in range(TPC):
                    ins = v.bn_aggr(moments[:, t + i, :], stats[:, t % (2 * TILES) + i, :])
                ins.then_inc(moments_of[k], 1)

            def normalised(k, c, tile_of, out):
                t = TILES * k + TPC * c
                dve.wait_ge(rstd_of[k], c + 1)
                for i in range(TPC):
                    ins = v.tensor_scalar(out[:, c % 2, i, :], tile_of(i), moments[:, t + i, 0:1],
                                          rstd[:, t + i:t + i + 1], ALU.subtract, ALU.mult)
                return ins

            def x_tile(c):
                return lambda i: x[:, TPC * c + i, :]

            def ps_tile(b):
                return lambda i: b[:, P * i:P * (i + 1)]

            def pre_stats(k, c):
                ln_stats(k, c, x_tile(c))

            def pre_norm(k, j, c):
                if c >= 2:
                    dve.wait_ge(xT_ps[j], c - 1)
                normalised(k, c, x_tile(c), xn).then_inc(xn_done[j], 1)

            def post_norm(k, c, tile_of, done):
                chained(normalised(k, c, tile_of, nrm))
                xs = x[:, TPC * c:TPC * (c + 1), :]
                v.tensor_tensor(xs, xs, nrm[:, c % 2, :, :], ALU.add).then_inc(done, 1)
                dve.wait_ge(done, c + 1)

            v.memset(eps_col[:, :], EPS).then_inc(eps_set, 1)
            v.memset(arena_q[:, :], 0.0).then_inc(pads, 1)
            v.memset(ks[PAIR:P, :, :], 1.0).then_inc(pads, 1)

            def split_parts(c):
                if c >= 2:
                    dve.wait_ge(parts_stored[c - 2], 32)
                for m in range(2):
                    dve.wait_ge(qkv_ps, 3 * c + m + 1)
                    ins = v.tensor_copy(parts[:, c % 2, m, 0, :], bank[1 + m])
                chained(ins)
                for m in range(2):
                    ins = v.tensor_tensor(resid[:, m, :], bank[1 + m], parts[:, c % 2, m, 0, :], ALU.subtract)
                chained(ins)
                for m in range(2):
                    ins = v.tensor_copy(parts[:, c % 2, m, 1, :], resid[:, m, :])
                chained(ins)
                for m in range(2):
                    v.tensor_tensor(parts[:, c % 2, m, 2, :], resid[:, m, :], parts[:, c % 2, m, 1, :],
                                    ALU.subtract).then_inc(parts_done, 1)
                dve.wait_ge(parts_done, 2 * c + 2)

            for c in range(CHUNKS):
                dve.wait_ge(x_in[c], 16)
                pre_stats(0, c)
                pre_norm(0, 0, c)
                if c:
                    split_parts(c - 1)
            split_parts(CHUNKS - 1)

            dve.wait_ge(weights_in, 16 * N_WEIGHTS)
            for k in range(CONV):
                for hf in range(HALVES):
                    ins = v.tensor_scalar(w_tap[:, k, hf, :], w_in[:, hf, :], conv_w[:, hf, k:k + 1], None, ALU.mult)
            ins.then_inc(prep_dve, 1)
            v.tensor_reduce(scl[:, 0, 0:HT], w_fc[:, :, :], AX.X, ALU.add, apply_absolute_value=True)
            chained(v.tensor_reduce(scl[:, 0, HT:HT + 1], w_pj[:, :], AX.X, ALU.add, apply_absolute_value=True))
            v.tensor_scalar(scl[:, 1, 0:HT], scl[:, 0, 0:HT], 1.0 / D, EPS, ALU.mult, ALU.max)
            chained(v.tensor_scalar(scl[:, 1, HT:HT + 1], scl[:, 0, HT:HT + 1], 1.0 / HIDDEN, EPS, ALU.mult, ALU.max))
            chained(v.tensor_scalar(scl[:, 2, :], scl[:, 1, :], 0.5, None, ALU.mult))
            chained(v.tensor_scalar(scl[:, 0, :], scl[:, 1, :], -0.5, None, ALU.mult))

            def ternary(out, w, col):
                n = w.shape[1]
                chained(v.tensor_scalar(tmp_w[:, 0, 0:n], w, scl[:, 2, col:col + 1], None, ALU.is_gt))
                chained(v.scalar_tensor_tensor(tmp_w[:, 1, 0:n], w, scl[:, 0, col:col + 1], tmp_w[:, 0, 0:n],
                                               ALU.is_lt, ALU.subtract))
                chained(v.scalar_tensor_tensor(tmp_w[:, 0, 0:n], tmp_w[:, 1, 0:n], -1.0, w, ALU.mult, ALU.subtract))
                chained(v.tensor_tensor(tmp_w[:, 1, 0:n], w, tmp_w[:, 0, 0:n], ALU.add))
                return v.tensor_scalar(out, tmp_w[:, 1, 0:n], scl[:, 1, col:col + 1], None, ALU.mult)

            ternary(tern_pj[:, :], w_pj[:, :], HT).then_inc(prep_dve, 1)
            dve.wait_ge(prep_dve, 2)
            for m in range(HT):
                ins = ternary(tern_fc[:, m, :], w_fc[:, m, :], m)
                if m < HT - 1:
                    chained(ins)
            ins.then_inc(prep_dve, 1)
            dve.wait_ge(act_step, 1)
            chained(v.tensor_scalar(neg_a[:, :, :], neg_a[:, :, :], -1.0, None, ALU.mult))
            v.tensor_reduce(a_max[:, :], neg_a[:, :, :], AX.X, ALU.max).then_inc(prep_dve, 1)

            def piece_max(w_, p):
                c, _ = unit[w_]
                i, n, g = pieces[w_][p]
                gp = piece_base[w_] + p
                dve.wait_ge(scores_ps, gp + 1)
                if gp >= 2:
                    dve.wait_ge(scores_max, gp - 1)
                out = maxcol[:, w_ % 2, i, n, g:g + 1]
                src = qk_ps[gp % 2]
                if g < c:
                    v.reduce_max(out, src, AX.X).then_inc(scores_max, 1)
                else:
                    w = P * (i + 1)
                    v.tensor_tensor_reduce(junk[:, gp % 2, 0:w], src[:, 0:w], mask_qk[:, CW - w:CW], 1.0, LOWEST,
                                           ALU.add, ALU.max, out).then_inc(scores_max, 1)

            def finish_max(w_):
                b = w_ % 2
                dve.wait_ge(scores_max, piece_base[w_ + 1])
                if w_ >= 2:
                    dve.wait_ge(maxT_ps, w_ - 1)
                chained(v.tensor_reduce(rowmax[:, b, :, :], maxcol[:, b, :, :, 0:unit[w_][0] + 1], AX.X, ALU.max))
                chained(v.tensor_scalar(maxparts[:, b, :, :, 0], rowmax[:, b, :, :], -1.0, None, ALU.mult))
                chained(v.scalar_tensor_tensor(maxres[:, b, :, :], rowmax[:, b, :, :], -1.0, maxparts[:, b, :, :, 0],
                                               ALU.mult, ALU.subtract))
                chained(v.tensor_copy(maxparts[:, b, :, :, 1], maxres[:, b, :, :]))
                v.tensor_tensor(maxparts[:, b, :, :, 2], maxres[:, b, :, :], maxparts[:, b, :, :, 1],
                                ALU.subtract).then_inc(max_parts, 1)

            def take_heads(u):
                c, quad = unit[u]
                o = misc.rearrange("p (i n e) -> p i n e", i=TPC, n=4)
                dve.wait_ge(oT_ps, u + 1)
                if c >= 2:
                    dve.wait_ge(attnT_ps, c - 1)
                chained(v.reciprocal(rsum[:, u % 2, :, :], o[:, :, :, DK]))
                v.tensor_tensor(attn[:, c % 2, :, 32 * quad:32 * quad + 32].rearrange("p i (n d) -> p i n d", n=4),
                                o[:, :, :, 0:DK],
                                rsum[:, u % 2, :, :].rearrange("p i (n a) -> p i n a", a=1).to_broadcast([P, TPC, 4, DK]),
                                ALU.mult).then_inc(attn_done, 1)

            dve.wait_ge(consts, 10)
            for u in range(FIRST):
                for p in range(len(pieces[u])):
                    piece_max(u, p)
                finish_max(u)
            for u in range(UNITS):
                for j in range(steps[u]):
                    for w_, p in pieces_at[step_base[u] + j]:
                        piece_max(w_, p)
                        if p == len(pieces[w_]) - 1:
                            finish_max(w_)
                    if j == 2 and u:
                        take_heads(u - 1)
            take_heads(UNITS - 1)

            for c in range(CHUNKS):
                dve.wait_ge(sub_done, c + 1)
                ln_stats(1, c, lambda i, c=c: sub[:, TPC * c + i, :])
                post_norm(1, c, lambda i, c=c: sub[:, TPC * c + i, :], x1_done)
            pre_stats(2, 0)
            for c in range(CHUNKS):
                pre_norm(2, 1, c)
                if c + 1 < CHUNKS:
                    pre_stats(2, c + 1)
                for m in range(HT):
                    dve.wait_ge(relu_done, HT * c + m + 1)
                    if c >= 2:
                        dve.wait_ge(pj_ps, c - 1)
                    v.tensor_tensor(relu2[:, c % 2, m, :], relu[:, m, :], relu[:, m, :],
                                    ALU.mult).then_inc(relu2_done, 1)
                if c:
                    dve.wait_ge(pj_ps, c)
                    ln_stats(3, c - 1, ps_tile(bank[5 + (c - 1) % 2]))
                    post_norm(3, c - 1, ps_tile(bank[5 + (c - 1) % 2]), x2_done)
            dve.wait_ge(pj_ps, CHUNKS)
            ln_stats(3, CHUNKS - 1, ps_tile(bank[5 + (CHUNKS - 1) % 2]))
            post_norm(3, CHUNKS - 1, ps_tile(bank[5 + (CHUNKS - 1) % 2]), x2_done)

            for c in range(CHUNKS):
                t = slice(CW * c, CW * (c + 1))
                pre_stats(4, c)
                pre_norm(4, 2, c)
                dve.wait_ge(bc_ps, c + 1)
                chained(v.tensor_copy(bc_hi[:, :], bank[6][0:96, :]))
                chained(v.tensor_tensor(bc_r[:, :], bank[6][0:96, :], bc_hi[:, :], ALU.subtract))
                chained(v.tensor_copy(bc_mid[:, :], bc_r[:, :]))
                v.tensor_copy(bcs[0:32, t], bc_hi[0:32, :])
                v.tensor_copy(bcs[32:64, t], bc_mid[32:64, :])
                v.tensor_tensor(bcs[64:96, t], bc_r[64:96, :], bc_mid[64:96, :], ALU.subtract).then_inc(bcs_done, 1)
                dve.wait_ge(bt_ps, c + 1)
                chained(v.tensor_reduce(bmax[:, c, :], bank[7][:, 0:TPC * NST].rearrange("p (i n) -> p i n", i=TPC),
                                        AX.X, ALU.max, apply_absolute_value=True))
                if c:
                    dve.wait_ge(bm_ps, c)
                for i in range(TPC):
                    ins = v.tensor_scalar(diag[:, i, :], ident[:, :], bmax[:, c, i:i + 1], None, ALU.mult)
                ins.then_inc(diag_done, 1)
                for hf in range(HALVES):
                    dve.wait_ge(dt_ps, 2 * c + hf + 1)
                    v.tensor_scalar(sp_a[:, hf, :], bank[1 + hf], b_dt[:, hf:hf + 1], 20.0, ALU.add,
                                    ALU.min).then_inc(sp_a_done, 1)
                for hf in range(HALVES):
                    dve.wait_ge(sp_ln, 2 * c + hf + 1)
                    v.tensor_scalar(delta[:, hf, t], sp_a[:, hf, :], 1e-4, 10.0, ALU.add,
                                    ALU.min).then_inc(delta_done, 1)
                dve.wait_ge(delta_done, 2 * (c + 1))
                dve.wait_ge(bm_ps, c + 1)
                for hf in range(HALVES):
                    dve.wait_ge(dxc_done, 2 * c + hf + 1)
                    v.tensor_tensor(bnd_b[:, hf, :], dxc[:, hf, t], bank[7], ALU.mult).then_inc(bnd_b_done, 1)
                for hf in range(HALVES):
                    dve.wait_ge(bnd_abs, 2 * c + hf + 1)
                    dve.wait_ge(bnd_exp, 2 * c + hf + 1)
                    chained(v.tensor_scalar(bnd_h[:, hf, :], bnd_h[:, hf, :], 10.0, None, ALU.min))
                    chained(v.tensor_tensor_scan(bnd_b[:, hf, :], bnd_a[:, hf, :], bnd_h[:, hf, :],
                                                 bnd_c[:, hf:hf + 1] if c else 0.0, ALU.mult, ALU.add))
                    v.tensor_copy(bnd_c[:, hf:hf + 1], bnd_b[:, hf, CW - 1:CW])
                    v.reduce_max(bnd_m[:, c, hf:hf + 1], bnd_b[:, hf, :], AX.X).then_inc(bnd_done, 1)
                dve.wait_ge(bnd_done, 2 * (c + 1))
            chained(v.tensor_reduce(bmax[:, 0, 0:1], bnd_m[:, :, :], AX.XY, ALU.max))
            v.tensor_scalar(over[:, :], bmax[:, 0, 0:1], H_BOUND, None, ALU.is_le).then_inc(over_done, 1)
            dve.wait_ge(over_ps, 1)
            v.tensor_copy(over_i[:, :], bank[5][0:1, 0:1]).then_inc(flag_done, 1)
            dve.wait_ge(flag_done, 1)
            sure = dve.value_load(over_i[0:1, 0:1])

            def scan_input(m):
                n_, hf = divmod(m, 2)
                c = n_ // NST
                b = bu_ring[m % NB]
                dve.wait_ge(b_ps, n_ + 1)
                if m >= NB:
                    dve.wait_ge(h_done, m - NB + 1)
                v.tensor_tensor(b, dxc[:, hf, CW * c:CW * (c + 1)], bank[2 + n_ % 2], ALU.mult).then_inc(bu_done, 1)

            def clip_input(m):
                b = bu_ring[m % NB]
                dve.wait_ge(bu_done, m + 1)
                v.tensor_scalar(b, b, 10.0, -10.0, ALU.min, ALU.max).then_inc(clip_done, 1)

            def ready_for_scan(m):
                dve.wait_ge(clip_done, m + 1)
                dve.wait_ge(decay_done, m + 1)
                if m >= NB:
                    dve.wait_ge(hc_done, m - NB + 1)

            def start_of(m):
                n_, hf = divmod(m, 2)
                return carry[:, hf, n_ % NST:n_ % NST + 1]

            def finish_y(c):
                t = slice(CW * c, CW * (c + 1))
                for hf in range(HALVES):
                    dve.wait_ge(hc_used, 2 * NST * (c + 1) - 1 + hf)
                    ins = v.scalar_tensor_tensor(bnd_a[:, hf, :], xc[:, hf, t], d_par[:, hf:hf + 1], y_bank(c, hf),
                                                 ALU.mult, ALU.add)
                    ins.then_inc(y_sum, 1)
                for hf in range(HALVES):
                    dve.wait_ge(y_sum, 2 * c + hf + 1)
                    v.tensor_scalar(bnd_b[:, hf, :], bnd_a[:, hf, :], 50.0, -50.0, ALU.min, ALU.max).then_inc(y_clip, 1)
                for hf in range(HALVES):
                    dve.wait_ge(y_clip, 2 * c + hf + 1)
                    v.tensor_tensor(sz[:, hf, t], bnd_b[:, hf, :], sz[:, hf, t], ALU.mult).then_inc(y_done, 1)

            M = CHUNKS * NST * HALVES
            Y_LAG = 5
            v.memset(carry[:, :, :], 0.0).then_inc(carry_set, 1)
            dve.wait_ge(carry_set, 1)

            def steps_of_scan(scan):
                scan_input(0)
                for m in range(M):
                    if m + 1 < M:
                        scan_input(m + 1)
                    clip_input(m)
                    ready_for_scan(m)
                    scan(m)
                    c, r = divmod(m, NST * HALVES)
                    if c and r == Y_LAG:
                        finish_y(c - 1)
                finish_y(CHUNKS - 1)

            def plain_scan(m):
                v.tensor_tensor_scan(h_ring[m % NB], a_ring[m % NA], bu_ring[m % NB], start_of(m), ALU.mult,
                                     ALU.add).then_inc(h_done, 1)

            def clipped_scan(m):
                h, dec, bu = h_ring[m % NB], a_ring[m % NA], bu_ring[m % NB]
                v.tensor_copy(h_last[:, :], start_of(m))
                dve.drain()
                with dve.Fori(0, CW) as i:
                    v.scalar_tensor_tensor(h_next[:, :], dec[:, bass.ds(i, 1)], h_last[:, 0:1], bu[:, bass.ds(i, 1)],
                                           ALU.mult, ALU.add)
                    dve.drain()
                    v.tensor_scalar(h_last[:, :], h_next[:, :], 20.0, -20.0, ALU.min, ALU.max)
                    dve.drain()
                    v.tensor_copy(h[:, bass.ds(i, 1)], h_last[:, :])
                dve.drain()
                v.tensor_copy(h_next[:, :], h_last[:, :]).then_inc(h_done, 1)

            with dve.If(sure == P):
                steps_of_scan(plain_scan)
            with dve.Else():
                steps_of_scan(clipped_scan)

            def after(k, c, b, ready, done):
                dve.wait_ge(ready, c + 1)
                ln_stats(k, c, ps_tile(b))
                post_norm(k, c, ps_tile(b), done)

            for c in range(CHUNKS):
                after(5, c, bank[2 + c % 2], yout_ps, x3_done)
            pre_stats(6, 0)
            for c in range(CHUNKS):
                pre_norm(6, 3, c)
                if c + 1 < CHUNKS:
                    pre_stats(6, c + 1)
                if c:
                    after(7, c - 1, bank[4 + (c - 1) % 2], fin_ps, x4_done)
            after(7, CHUNKS - 1, bank[4 + (CHUNKS - 1) % 2], fin_ps, x4_done)


_INS = ['L0_attn_x', 'L0_attn_WQ', 'L0_attn_WK', 'L0_attn_WV', 'L0_attn_WO', 'L0_ffn_fast_b', 'L0_ffn_w_fc',
        'L0_ffn_w_proj', 'L0_ffn_u', 'L0_ffn_v', 'L0_ffn_gate', 'L1_attn_W_in', 'L1_attn_conv_w', 'L1_attn_conv_b',
        'L1_attn_W_x', 'L1_attn_W_dt', 'L1_attn_b_dt', 'L1_attn_A_log', 'L1_attn_D_param', 'L1_attn_W_out',
        'L1_ffn_W', 'L1_ffn_b', 'L1_ffn_lora_down', 'L1_ffn_lora_up', 'L1_ffn_down_aux', 'L1_ffn_up_aux']


def kernel(**inputs):
    import numpy as np
    import concourse.bacc as bacc
    from concourse.bass_utils import run_bass_kernel_spmd as run

    nc = bacc.Bacc("TRN2", target_bir_lowering=False, num_devices=1)
    arrays, aps = {}, {}
    for name in _INS:
        arr = np.ascontiguousarray(inputs[name]).reshape(np.shape(inputs[name]) or (1, 1))
        arrays[f"in_{name}"] = arr
        aps[name] = nc.dram_tensor(f"in_{name}", arr.shape, mybir.dt.from_np(arr.dtype), kind="ExternalInput").ap()
    aps["out"] = nc.dram_tensor("out_x", (1, S, D), F32, kind="ExternalOutput").ap()
    build(nc, aps)
    return run(nc, [arrays], core_ids=[0]).results[0]["out_x"]
```

```python
from contextlib import ExitStack

import concourse.bass as bass
from concourse import mybir

ALU = mybir.AluOpType
ACT = mybir.ActivationFunctionType
AX = mybir.AxisListType
F32 = mybir.dt.float32
BF16 = mybir.dt.bfloat16
I32 = mybir.dt.int32

P = 128
S = 2048
D = 128
HEADS, DK = 16, 8
TILES = S // P
CW = 512
CHUNKS = S // CW
TPC = CW // P
QUADS = HEADS // 4
UNITS = CHUNKS * QUADS
HIDDEN, RANK = 512, 16
HT = HIDDEN // P
DI, NST, DTR, CONV = 256, 16, 64, 4
HALVES = DI // P
LR, DDIM, UDIM = 4, 100, 50
EPS = 1e-5
MASKED = -1.0e30
LOWEST = -3.0e38
ROUND = 6
SPLIT_Q = (0, 0, 1, 1, 0, 2)
SPLIT_K = (0, 1, 0, 1, 2, 0)
ROWS = ROUND * DK
PAIR = 2 * ROWS
AUG = PAIR + 3
NORMS = 8
H_BOUND = 19.99


def build(nc, a):
    ctx = ExitStack()
    with ctx:
        def sb(name, shape, dt=F32):
            return ctx.enter_context(nc.sbuf_tensor(name, shape, dt))

        def sem(name):
            return ctx.enter_context(nc.semaphore(name))

        st_ps = ctx.enter_context(nc.psum_tensor("st_ps", [P, 4, CW], F32))
        bank = [st_ps[:, i, :] for i in range(4)] + [
            ctx.enter_context(nc.psum_tensor(f"bank{i}", [P, CW], F32))[:, :] for i in range(4, 8)]
        qk_ps = [bank[4], bank[5]]
        pv_ps = bank[6]
        misc = bank[7]

        x = sb("x", [P, TILES, D])
        xn = sb("xn", [P, 2, TPC, D])
        xT = sb("xT", [P, 4 + S])
        xTc = [xT[:, 4 + CW * c:4 + CW * (c + 1)] for c in range(CHUNKS)]
        stats = sb("stats", [P, 2 * TILES, 6])
        moments = sb("moments", [P, NORMS * TILES, 2])
        lnvar = sb("lnvar", [P, NORMS * TILES])
        rstd = sb("rstd", [P, NORMS * TILES])
        nrm = sb("nrm", [P, 2, TPC, D])
        arena_q = sb("arena_q", [P, 8192])
        arena_k = sb("arena_k", [P, 8192])
        arena_v = sb("arena_v", [P, 8192])
        qs = arena_q[:, :].bitcast(BF16).rearrange("p (b h t) -> p b h t", b=2, h=HEADS)
        ks = arena_k[:, :].bitcast(BF16).rearrange("p (h t) -> p h t", h=8)
        vaug = arena_v[:, :].rearrange("p (j h e) -> p j h e", j=TILES, h=HEADS)
        parts = sb("parts", [P, 2, 2, 3, CW], BF16)
        probs = sb("probs", [P, 3, 4, CW])
        junk = sb("junk", [P, 2, CW], BF16)
        maxcol = sb("maxcol", [P, 2, TPC, 4, CHUNKS])
        rowmax = sb("rowmax", [P, 2, TPC, 4])
        maxres = sb("maxres", [P, 2, TPC, 4])
        maxparts = sb("maxparts", [P, 2, TPC, 4, 3], BF16)
        maxT = sb("maxT", [12, 2, CW], BF16)
        oT = sb("oT", [P, 2, CW])
        resid = oT
        rsum = sb("rsum", [P, 2, TPC, 4])
        attn = sb("attn", [P, 2, TPC, D])
        attnT = sb("attnT", [P, CW])
        sub = xT[:, 4:].rearrange("p (i e) -> p i e", e=D)
        xc = arena_q[:, 0:4096].rearrange("p (h t) -> p h t", h=2)
        sz = arena_q[:, 4096:8192].rearrange("p (h t) -> p h t", h=2)
        delta = arena_k[:, 0:4096].rearrange("p (h t) -> p h t", h=2)
        dxc = arena_k[:, 4096:8192].rearrange("p (h t) -> p h t", h=2)
        ring = arena_v[:, :].rearrange("p (r t) -> p r t", t=CW)
        NA, NB, NC_RING = 4, 3, 3
        a_ring = [ring[:, i, :] for i in range(0, 4)]
        bu_ring = [ring[:, i, :] for i in range(4, 7)]
        h_ring = [ring[:, i, :] for i in range(7, 10)]
        hc_ring = [ring[:, i, :] for i in range(10, 13)]
        c_ring = [ring[:, i, :] for i in range(13, 16)]
        flat = parts[:, :, :, :, :].rearrange("p a m s t -> p (a m s t)")
        bcs = flat[0:96, 0:S]
        bc_hi = flat[0:96, S:S + CW]
        bc_mid = flat[0:96, S + CW:S + 2 * CW]
        bc_r = flat[0:96, S + 2 * CW:S + 4 * CW].bitcast(F32)
        dtl = flat[0:DTR, S + 4 * CW:S + 8 * CW].bitcast(F32).rearrange("p (a t) -> p a t", a=2)
        sp_a, sp_b = ring[:, 0:2, :], ring[:, 2:4, :]
        carry = sb("carry", [P, HALVES, NST])
        relu = probs[:, 0, :, :]
        relu2 = probs[:, 1:3, :, :]
        ident = sb("ident", [P, P])
        ident_b = sb("ident_b", [P, P], BF16)
        ones = sb("ones", [P, P])
        mask_kq = sb("mask_kq", [P, P], BF16)
        mask_qk = sb("mask_qk", [P, CW])
        pick = sb("pick", [96, 2 * NST, P], BF16)
        w_qkvo = sb("w_qkvo", [P, 4, D])
        w_fc = probs[:, 0, 0, :].rearrange("p (m e) -> p m e", m=HT)
        w_pj = probs[:, 0, 1, :]
        fb = sb("fb", [RANK, RANK])
        w_u = sb("w_u", [P, HT, RANK])
        w_v = sb("w_v", [RANK, D])
        gate = sb("gate", [P, 1])
        w_in = probs[:, 0, 2, :].rearrange("p (m e) -> p m e", m=4)
        conv_w = sb("conv_w", [P, HALVES, CONV])
        conv_b = sb("conv_b", [P, HALVES])
        w_x = probs[0:96, 0, 3, 0:DI]
        w_dt = sb("w_dt", [P, HALVES, DTR])
        b_dt = sb("b_dt", [P, HALVES])
        a_log = sb("a_log", [P, HALVES, NST])
        d_par = sb("d_par", [P, HALVES])
        w_out = probs[:, 0, 3, DI:]
        w_l = probs[:, 1, 0, 0:D]
        b_l = sb("b_l", [P, D])
        l_down = sb("l_down", [LR, DDIM])
        l_up = sb("l_up", [UDIM, LR])
        d_aux = probs[0:DDIM, 1, 0, D:2 * D]
        u_aux = probs[:, 1, 0, 2 * D:2 * D + UDIM]
        tern_fc = attn[:, 0, :, :]
        tern_pj = attn[:, 1, :, :].rearrange("p i e -> p (i e)")
        tmp_w = nrm[:, :, :, :].rearrange("p a i e -> p a (i e)")
        scl = sb("scl", [P, 3, HT + 1])
        fcT = sb("fcT", [P, HIDDEN])
        pjT = sb("pjT", [P, HT, D])
        uT = probs[0:RANK, 1, 1, :]
        fbT = probs[0:RANK, 1, 2, 0:RANK]
        q1 = probs[0:RANK, 1, 2, D:2 * D]
        w_tap = oT[:, :, :].rearrange("p a t -> p (a t)").rearrange("p (k h e) -> p k h e", k=CONV, h=HALVES)
        tapT = sb("tapT", [P, CONV, DI])
        zT = sb("zT", [P, DI])
        wxT = sb("wxT", [P, HALVES, 96])
        wbcT = sb("wbcT", [P, HALVES, 96])
        wdtT = sb("wdtT", [DTR, DI])
        woutT = sb("woutT", [P, HALVES, D])
        neg_a = sb("neg_a", [P, HALVES, NST])
        a_max = sb("a_max", [P, HALVES])
        ldT = probs[0:DDIM, 1, 2, 16:16 + LR]
        luT = probs[0:LR, 1, 2, 32:32 + UDIM]
        uaT = probs[0:UDIM, 1, 2, 2 * D:3 * D]
        r1 = probs[0:LR, 1, 2, 3 * D:4 * D]
        r2 = probs[0:UDIM, 1, 3, 0:D]
        wlT = sb("wlT", [P, D])
        bmax = sb("bmax", [P, CHUNKS, TPC])
        diag = ring[:, 4, :].rearrange("p (i t) -> p i t", i=TPC)
        bnd_a, bnd_b, bnd_h = ring[:, 5:7, :], ring[:, 7:9, :], ring[:, 9:11, :]
        y_a, y_b = probs[:, 0, 0:2, :], probs[:, 0, 2:4, :]
        bnd_c = sb("bnd_c", [P, HALVES])
        bnd_m = sb("bnd_m", [P, CHUNKS, HALVES])
        over = sb("over", [P, 1])
        over_i = sb("over_i", [1, 1], I32)
        eps_col = sb("eps_col", [P, 1])
        h_last, h_next = sb("h_last", [P, 1]), sb("h_next", [P, 1])

        def prep_bank(n):
            return bank[6 + n % 2]

        def y_bank(c, hf):
            return bank[hf if c % 2 == 0 else 6 + hf]

        scratch = nc.dram_tensor("split_parts", (2, 3, P, S), BF16, kind="Internal").ap()

        x_in = [sem(f"x_in{c}") for c in range(CHUNKS)]
        wqkv_in, weights_in = sem("wqkv_in"), sem("weights_in")
        N_WEIGHTS = 21
        PREP_SLOTS = 11
        consts, consts_b = sem("consts"), sem("consts_b")
        stats_of = [sem(f"stats{k}") for k in range(8)]
        moments_of = [sem(f"moments{k}") for k in range(8)]
        lnvar_of = [sem(f"lnvar{k}") for k in range(8)]
        rstd_of = [sem(f"rstd{k}") for k in range(8)]
        dve_step = sem("dve_step")
        act_step = sem("act_step")
        xn_done = [sem(f"xn_done{k}") for k in range(4)]
        xT_ps = [sem(f"xT_ps{k}") for k in range(4)]
        xT_done = [sem(f"xT_done{k}") for k in range(4)]
        prep_dve, prep_pe, prep_act = sem("prep_dve"), sem("prep_pe"), sem("prep_act")
        qkv_ps, v_taken, parts_done = sem("qkv_ps"), sem("v_taken"), sem("parts_done")
        k_hi, q_hi = sem("k_hi"), sem("q_hi")
        parts_stored = [sem(f"parts_stored{c}") for c in range(CHUNKS)]
        stacked = [sem(f"stacked{c}") for c in range(CHUNKS)]
        pads = sem("pads")
        scores_ps, scores_max = sem("scores_ps"), sem("scores_max")
        max_parts, maxT_ps, maxT_done = sem("max_parts"), sem("maxT_ps"), sem("maxT_done")
        max_rows = [sem(f"max_rows{i}") for i in range(2)]
        sT_ps, exp_done, pv_done, pv_taken = sem("sT_ps"), sem("exp_done"), sem("pv_done"), sem("pv_taken")
        oT_ps, attn_done, attnT_ps, attnT_done = sem("oT_ps"), sem("attn_done"), sem("attnT_ps"), sem("attnT_done")
        wo_ps, sub_done = sem("wo_ps"), sem("sub_done")
        x1_done, x2_done, x3_done, x4_done = (sem(f"x{i}_done") for i in range(1, 5))
        fc_ps, relu_done, relu2_done, pj_ps = sem("fc_ps"), sem("relu_done"), sem("relu2_done"), sem("pj_ps")
        pad_done, pre_ps, silu_done = sem("pad_done"), sem("pre_ps"), sem("silu_done")
        dtl_ps, dtl_done, bc_ps, bcs_done, bmax_done = sem("dtl_ps"), sem("dtl_done"), sem("bc_ps"), sem("bcs_done"), sem("bmax_done")
        dt_ps, sp_a_done, sp_exp, sp_ln, delta_done, dxc_done = (sem(n) for n in ("dt_ps", "sp_a_done", "sp_exp", "sp_ln", "delta_done", "dxc_done"))
        bt_ps, diag_done, bm_ps, bnd_b_done, bnd_abs, bnd_exp, bnd_done = (sem(n) for n in ("bt_ps", "diag_done", "bm_ps", "bnd_b_done", "bnd_abs", "bnd_exp", "bnd_done"))
        over_done, over_ps, flag_done = sem("over_done"), sem("over_ps"), sem("flag_done")
        b_ps, c_ps, c_done, decay_done, bu_done, h_done, hc_done, y_ps, hc_used = (
            sem(n) for n in ("b_ps", "c_ps", "c_done", "decay_done", "bu_done", "h_done", "hc_done", "y_ps", "hc_used"))
        y_done, yout_ps, fin_ps, stored = (sem(n) for n in ("y_done", "yout_ps", "fin_ps", "stored"))
        clip_done, carry_set, y_sum, y_clip = (sem(n) for n in ("clip_done", "carry_set", "y_sum", "y_clip"))
        eps_set = sem("eps_set")

        unit = [(u // QUADS, u % QUADS) for u in range(UNITS)]
        pieces = [[(i, n, g) for g in range(c + 1) for i in range(TPC) for n in range(4)] for c, _ in unit]
        steps = [TPC * (c + 1) for c, _ in unit]
        piece_base = [sum(len(p) for p in pieces[:u]) for u in range(UNITS + 1)]
        step_base = [sum(steps[:u]) for u in range(UNITS + 1)]
        FIRST = 2
        LEAD = 3
        STEPS = step_base[UNITS]

        def deal_pieces():
            order = [(v, p) for v in range(FIRST, UNITS) for p in range(len(pieces[v]))]
            due = {max(step_base[v] - LEAD, 1): piece_base[v + 1] - piece_base[FIRST] for v in range(FIRST, UNITS)}
            at, done = [], 0
            for s in range(STEPS):
                need = [-(-(n - done) // (t - s)) for t, n in due.items() if t > s]
                upto = min(done + max(need + [0]), len(order))
                at.append(order[done:upto])
                done = upto
            return at

        pieces_at = deal_pieces()
        turn_at = [[v for v in range(FIRST, UNITS) if s and (v, len(pieces[v]) - 1) in pieces_at[s - 1]]
                   for s in range(STEPS)]
        misc_order = [("max", v) for v in range(FIRST)]
        for u in range(UNITS):
            for j in range(steps[u]):
                misc_order += [("max", v) for v in turn_at[step_base[u] + j]]
                misc_order += [("out", u - 1)] * (j == 2 and u > 0)
                misc_order += [("project", u // QUADS - 1)] * (j == 3 and u > 0 and u % QUADS == 0)
        misc_order += [("out", UNITS - 1), ("project", CHUNKS - 1)]

        ROUNDS = CHUNKS + 3
        LAST_PIECE = max(s for s in range(STEPS) if pieces_at[s])
        EARLY = [LAST_PIECE + 2, LAST_PIECE + 4]

        def in_round(k, lag):
            return 0 <= k - lag < CHUNKS

        Y_LAG, STATS5, NORM5, NORM6, STATS7, NORM7 = 5, 12, 15, 18, 25, 28
        YOUT_AT, RSTD5_AT, RSTD6_AT, XT3_AT, FIN_AT, RSTD7_AT = 4, 6, 8, 10, 11, 13

        block = ctx.enter_context(nc.Block())

        @block.sync
        def _(sp):
            xr = a["L0_attn_x"][0].rearrange("(i p) e -> p i e", p=P)
            for c in range(CHUNKS):
                sp.dma_start(x[:, TPC * c:TPC * (c + 1), :], xr[:, TPC * c:TPC * (c + 1), :]).then_inc(x_in[c], 16)
                if c == 0:
                    for n, w in enumerate(("WQ", "WK", "WV", "WO")):
                        sp.dma_start(w_qkvo[:, n, :], a[f"L0_attn_{w}"]).then_inc(wqkv_in, 16)

            def stack_q(c):
                for par in range(2):
                    for t in range(ROUND):
                        src = scratch[0, SPLIT_Q[t]].rearrange("(hp par d) t -> par d hp t", par=2, d=DK)[par]
                        row = ROWS * par + DK * t
                        sp.dma_start(qs[row:row + DK, c % 2, par::2, :], src[:, :, CW * c:CW * (c + 1)]).then_inc(stacked[c], 16)

            sp.wait_ge(pads, 2)
            for c in range(CHUNKS):
                for m in range(2):
                    sp.wait_ge(parts_done, 2 * c + m + 1)
                    sp.dma_start(scratch[m, :, :, CW * c:CW * (c + 1)].rearrange("s p t -> p s t"),
                                 parts[:, c % 2, m, :, :]).then_inc(parts_stored[c], 16)
                sp.wait_ge(parts_stored[c], 32)
                if c < 2:
                    stack_q(c)
                for par in range(2):
                    for t in range(ROUND):
                        src = scratch[1, SPLIT_K[t]].rearrange("(hp par d) t -> par d hp t", par=2, d=DK)[par]
                        row = ROWS * par + DK * t
                        sp.dma_start(ks[row:row + DK, :, CW * c:CW * (c + 1)],
                                     src[:, :, CW * c:CW * (c + 1)]).then_inc(stacked[c], 16)
            for u, (c, quad) in enumerate(unit):
                for c2 in range(2, CHUNKS):
                    if u in next(t for t in turn_at[step_base[QUADS * (c2 - 1)]:] if t)[:1]:
                        sp.wait_ge(sT_ps, 2 * step_base[QUADS * (c2 - 1)])
                        stack_q(c2)
                sp.wait_ge(maxT_done, u + 1)
                for n in range(4):
                    sp.dma_start(qs[PAIR:AUG, c % 2, 4 * quad + n, :],
                                 maxT[3 * n:3 * n + 3, u % 2, :]).then_inc(max_rows[u % 2], 16)
            outr = a["out"][0].rearrange("(i p) e -> p i e", p=P)
            for c in range(CHUNKS):
                sp.wait_ge(x4_done, c + 1)
                sp.dma_start(outr[:, TPC * c:TPC * (c + 1), :], x[:, TPC * c:TPC * (c + 1), :]).then_inc(stored, 16)
            sp.wait_ge(stored, 16 * CHUNKS)

        @block.gpsimd
        def _(pool):
            def chained(ins, n):
                ins.then_inc(consts, 1)
                pool.wait_ge(consts, n)

            chained(nc.gpsimd.memset(ident[:], 1.0), 1)
            chained(nc.gpsimd.affine_select(out=ident[:], in_=ident[:], compare_op=ALU.is_equal, fill=0.0, base=0,
                                            pattern=[[-1, P]], channel_multiplier=1), 2)
            nc.gpsimd.memset(ones[:], 1.0).then_inc(consts, 1)
            nc.gpsimd.memset(xT[:, 0:4], 0.0).then_inc(consts, 1)
            nc.gpsimd.tensor_copy(ident_b[:], ident[:]).then_inc(consts, 1)
            nc.gpsimd.memset(mask_kq[:], 0.0).then_inc(consts, 1)
            chained(nc.gpsimd.memset(mask_qk[:], 0.0), 7)
            nc.gpsimd.affine_select(out=mask_kq[:], in_=mask_kq[:], compare_op=ALU.is_ge, fill=MASKED, base=0,
                                    pattern=[[1, P]], channel_multiplier=-1).then_inc(consts, 1)
            nc.gpsimd.affine_select(out=mask_qk[:, CW - P:], in_=mask_qk[:, CW - P:], compare_op=ALU.is_ge,
                                    fill=MASKED, base=0, pattern=[[-1, P]], channel_multiplier=1).then_inc(consts, 1)
            nc.gpsimd.memset(vaug[:, :, :, DK:], 1.0).then_inc(consts, 1)
            chained(nc.gpsimd.memset(pick[:], 0.0), 11)
            for g in range(3):
                chained(nc.gpsimd.affine_select(out=pick[:], in_=pick[:], compare_op=ALU.not_equal, fill=1.0,
                                                base=-32 * g, pattern=[[-1, 2 * NST], [0, P]],
                                                channel_multiplier=1), 12 + g)
            for k in range(ROUNDS):
                if in_round(k, 0):
                    for m in range(HT):
                        pool.wait_ge(relu_done, HT * k + m + 1)
                        if k >= 2:
                            pool.wait_ge(pj_ps, k - 1)
                        nc.gpsimd.tensor_tensor(relu2[:, k % 2, m, :], relu[:, m, :], relu[:, m, :],
                                                ALU.mult).then_inc(relu2_done, 1)
                if in_round(k, 2):
                    c = k - 2
                    for hf in range(HALVES):
                        pool.wait_ge(delta_done, 2 * c + hf + 1)
                        pool.wait_ge(silu_done, 4 * c + hf + 1)
                        nc.gpsimd.tensor_tensor(dxc[:, hf, CW * c:CW * (c + 1)], delta[:, hf, CW * c:CW * (c + 1)],
                                                xc[:, hf, CW * c:CW * (c + 1)], ALU.mult).then_inc(dxc_done, 1)
            for m in range(CHUNKS * NST * HALVES):
                pool.wait_ge(c_done, m // 2 + 1)
                pool.wait_ge(h_done, m + 1)
                if m >= NB:
                    pool.wait_ge(hc_used, m - NB + 1)
                c, n, hf = m // (2 * NST), (m // 2) % NST, m % 2
                if m == 0:
                    pool.wait_ge(carry_set, 1)
                if c < CHUNKS - 1:
                    nc.gpsimd.tensor_copy(carry[:, hf, n:n + 1], h_ring[m % NB][:, CW - 1:CW])
                nc.gpsimd.tensor_tensor(hc_ring[m % NB], h_ring[m % NB], c_ring[(m // 2) % NC_RING],
                                        ALU.mult).then_inc(hc_done, 1)

        @block.tensor
        def _(pe):
            mm, tr = pe.matmul, pe.transpose

            def transposed_chunk(k, c, src, dst):
                for i in range(TPC):
                    ins = tr(dst[:, P * i:P * (i + 1)], src[:, c % 2, i, :], ident[:, :])
                ins.then_inc(xT_ps[k], 1)

            pe.wait_ge(consts, 2)
            for c in range(CHUNKS):
                pe.wait_ge(xn_done[0], c + 1)
                if c:
                    pe.wait_ge(xT_done[0], c)
                transposed_chunk(0, c, xn, bank[0])
                pe.wait_ge(xT_done[0], c + 1)
                if c == 0:
                    pe.wait_ge(wqkv_in, 64)
                else:
                    pe.wait_ge(parts_done, 2 * c)
                    pe.wait_ge(v_taken, c)
                mm(bank[1], w_qkvo[:, 0, :], xTc[c], start=True, stop=True).then_inc(qkv_ps, 1)
                mm(bank[2], w_qkvo[:, 1, :], xTc[c], start=True, stop=True).then_inc(qkv_ps, 1)
                for i in range(TPC):
                    ins = mm(bank[3][:, P * i:P * (i + 1)], xTc[c][:, P * i:P * (i + 1)], w_qkvo[:, 2, :],
                             start=(i == 0), stop=(i == TPC - 1), skip_group_check=True)
                ins.then_inc(qkv_ps, 1)

            def slot(n):
                if n >= 2:
                    pe.wait_ge(prep_act, n - 1)
                return prep_bank(n)

            pe.wait_ge(weights_in, 16 * N_WEIGHTS)
            b0 = slot(0)
            for m in range(HT):
                ins = tr(b0[0:RANK, P * m:P * (m + 1)], w_u[:, m, :], ident[:, :])
            ins.then_inc(prep_pe, 1)
            b1 = slot(1)
            tr(b1[0:RANK, 0:RANK], fb[:, :], ident[0:RANK, 0:RANK])
            tr(b1[0:DDIM, 32:32 + LR], l_down[:, :], ident[0:LR, 0:LR])
            tr(b1[0:LR, 64:64 + UDIM], l_up[:, :], ident[0:UDIM, 0:UDIM])
            tr(b1[0:UDIM, P:2 * P], u_aux[:, :], ident[:, :]).then_inc(prep_pe, 1)
            b2 = slot(2)
            for i in range(2):
                tr(b2[:, P * i:P * (i + 1)], w_in[:, 2 + i, :], ident[:, :])
            for i in range(2):
                ins = tr(b2[:, 2 * P + P * i:3 * P + P * i], w_out[:, P * i:P * (i + 1)], ident[:, :])
            ins.then_inc(prep_pe, 1)
            b3 = slot(3)
            for i in range(2):
                tr(b3[:, P * i:P * i + 96], w_x[:, P * i:P * (i + 1)], ident[0:96, 0:96])
            for i in range(2):
                ins = tr(b3[0:DTR, 2 * P + P * i:3 * P + P * i], w_dt[:, i, :], ident[:, :])
            ins.then_inc(prep_pe, 1)
            for g in range(2):
                b = slot(4 + g)
                if g == 0:
                    pe.wait_ge(prep_dve, 1)
                for k in range(2):
                    for hf in range(HALVES):
                        o = 2 * P * k + P * hf
                        ins = tr(b[:, o:o + P], w_tap[:, 2 * g + k, hf, :], ident[:, :])
                ins.then_inc(prep_pe, 1)
            b6 = slot(6)
            pe.wait_ge(prep_dve, 2)
            for m in range(HT):
                ins = tr(b6[:, P * m:P * (m + 1)], tern_pj[:, P * m:P * (m + 1)], ident[:, :])
            ins.then_inc(prep_pe, 1)
            b7 = slot(7)
            mm(b7[0:RANK, 0:D], fbT[:, :], w_v[:, :], start=True, stop=True)
            mm(b7[0:LR, P:2 * P], ldT[:, :], d_aux[:, :], start=True, stop=True,
               skip_group_check=True).then_inc(prep_pe, 1)
            b8 = slot(8)
            pe.wait_ge(prep_act, 8)
            mm(b8[0:UDIM, 0:D], luT[:, :], r1[:, :], start=True, stop=True).then_inc(prep_pe, 1)
            b9 = slot(9)
            pe.wait_ge(prep_dve, 3)
            for m in range(HT):
                mm(b9[:, P * m:P * (m + 1)], tern_fc[:, m, :], ident[:, :], start=(m == 0), stop=False,
                   skip_group_check=True)
                ins = mm(b9[:, P * m:P * (m + 1)], q1[:, :], uT[:, P * m:P * (m + 1)], start=False,
                         stop=(m == HT - 1), skip_group_check=True)
            ins.then_inc(prep_pe, 1)
            b10 = slot(10)
            pe.wait_ge(prep_act, 9)
            mm(b10[:, 0:D], w_l[:, :], ident[:, :], start=True, stop=False)
            mm(b10[:, 0:D], r2[:, :], uaT[:, :], start=False, stop=True).then_inc(prep_pe, 1)

            pe.wait_ge(xT_done[0], CHUNKS)
            pe.wait_ge(parts_done, 2 * CHUNKS)
            pe.wait_ge(v_taken, CHUNKS)
            pe.wait_ge(prep_act, PREP_SLOTS)
            pe.wait_ge(consts, 10)
            pe.wait_ge(pads, 2)

            def scores(v, p):
                c, quad = unit[v]
                i, n, g = pieces[v][p]
                h, gp = 4 * quad + n, piece_base[v] + p
                if p == 0 and quad == 0:
                    pe.wait_ge(stacked[c], 16 * 4 * ROUND)
                if gp >= 2:
                    pe.wait_ge(scores_max, gp - 1)
                w = CW if g < c else P * (i + 1)
                mm(qk_ps[gp % 2][:, 0:w], qs[0:PAIR, c % 2, h, P * i:P * (i + 1)],
                   ks[0:PAIR, h // 2, CW * g:CW * g + w], start=True, stop=True).then_inc(scores_ps, 1)

            def scores_T(u, j, pair):
                c, quad = unit[u]
                s = step_base[u] + j
                if s >= 1:
                    pe.wait_ge(exp_done, 2 * (s - 1) + pair + 1)
                q0 = max(0, P * (j - TPC * c))
                for n in (2 * pair, 2 * pair + 1):
                    h = 4 * quad + n
                    on_diag = j >= TPC * c
                    ins = mm(st_ps[:, n, q0:CW], ks[0:AUG, h // 2, P * j:P * (j + 1)],
                             qs[0:AUG, c % 2, h, q0:CW], start=True, stop=not on_diag)
                if on_diag:
                    for n in (2 * pair, 2 * pair + 1):
                        ins = mm(st_ps[:, n, q0:q0 + P], ident_b[:, :], mask_kq[:, :], start=False, stop=True)
                ins.then_inc(sT_ps, 1)

            def weigh(u, j, part):
                c, quad = unit[u]
                s = step_base[u] + j
                q0 = max(0, P * (j - TPC * c))
                cut = q0 + (CW - q0 + 1) // 2
                lo, hi = (q0, cut) if part == 0 else (cut, CW)
                if part == 0:
                    if j == 0 and u:
                        pe.wait_ge(pv_taken, u)
                    pe.wait_ge(exp_done, 2 * (s + 1))
                for n in range(4):
                    ins = mm(pv_ps[32 * n:32 * n + 32, lo:hi], vaug[:, j, 4 * quad + n, :],
                             probs[:, s % 3, n, lo:hi], start=(j == 0 and part == 0),
                             stop=(j == steps[u] - 1 and part == 1), tile_position=(0, 32 * n),
                             skip_group_check=True)
                if part == 1:
                    ins.then_inc(pv_done, 1)

            def misc_free(job):
                k = misc_order.index(job)
                if k:
                    kind, n = misc_order[k - 1]
                    pe.wait_ge({"max": maxT_done, "out": attn_done, "project": sub_done}[kind], n + 1)

            def turn_max(v):
                pe.wait_ge(max_parts, v + 1)
                misc_free(("max", v))
                m16 = misc.bitcast(BF16)
                for i in range(TPC):
                    ins = tr(m16[0:12, P * i:P * (i + 1)], maxparts[:, v % 2, i, :, :].rearrange("p n s -> p (n s)"),
                             ident_b[:, :])
                ins.then_inc(maxT_ps, 1)

            def turn_out(u):
                pe.wait_ge(pv_taken, u + 1)
                misc_free(("out", u))
                for i in range(TPC):
                    ins = tr(misc[:, P * i:P * (i + 1)], oT[:, u % 2, P * i:P * (i + 1)], ident[:, :])
                ins.then_inc(oT_ps, 1)

            def project_out(c):
                pe.wait_ge(attn_done, QUADS * (c + 1))
                misc_free(("project", c))
                for i in range(TPC):
                    ins = tr(misc[:, P * i:P * (i + 1)], attn[:, c % 2, i, :], ident[:, :])
                ins.then_inc(attnT_ps, 1)
                pe.wait_ge(attnT_done, c + 1)
                for i in range(TPC):
                    ins = mm(misc[:, P * i:P * (i + 1)], attnT[:, P * i:P * (i + 1)], w_qkvo[:, 3, :],
                             start=(i == 0), stop=(i == TPC - 1), skip_group_check=True)
                ins.then_inc(wo_ps, 1)

            for u in range(FIRST):
                for p in range(len(pieces[u])):
                    scores(u, p)
                turn_max(u)
            last = None
            for u in range(UNITS):
                pe.wait_ge(max_rows[u % 2], 64 * (u // 2 + 1))
                for j in range(steps[u]):
                    s_ = step_base[u] + j
                    todo = pieces_at[s_]
                    cut = [len(todo) * k // 4 for k in range(5)]
                    for k in range(4):
                        if k % 2 == 0:
                            scores_T(u, j, k // 2)
                        elif last is not None:
                            weigh(*last, k // 2)
                        for v, p in todo[cut[k]:cut[k + 1]]:
                            scores(v, p)
                    last = (u, j)
                    for v in turn_at[s_]:
                        turn_max(v)
                    if j == 2 and u:
                        turn_out(u - 1)
                    if j == 3 and u and u % QUADS == 0:
                        project_out(u // QUADS - 1)
            weigh(*last, 0)
            weigh(*last, 1)
            turn_out(UNITS - 1)
            project_out(CHUNKS - 1)

            def up(c):
                pe.wait_ge(xn_done[1], c + 1)
                if c >= 2:
                    pe.wait_ge(xT_done[2], c - 1)
                transposed_chunk(1, c, xn, bank[0])
                pe.wait_ge(xT_done[1], c + 1)
                for m in range(HT):
                    if HT * c + m >= 2:
                        pe.wait_ge(relu_done, HT * c + m - 1)
                    mm(bank[1 + m % 2], fcT[:, P * m:P * (m + 1)], xTc[c], start=True, stop=True).then_inc(fc_ps, 1)

            def down(c):
                pe.wait_ge(relu2_done, HT * (c + 1))
                if c:
                    pe.wait_ge(x2_done, c)
                for i in range(TPC):
                    for m in range(HT):
                        ins = mm(bank[3][:, P * i:P * (i + 1)], relu2[:, c % 2, m, P * i:P * (i + 1)], pjT[:, m, :],
                                 start=(i == 0 and m == 0), stop=(m == HT - 1), skip_group_check=True)
                ins.then_inc(pj_ps, 1)

            def in_projection(c):
                pe.wait_ge(xT_done[2], c + 1)
                t0 = 4 + CW * c - (CONV - 1)
                for hf in range(HALVES):
                    if c:
                        pe.wait_ge(sp_a_done, 2 * (c - 1) + hf + 1)
                    for k in range(CONV):
                        ins = mm(bank[4 + hf], tapT[:, k, P * hf:P * (hf + 1)], xT[:, t0 + k:t0 + k + CW],
                                 start=(k == 0), stop=(k == CONV - 1))
                    ins.then_inc(pre_ps, 1)
                if c:
                    pe.wait_ge(bnd_b_done, 2 * c)
                    pe.wait_ge(bcs_done, c)
                for hf in range(HALVES):
                    mm(bank[6 + hf], zT[:, P * hf:P * (hf + 1)], xTc[c], start=True, stop=True).then_inc(pre_ps, 1)

            def mamba_transpose(c):
                pe.wait_ge(xn_done[2], c + 1)
                pe.wait_ge(xT_done[1], min(c + 2, CHUNKS))
                transposed_chunk(2, c, attn, bank[0])

            def x_projection(c):
                pe.wait_ge(silu_done, 4 * c + 3)
                for hf in range(HALVES):
                    ins = mm(bank[6][0:DTR, :], wxT[:, hf, 0:DTR], xc[:, hf, CW * c:CW * (c + 1)],
                             start=(hf == 0), stop=(hf == HALVES - 1))
                ins.then_inc(dtl_ps, 1)
                pe.wait_ge(silu_done, 4 * c + 4)
                for hf in range(HALVES):
                    ins = mm(bank[7][0:96, :], wbcT[:, hf, :], xc[:, hf, CW * c:CW * (c + 1)],
                             start=(hf == 0), stop=(hf == HALVES - 1))
                ins.then_inc(bc_ps, 1)
                pe.wait_ge(dtl_done, c + 1)
                for i in range(TPC):
                    for hf in range(HALVES):
                        t1 = CW * c + P * i
                        ins = mm(bank[6][:, NST * i:NST * (i + 1)], xc[:, hf, t1:t1 + P], wxT[:, hf, DTR:DTR + NST],
                                 start=(i == 0 and hf == 0), stop=(hf == HALVES - 1), skip_group_check=True)
                ins.then_inc(bt_ps, 1)
                for hf in range(HALVES):
                    mm(bank[4 + hf], wdtT[:, P * hf:P * (hf + 1)], dtl[:, c % 2, :], start=True,
                       stop=True).then_inc(dt_ps, 1)

            def spread_bmax(c):
                pe.wait_ge(diag_done, c + 1)
                for i in range(TPC):
                    ins = mm(bank[6][:, P * i:P * (i + 1)], ones[:, :], diag[:, i, :], start=(i == 0),
                             stop=(i == TPC - 1), skip_group_check=True)
                ins.then_inc(bm_ps, 1)

            pe.wait_ge(sub_done, CHUNKS)
            for k in range(ROUNDS):
                if in_round(k, 0):
                    up(k)
                if in_round(k, 3):
                    spread_bmax(k - 3)
                if in_round(k, 1):
                    down(k - 1)
                if in_round(k, 2):
                    in_projection(k - 2)
                if in_round(k, 1):
                    mamba_transpose(k - 1)
                if in_round(k, 2):
                    x_projection(k - 2)
            pe.wait_ge(over_done, 1)
            mm(bank[5][0:1, 0:1], over[:, :], ones[:, 0:1], start=True, stop=True).then_inc(over_ps, 1)

            pe.wait_ge(consts, 14)
            pe.wait_ge(bcs_done, CHUNKS)
            pe.wait_ge(bnd_b_done, 2 * CHUNKS)
            pe.wait_ge(flag_done, 1)
            pe.wait_ge(silu_done, 4 * CHUNKS)

            def spread(n_):
                c, n = divmod(n_, NST)
                if n_ >= 2:
                    pe.wait_ge(bu_done, 2 * (n_ - 2) + 2)
                mm(bank[2 + n_ % 2], pick[:, n, :], bcs[:, CW * c:CW * (c + 1)], start=True,
                   stop=True).then_inc(b_ps, 1)
                if n_ >= 2:
                    pe.wait_ge(c_done, n_ - 1)
                mm(bank[4 + n_ % 2], pick[:, NST + n, :], bcs[:, CW * c:CW * (c + 1)], start=True,
                   stop=True).then_inc(c_ps, 1)

            def out_projection(c):
                pe.wait_ge(y_done, 2 * (c + 1))
                for i in range(TPC):
                    t1 = CW * c + P * i
                    for hf in range(HALVES):
                        ins = mm(y_bank(c, 0)[:, P * i:P * (i + 1)], sz[:, hf, t1:t1 + P], woutT[:, hf, :],
                                 start=(i == 0 and hf == 0), stop=(hf == HALVES - 1), skip_group_check=True)
                ins.then_inc(yout_ps, 1)

            def last_transpose(c):
                pe.wait_ge(xn_done[3], c + 1)
                transposed_chunk(3, c, xn, y_bank(c, 1))

            def last_linear(c):
                pe.wait_ge(xT_done[3], c + 1)
                pe.wait_ge(x3_done, c + 1)
                for i in range(TPC):
                    mm(y_bank(c, 0)[:, P * i:P * (i + 1)], xTc[c][:, P * i:P * (i + 1)], wlT[:, :],
                       start=(i == 0), stop=False, skip_group_check=True)
                    ins = mm(y_bank(c, 0)[:, P * i:P * (i + 1)], ones[0:1, :], b_l[0:1, :],
                             start=False, stop=(i == TPC - 1), skip_group_check=True)
                ins.then_inc(fin_ps, 1)

            spread(0)
            spread(1)
            for n_ in range(CHUNKS * NST):
                c, n = divmod(n_, NST)
                if n_ + 2 < CHUNKS * NST:
                    spread(n_ + 2)
                for hf in range(HALVES):
                    m = 2 * n_ + hf
                    if n == 0 and c >= 2:
                        pe.wait_ge(x4_done, c - 1)
                    pe.wait_ge(hc_done, m + 1)
                    mm(y_bank(c, hf), ident[:, :], hc_ring[m % NB], start=(n == 0),
                       stop=(n == NST - 1)).then_inc(hc_used, 1)
                if c and n == YOUT_AT:
                    out_projection(c - 1)
                if c and n == XT3_AT:
                    last_transpose(c - 1)
                if c and n == FIN_AT:
                    last_linear(c - 1)

            out_projection(CHUNKS - 1)
            last_transpose(CHUNKS - 1)
            last_linear(CHUNKS - 1)

        @block.scalar
        def _(act):
            f = nc.scalar.activation

            def ln_rstd(k, c):
                t = TILES * k + TPC * c
                act.wait_ge(moments_of[k], c + 1)
                f(lnvar[:, t:t + TPC], moments[:, t:t + TPC, 1], ACT.Ln, bias=eps_col[:, 0:1]).then_inc(lnvar_of[k], 1)
                act.wait_ge(lnvar_of[k], c + 1)
                f(rstd[:, t:t + TPC], lnvar[:, t:t + TPC], ACT.Exp, scale=-0.5).then_inc(rstd_of[k], 1)

            def take_xT(k, c, src):
                act.wait_ge(xT_ps[k], c + 1)
                f(xTc[c], src, ACT.Copy).then_inc(xT_done[k], 1)

            nc.scalar.preload_act_table_set("natural_log_exp_and_others")
            d = lambda dst, src, **k: act.dma_start(dst, src, **k).then_inc(weights_in, 16)
            d(w_fc[:], a["L0_ffn_w_fc"].rearrange("(m p) e -> p m e", p=P))
            d(w_pj[:], a["L0_ffn_w_proj"])
            d(w_in[:], a["L1_attn_W_in"].rearrange("(m p) e -> p m e", p=P))
            d(conv_w[:], a["L1_attn_conv_w"].rearrange("(h p) o k -> p h (o k)", p=P))
            d(conv_b[:], a["L1_attn_conv_b"].rearrange("(h p) -> p h", p=P), allow_slow_non_contiguous=True)
            d(a_log[:], a["L1_attn_A_log"].rearrange("(h p) n -> p h n", p=P))
            d(w_u[:], a["L0_ffn_u"].rearrange("(m p) r -> p m r", p=P))
            d(fb[:], a["L0_ffn_fast_b"])
            d(w_v[:], a["L0_ffn_v"])
            d(gate[0:RANK, :], a["L0_ffn_gate"].to_broadcast([RANK, 1]))
            d(w_x[:], a["L1_attn_W_x"])
            d(w_dt[:], a["L1_attn_W_dt"].rearrange("(h p) r -> p h r", p=P))
            d(b_dt[:], a["L1_attn_b_dt"].rearrange("(h p) -> p h", p=P), allow_slow_non_contiguous=True)
            d(d_par[:], a["L1_attn_D_param"].rearrange("(h p) -> p h", p=P), allow_slow_non_contiguous=True)
            d(w_out[:], a["L1_attn_W_out"])
            d(w_l[:], a["L1_ffn_W"])
            d(b_l[0:1, :], a["L1_ffn_b"].rearrange("(a o) -> a o", a=1))
            d(l_down[:], a["L1_ffn_lora_down"])
            d(l_up[:], a["L1_ffn_lora_up"])
            d(d_aux[:], a["L1_ffn_down_aux"])
            d(u_aux[:], a["L1_ffn_up_aux"])

            act.wait_ge(eps_set, 1)
            for c in range(CHUNKS):
                ln_rstd(0, c)
                take_xT(0, c, bank[0])
                act.wait_ge(qkv_ps, 3 * c + 3)
                act.wait_ge(consts, 10)
                f(vaug[:, TPC * c:TPC * (c + 1), :, 0:DK],
                  bank[3].rearrange("p (i h d) -> p i h d", i=TPC, h=HEADS), ACT.Copy).then_inc(v_taken, 1)

            def took(ins):
                ins.then_inc(prep_act, 1)

            act.wait_ge(weights_in, 16 * N_WEIGHTS)
            f(neg_a[:, :, :], a_log[:, :, :], ACT.Exp).then_inc(act_step, 1)
            act.wait_ge(prep_pe, 1)
            took(f(uT[:, :], prep_bank(0)[0:RANK, :], ACT.Copy))
            act.wait_ge(prep_pe, 2)
            b1 = prep_bank(1)
            f(fbT[:, :], b1[0:RANK, 0:RANK], ACT.Copy)
            f(ldT[:, :], b1[0:DDIM, 32:32 + LR], ACT.Copy)
            f(luT[:, :], b1[0:LR, 64:64 + UDIM], ACT.Copy)
            took(f(uaT[:, :], b1[0:UDIM, P:2 * P], ACT.Copy))
            act.wait_ge(prep_pe, 3)
            b2 = prep_bank(2)
            f(zT[:, :], b2[:, 0:2 * P], ACT.Copy)
            took(f(woutT[:, :, :].rearrange("p h e -> p (h e)"), b2[:, 2 * P:4 * P], ACT.Copy))
            act.wait_ge(prep_pe, 4)
            b3 = prep_bank(3)
            wx_ps = b3[:, 0:2 * P].rearrange("p (h e) -> p h e", h=2)
            f(wxT[:, :, :], wx_ps[:, :, 0:96], ACT.Copy)
            for g in range(3):
                f(wbcT[:, :, 32 * g:32 * (g + 1)], wx_ps[:, :, DTR:96], ACT.Copy)
            took(f(wdtT[:, :], b3[0:DTR, 2 * P:4 * P], ACT.Copy))
            for g in range(2):
                act.wait_ge(prep_pe, 5 + g)
                took(f(tapT[:, 2 * g:2 * g + 2, :].rearrange("p k d -> p (k d)"), prep_bank(4 + g), ACT.Copy))
            act.wait_ge(prep_pe, 7)
            took(f(pjT[:, :, :].rearrange("p m e -> p (m e)"), prep_bank(6), ACT.Copy))
            act.wait_ge(prep_pe, 8)
            f(q1[:, :], prep_bank(7)[0:RANK, 0:D], ACT.Copy, scale=gate[0:RANK, 0:1])
            took(f(r1[:, :], prep_bank(7)[0:LR, P:2 * P], ACT.Copy))
            act.wait_ge(prep_pe, 9)
            took(f(r2[:, :], prep_bank(8)[0:UDIM, 0:D], ACT.Copy))
            act.wait_ge(prep_pe, 10)
            took(f(fcT[:, :], prep_bank(9), ACT.Copy))
            act.wait_ge(prep_pe, 11)
            took(f(wlT[:, :], prep_bank(10)[:, 0:D], ACT.Copy))

            def take_max(u):
                act.wait_ge(maxT_ps, u + 1)
                if u >= 2:
                    act.wait_ge(max_rows[u % 2], 64 * (u // 2))
                f(maxT[:, u % 2, :], misc.bitcast(BF16)[0:12, 0:CW], ACT.Copy).then_inc(maxT_done, 1)

            def take_out(u):
                act.wait_ge(pv_done, step_base[u + 1])
                if u >= 2:
                    act.wait_ge(oT_ps, u - 1)
                f(oT[:, u % 2, :], pv_ps, ACT.Copy).then_inc(pv_taken, 1)

            def take_projection(c):
                act.wait_ge(attnT_ps, c + 1)
                if c:
                    act.wait_ge(wo_ps, c)
                f(attnT[:, :], misc, ACT.Copy).then_inc(attnT_done, 1)
                act.wait_ge(wo_ps, c + 1)
                f(sub[:, TPC * c:TPC * (c + 1), :].rearrange("p i e -> p (i e)"), misc,
                  ACT.Copy).then_inc(sub_done, 1)

            for u in range(FIRST):
                take_max(u)
            for u, (c, _) in enumerate(unit):
                for j in range(steps[u]):
                    s_ = step_base[u] + j
                    q0 = max(0, P * (j - TPC * c))
                    for pair in range(2):
                        act.wait_ge(sT_ps, 2 * s_ + pair + 1)
                        if s_ >= 3:
                            act.wait_ge(pv_done, s_ - 2)
                        f(probs[:, s_ % 3, 2 * pair:2 * pair + 2, q0:CW], st_ps[:, 2 * pair:2 * pair + 2, q0:CW],
                          ACT.Exp, scale=DK ** -0.5).then_inc(exp_done, 1)
                    if j == 0 and u:
                        take_out(u - 1)
                    for v in turn_at[s_]:
                        take_max(v)
                    if j == 3 and u and u % QUADS == 0:
                        take_projection(u // QUADS - 1)
                    if s_ in EARLY:
                        for c2 in range(CHUNKS - 1):
                            ln_rstd(1 + EARLY.index(s_), c2)
            take_out(UNITS - 1)
            take_projection(CHUNKS - 1)

            for k in range(ROUNDS):
                if in_round(k, 0):
                    take_xT(1, k, bank[0])
                    if k == 0:
                        ln_rstd(1, CHUNKS - 1)
                    for m in range(HT):
                        act.wait_ge(fc_ps, HT * k + m + 1)
                        if k:
                            act.wait_ge(relu2_done, HT * (k - 1) + m + 1)
                        f(relu[:, m, :], bank[1 + m % 2], ACT.Relu).then_inc(relu_done, 1)
                    if k == 0:
                        ln_rstd(2, CHUNKS - 1)
                if in_round(k, 3):
                    c = k - 3
                    for hf in range(HALVES):
                        act.wait_ge(delta_done, 2 * c + hf + 1)
                        if c:
                            act.wait_ge(bnd_done, 2 * (c - 1) + hf + 1)
                        act.wait_ge(prep_dve, 4)
                        f(bnd_a[:, hf, :], delta[:, hf, CW * c:CW * (c + 1)], ACT.Exp,
                          scale=a_max[:, hf:hf + 1]).then_inc(bnd_exp, 1)
                    for hf in range(HALVES):
                        act.wait_ge(bnd_b_done, 2 * c + hf + 1)
                        f(bnd_h[:, hf, :], bnd_b[:, hf, :], ACT.Abs).then_inc(bnd_abs, 1)
                if in_round(k, 1):
                    ln_rstd(3, k - 1)
                    ln_rstd(4, k - 1)
                if in_round(k, 2):
                    c = k - 2
                    t = slice(CW * c, CW * (c + 1))
                    nc.scalar.preload_act_table_set("silu_and_others")
                    for hf in range(HALVES):
                        act.wait_ge(pre_ps, 4 * c + hf + 1)
                        f(xc[:, hf, t], bank[4 + hf], ACT.Silu, bias=conv_b[:, hf:hf + 1]).then_inc(silu_done, 1)
                    for hf in range(HALVES):
                        act.wait_ge(pre_ps, 4 * c + hf + 3)
                        f(sz[:, hf, t], bank[6 + hf], ACT.Silu).then_inc(silu_done, 1)
                    nc.scalar.preload_act_table_set("natural_log_exp_and_others")
                if in_round(k, 1):
                    take_xT(2, k - 1, bank[0])
                if in_round(k, 2):
                    act.wait_ge(dtl_ps, c + 1)
                    if c >= 2:
                        act.wait_ge(dt_ps, 2 * (c - 1))
                    f(dtl[:, c % 2, :], bank[6][0:DTR, :], ACT.Copy).then_inc(dtl_done, 1)
                    for hf in range(HALVES):
                        act.wait_ge(sp_a_done, 2 * c + hf + 1)
                        f(sp_b[:, hf, :], sp_a[:, hf, :], ACT.Exp).then_inc(sp_exp, 1)
                    for hf in range(HALVES):
                        act.wait_ge(sp_exp, 2 * c + hf + 1)
                        f(sp_a[:, hf, :], sp_b[:, hf, :], ACT.Ln, bias=1.0).then_inc(sp_ln, 1)

            for n_ in range(CHUNKS * NST):
                c, n = divmod(n_, NST)
                act.wait_ge(c_ps, n_ + 1)
                if n_ >= NC_RING:
                    act.wait_ge(hc_done, 2 * (n_ - NC_RING) + 2)
                f(c_ring[n_ % NC_RING], bank[4 + n_ % 2], ACT.Copy).then_inc(c_done, 1)
                for hf in range(HALVES):
                    m = 2 * n_ + hf
                    if m >= NA:
                        act.wait_ge(h_done, m - NA + 1)
                    f(a_ring[m % NA], delta[:, hf, CW * c:CW * (c + 1)], ACT.Exp,
                      scale=neg_a[:, hf, n:n + 1]).then_inc(decay_done, 1)

                if c and n == RSTD5_AT:
                    ln_rstd(5, c - 1)
                if c and n == RSTD6_AT:
                    ln_rstd(6, c - 1)
                if c and n == XT3_AT:
                    take_xT(3, c - 1, y_bank(c - 1, 1))
                if c and n == RSTD7_AT:
                    ln_rstd(7, c - 1)
            ln_rstd(5, CHUNKS - 1)
            ln_rstd(6, CHUNKS - 1)
            take_xT(3, CHUNKS - 1, y_bank(CHUNKS - 1, 1))
            ln_rstd(7, CHUNKS - 1)

        @block.vector
        def _(dve):
            v = nc.vector
            step = [0]

            def chained(ins):
                ins.then_inc(dve_step, 1)
                step[0] += 1
                dve.wait_ge(dve_step, step[0])

            def ln_stats(k, c, tile_of):
                t = TILES * k + TPC * c
                for i in range(TPC):
                    ins = v.bn_stats(stats[:, t % (2 * TILES) + i, :], tile_of(i))
                ins.then_inc(stats_of[k], 1)
                dve.wait_ge(stats_of[k], c + 1)
                for i in range(TPC):
                    ins = v.bn_aggr(moments[:, t + i, :], stats[:, t % (2 * TILES) + i, :])
                ins.then_inc(moments_of[k], 1)

            def normalised(k, c, tile_of, out):
                t = TILES * k + TPC * c
                dve.wait_ge(rstd_of[k], c + 1)
                for i in range(TPC):
                    ins = v.tensor_scalar(out[:, c % 2, i, :], tile_of(i), moments[:, t + i, 0:1],
                                          rstd[:, t + i:t + i + 1], ALU.subtract, ALU.mult)
                return ins

            def x_tile(c):
                return lambda i: x[:, TPC * c + i, :]

            def ps_tile(b):
                return lambda i: b[:, P * i:P * (i + 1)]

            def pre_stats(k, c):
                ln_stats(k, c, x_tile(c))

            def pre_norm(k, j, c):
                if c >= 2:
                    dve.wait_ge(xT_ps[j], c - 1)
                normalised(k, c, x_tile(c), attn if j == 2 else xn).then_inc(xn_done[j], 1)

            def post_norm(k, c, tile_of, done):
                chained(normalised(k, c, tile_of, nrm))
                xs = x[:, TPC * c:TPC * (c + 1), :]
                v.tensor_tensor(xs, xs, nrm[:, c % 2, :, :], ALU.add).then_inc(done, 1)
                dve.wait_ge(done, c + 1)

            v.memset(eps_col[:, :], EPS).then_inc(eps_set, 1)
            v.memset(arena_q[:, :], 0.0).then_inc(pads, 1)
            v.memset(ks[PAIR:P, :, :], 1.0).then_inc(pads, 1)

            def split_parts(c):
                if c >= 2:
                    dve.wait_ge(parts_stored[c - 2], 32)
                for m in range(2):
                    dve.wait_ge(qkv_ps, 3 * c + m + 1)
                    ins = v.tensor_copy(parts[:, c % 2, m, 0, :], bank[1 + m])
                chained(ins)
                for m in range(2):
                    ins = v.tensor_tensor(resid[:, m, :], bank[1 + m], parts[:, c % 2, m, 0, :], ALU.subtract)
                chained(ins)
                for m in range(2):
                    ins = v.tensor_copy(parts[:, c % 2, m, 1, :], resid[:, m, :])
                chained(ins)
                for m in range(2):
                    v.tensor_tensor(parts[:, c % 2, m, 2, :], resid[:, m, :], parts[:, c % 2, m, 1, :],
                                    ALU.subtract).then_inc(parts_done, 1)
                dve.wait_ge(parts_done, 2 * c + 2)

            for c in range(CHUNKS):
                dve.wait_ge(x_in[c], 16)
                pre_stats(0, c)
                pre_norm(0, 0, c)
                if c:
                    split_parts(c - 1)
            split_parts(CHUNKS - 1)

            dve.wait_ge(weights_in, 16 * N_WEIGHTS)
            for k in range(CONV):
                for hf in range(HALVES):
                    ins = v.tensor_scalar(w_tap[:, k, hf, :], w_in[:, hf, :], conv_w[:, hf, k:k + 1], None, ALU.mult)
            ins.then_inc(prep_dve, 1)
            v.tensor_reduce(scl[:, 0, 0:HT], w_fc[:, :, :], AX.X, ALU.add, apply_absolute_value=True)
            chained(v.tensor_reduce(scl[:, 0, HT:HT + 1], w_pj[:, :], AX.X, ALU.add, apply_absolute_value=True))
            v.tensor_scalar(scl[:, 1, 0:HT], scl[:, 0, 0:HT], 1.0 / D, EPS, ALU.mult, ALU.max)
            chained(v.tensor_scalar(scl[:, 1, HT:HT + 1], scl[:, 0, HT:HT + 1], 1.0 / HIDDEN, EPS, ALU.mult, ALU.max))
            chained(v.tensor_scalar(scl[:, 2, :], scl[:, 1, :], 0.5, None, ALU.mult))
            chained(v.tensor_scalar(scl[:, 0, :], scl[:, 1, :], -0.5, None, ALU.mult))

            def ternary(out, w, col):
                n = w.shape[1]
                chained(v.tensor_scalar(tmp_w[:, 0, 0:n], w, scl[:, 2, col:col + 1], None, ALU.is_gt))
                chained(v.scalar_tensor_tensor(tmp_w[:, 1, 0:n], w, scl[:, 0, col:col + 1], tmp_w[:, 0, 0:n],
                                               ALU.is_lt, ALU.subtract))
                chained(v.scalar_tensor_tensor(tmp_w[:, 0, 0:n], tmp_w[:, 1, 0:n], -1.0, w, ALU.mult, ALU.subtract))
                chained(v.tensor_tensor(tmp_w[:, 1, 0:n], w, tmp_w[:, 0, 0:n], ALU.add))
                return v.tensor_scalar(out, tmp_w[:, 1, 0:n], scl[:, 1, col:col + 1], None, ALU.mult)

            ternary(tern_pj[:, :], w_pj[:, :], HT).then_inc(prep_dve, 1)
            dve.wait_ge(prep_dve, 2)
            for m in range(HT):
                ins = ternary(tern_fc[:, m, :], w_fc[:, m, :], m)
                if m < HT - 1:
                    chained(ins)
            ins.then_inc(prep_dve, 1)
            dve.wait_ge(act_step, 1)
            chained(v.tensor_scalar(neg_a[:, :, :], neg_a[:, :, :], -1.0, None, ALU.mult))
            v.tensor_reduce(a_max[:, :], neg_a[:, :, :], AX.X, ALU.max).then_inc(prep_dve, 1)

            def piece_max(w_, p):
                c, _ = unit[w_]
                i, n, g = pieces[w_][p]
                gp = piece_base[w_] + p
                dve.wait_ge(scores_ps, gp + 1)
                if gp >= 2:
                    dve.wait_ge(scores_max, gp - 1)
                out = maxcol[:, w_ % 2, i, n, g:g + 1]
                src = qk_ps[gp % 2]
                if g < c:
                    v.reduce_max(out, src, AX.X).then_inc(scores_max, 1)
                else:
                    w = P * (i + 1)
                    v.tensor_tensor_reduce(junk[:, gp % 2, 0:w], src[:, 0:w], mask_qk[:, CW - w:CW], 1.0, LOWEST,
                                           ALU.add, ALU.max, out).then_inc(scores_max, 1)

            def finish_max(w_):
                b = w_ % 2
                dve.wait_ge(scores_max, piece_base[w_ + 1])
                if w_ >= 2:
                    dve.wait_ge(maxT_ps, w_ - 1)
                chained(v.tensor_reduce(rowmax[:, b, :, :], maxcol[:, b, :, :, 0:unit[w_][0] + 1], AX.X, ALU.max))
                chained(v.tensor_scalar(maxparts[:, b, :, :, 0], rowmax[:, b, :, :], -1.0, None, ALU.mult))
                chained(v.scalar_tensor_tensor(maxres[:, b, :, :], rowmax[:, b, :, :], -1.0, maxparts[:, b, :, :, 0],
                                               ALU.mult, ALU.subtract))
                chained(v.tensor_copy(maxparts[:, b, :, :, 1], maxres[:, b, :, :]))
                v.tensor_tensor(maxparts[:, b, :, :, 2], maxres[:, b, :, :], maxparts[:, b, :, :, 1],
                                ALU.subtract).then_inc(max_parts, 1)

            def take_heads(u):
                c, quad = unit[u]
                o = misc.rearrange("p (i n e) -> p i n e", i=TPC, n=4)
                dve.wait_ge(oT_ps, u + 1)
                if c >= 2:
                    dve.wait_ge(attnT_ps, c - 1)
                chained(v.reciprocal(rsum[:, u % 2, :, :], o[:, :, :, DK]))
                v.tensor_tensor(attn[:, c % 2, :, 32 * quad:32 * quad + 32].rearrange("p i (n d) -> p i n d", n=4),
                                o[:, :, :, 0:DK],
                                rsum[:, u % 2, :, :].rearrange("p i (n a) -> p i n a", a=1).to_broadcast([P, TPC, 4, DK]),
                                ALU.mult).then_inc(attn_done, 1)

            def attention_stats(c):
                dve.wait_ge(sub_done, c + 1)
                ln_stats(1, c, lambda i: sub[:, TPC * c + i, :])

            def attention_norm(c):
                post_norm(1, c, lambda i: sub[:, TPC * c + i, :], x1_done)
                pre_stats(2, c)

            dve.wait_ge(consts, 10)
            for u in range(FIRST):
                for p in range(len(pieces[u])):
                    piece_max(u, p)
                finish_max(u)
            for u in range(UNITS):
                for j in range(steps[u]):
                    for w_, p in pieces_at[step_base[u] + j]:
                        piece_max(w_, p)
                        if p == len(pieces[w_]) - 1:
                            finish_max(w_)
                    if j == 2 and u:
                        take_heads(u - 1)
                    if step_base[u] + j == EARLY[0]:
                        for c in range(CHUNKS - 1):
                            attention_stats(c)
                        for c in range(CHUNKS - 1):
                            attention_norm(c)
                    if step_base[u] + j == EARLY[1]:
                        for c in range(2):
                            pre_norm(2, 1, c)
            take_heads(UNITS - 1)

            def split_bc(c):
                t = slice(CW * c, CW * (c + 1))
                dve.wait_ge(bc_ps, c + 1)
                chained(v.tensor_copy(bc_hi[:, :], bank[7][0:96, :]))
                chained(v.tensor_tensor(bc_r[:, :], bank[7][0:96, :], bc_hi[:, :], ALU.subtract))
                chained(v.tensor_copy(bc_mid[:, :], bc_r[:, :]))
                v.tensor_copy(bcs[0:32, t], bc_hi[0:32, :])
                v.tensor_copy(bcs[32:64, t], bc_mid[32:64, :])
                v.tensor_tensor(bcs[64:96, t], bc_r[64:96, :], bc_mid[64:96, :], ALU.subtract).then_inc(bcs_done, 1)

            def largest_b(c):
                dve.wait_ge(bt_ps, c + 1)
                chained(v.tensor_reduce(bmax[:, c, :], bank[6][:, 0:TPC * NST].rearrange("p (i n) -> p i n", i=TPC),
                                        AX.X, ALU.max, apply_absolute_value=True))
                if c:
                    dve.wait_ge(bm_ps, c)
                for i in range(TPC):
                    ins = v.tensor_scalar(diag[:, i, :], ident[:, :], bmax[:, c, i:i + 1], None, ALU.mult)
                ins.then_inc(diag_done, 1)

            def take_dt(c):
                for hf in range(HALVES):
                    dve.wait_ge(dt_ps, 2 * c + hf + 1)
                    v.tensor_scalar(sp_a[:, hf, :], bank[4 + hf], b_dt[:, hf:hf + 1], 20.0, ALU.add,
                                    ALU.min).then_inc(sp_a_done, 1)

            def take_delta(c):
                for hf in range(HALVES):
                    dve.wait_ge(sp_ln, 2 * c + hf + 1)
                    v.tensor_scalar(delta[:, hf, CW * c:CW * (c + 1)], sp_a[:, hf, :], 1e-4, 10.0, ALU.add,
                                    ALU.min).then_inc(delta_done, 1)

            def bound_input(c):
                dve.wait_ge(bm_ps, c + 1)
                for hf in range(HALVES):
                    dve.wait_ge(dxc_done, 2 * c + hf + 1)
                    v.tensor_tensor(bnd_b[:, hf, :], dxc[:, hf, CW * c:CW * (c + 1)], bank[6],
                                    ALU.mult).then_inc(bnd_b_done, 1)

            def bound_scan(c):
                for hf in range(HALVES):
                    dve.wait_ge(bnd_abs, 2 * c + hf + 1)
                    dve.wait_ge(bnd_exp, 2 * c + hf + 1)
                    ins = v.tensor_scalar(bnd_h[:, hf, :], bnd_h[:, hf, :], 10.0, None, ALU.min)
                chained(ins)
                for hf in range(HALVES):
                    ins = v.tensor_tensor_scan(bnd_b[:, hf, :], bnd_a[:, hf, :], bnd_h[:, hf, :],
                                               bnd_c[:, hf:hf + 1] if c else 0.0, ALU.mult, ALU.add)
                chained(ins)
                for hf in range(HALVES):
                    v.tensor_copy(bnd_c[:, hf:hf + 1], bnd_b[:, hf, CW - 1:CW])
                    v.reduce_max(bnd_m[:, c, hf:hf + 1], bnd_b[:, hf, :], AX.X).then_inc(bnd_done, 1)
                dve.wait_ge(bnd_done, 2 * (c + 1))

            for k in range(ROUNDS):
                if k == 0:
                    attention_stats(CHUNKS - 1)
                    attention_norm(CHUNKS - 1)
                    pre_norm(2, 1, 2)
                if k == 1:
                    pre_norm(2, 1, 3)
                if in_round(k, 3):
                    bound_input(k - 3)
                if in_round(k, 1):
                    dve.wait_ge(pj_ps, k)
                    ln_stats(3, k - 1, ps_tile(bank[3]))
                    post_norm(3, k - 1, ps_tile(bank[3]), x2_done)
                    pre_stats(4, k - 1)
                    pre_norm(4, 2, k - 1)
                if in_round(k, 3):
                    bound_scan(k - 3)
                if in_round(k, 2):
                    split_bc(k - 2)
                    take_dt(k - 2)
                    largest_b(k - 2)
                    take_delta(k - 2)
            chained(v.tensor_reduce(bmax[:, 0, 0:1], bnd_m[:, :, :], AX.XY, ALU.max))
            v.tensor_scalar(over[:, :], bmax[:, 0, 0:1], H_BOUND, None, ALU.is_le).then_inc(over_done, 1)
            dve.wait_ge(over_ps, 1)
            v.tensor_copy(over_i[:, :], bank[5][0:1, 0:1]).then_inc(flag_done, 1)
            dve.wait_ge(flag_done, 1)
            sure = dve.value_load(over_i[0:1, 0:1])

            def scan_input(m):
                n_, hf = divmod(m, 2)
                c = n_ // NST
                b = bu_ring[m % NB]
                dve.wait_ge(b_ps, n_ + 1)
                if m >= NB:
                    dve.wait_ge(h_done, m - NB + 1)
                v.tensor_tensor(b, dxc[:, hf, CW * c:CW * (c + 1)], bank[2 + n_ % 2], ALU.mult).then_inc(bu_done, 1)

            def clip_input(m):
                b = bu_ring[m % NB]
                dve.wait_ge(bu_done, m + 1)
                v.tensor_scalar(b, b, 10.0, -10.0, ALU.min, ALU.max).then_inc(clip_done, 1)

            def ready_for_scan(m):
                dve.wait_ge(clip_done, m + 1)
                dve.wait_ge(decay_done, m + 1)
                if m >= NB:
                    dve.wait_ge(hc_done, m - NB + 1)

            def start_of(m):
                n_, hf = divmod(m, 2)
                return carry[:, hf, n_ % NST:n_ % NST + 1]

            def finish_y(c):
                t = slice(CW * c, CW * (c + 1))
                for hf in range(HALVES):
                    dve.wait_ge(hc_used, 2 * NST * (c + 1) - 1 + hf)
                    ins = v.scalar_tensor_tensor(y_a[:, hf, :], xc[:, hf, t], d_par[:, hf:hf + 1], y_bank(c, hf),
                                                 ALU.mult, ALU.add)
                    ins.then_inc(y_sum, 1)
                for hf in range(HALVES):
                    dve.wait_ge(y_sum, 2 * c + hf + 1)
                    v.tensor_scalar(y_b[:, hf, :], y_a[:, hf, :], 50.0, -50.0, ALU.min, ALU.max).then_inc(y_clip, 1)
                for hf in range(HALVES):
                    dve.wait_ge(y_clip, 2 * c + hf + 1)
                    v.tensor_tensor(sz[:, hf, t], y_b[:, hf, :], sz[:, hf, t], ALU.mult).then_inc(y_done, 1)

            def finish_chunk(c, r):
                if r == Y_LAG:
                    finish_y(c)
                if r == STATS5:
                    dve.wait_ge(yout_ps, c + 1)
                    ln_stats(5, c, ps_tile(y_bank(c, 0)))
                if r == NORM5:
                    post_norm(5, c, ps_tile(y_bank(c, 0)), x3_done)
                    pre_stats(6, c)
                if r == NORM6:
                    pre_norm(6, 3, c)
                if r == STATS7:
                    dve.wait_ge(fin_ps, c + 1)
                    ln_stats(7, c, ps_tile(y_bank(c, 0)))
                if r == NORM7:
                    post_norm(7, c, ps_tile(y_bank(c, 0)), x4_done)

            M = CHUNKS * NST * HALVES
            v.memset(carry[:, :, :], 0.0).then_inc(carry_set, 1)
            dve.wait_ge(carry_set, 1)

            def steps_of_scan(scan):
                scan_input(0)
                for m in range(M):
                    if m + 1 < M:
                        scan_input(m + 1)
                    clip_input(m)
                    ready_for_scan(m)
                    scan(m)
                    c, r = divmod(m, NST * HALVES)
                    if c:
                        finish_chunk(c - 1, r)
                for r in (Y_LAG, STATS5, NORM5, NORM6, STATS7, NORM7):
                    finish_chunk(CHUNKS - 1, r)

            def plain_scan(m):
                v.tensor_tensor_scan(h_ring[m % NB], a_ring[m % NA], bu_ring[m % NB], start_of(m), ALU.mult,
                                     ALU.add).then_inc(h_done, 1)

            def clipped_scan(m):
                h, dec, bu = h_ring[m % NB], a_ring[m % NA], bu_ring[m % NB]
                v.tensor_copy(h_last[:, :], start_of(m))
                dve.drain()
                with dve.Fori(0, CW) as i:
                    v.scalar_tensor_tensor(h_next[:, :], dec[:, bass.ds(i, 1)], h_last[:, 0:1], bu[:, bass.ds(i, 1)],
                                           ALU.mult, ALU.add)
                    dve.drain()
                    v.tensor_scalar(h_last[:, :], h_next[:, :], 20.0, -20.0, ALU.min, ALU.max)
                    dve.drain()
                    v.tensor_copy(h[:, bass.ds(i, 1)], h_last[:, :])
                dve.drain()
                v.tensor_copy(h_next[:, :], h_last[:, :]).then_inc(h_done, 1)

            with dve.If(sure == P):
                steps_of_scan(plain_scan)
            with dve.Else():
                steps_of_scan(clipped_scan)


_INS = ['L0_attn_x', 'L0_attn_WQ', 'L0_attn_WK', 'L0_attn_WV', 'L0_attn_WO', 'L0_ffn_fast_b', 'L0_ffn_w_fc',
        'L0_ffn_w_proj', 'L0_ffn_u', 'L0_ffn_v', 'L0_ffn_gate', 'L1_attn_W_in', 'L1_attn_conv_w', 'L1_attn_conv_b',
        'L1_attn_W_x', 'L1_attn_W_dt', 'L1_attn_b_dt', 'L1_attn_A_log', 'L1_attn_D_param', 'L1_attn_W_out',
        'L1_ffn_W', 'L1_ffn_b', 'L1_ffn_lora_down', 'L1_ffn_lora_up', 'L1_ffn_down_aux', 'L1_ffn_up_aux']


def kernel(**inputs):
    import numpy as np
    import concourse.bacc as bacc
    from concourse.bass_utils import run_bass_kernel_spmd as run

    nc = bacc.Bacc("TRN2", target_bir_lowering=False, num_devices=1)
    arrays, aps = {}, {}
    for name in _INS:
        arr = np.ascontiguousarray(inputs[name]).reshape(np.shape(inputs[name]) or (1, 1))
        arrays[f"in_{name}"] = arr
        aps[name] = nc.dram_tensor(f"in_{name}", arr.shape, mybir.dt.from_np(arr.dtype), kind="ExternalInput").ap()
    aps["out"] = nc.dram_tensor("out_x", (1, S, D), F32, kind="ExternalOutput").ap()
    build(nc, aps)
    return run(nc, [arrays], core_ids=[0]).results[0]["out_x"]
```

```python
from contextlib import ExitStack

import numpy as np

import concourse.bass as bass
from concourse import mybir

ALU = mybir.AluOpType
ACT = mybir.ActivationFunctionType
AX = mybir.AxisListType
F32 = mybir.dt.float32
BF16 = mybir.dt.bfloat16
I32 = mybir.dt.int32

P = 128
S = 2048
D = 128
HEADS, DK = 16, 8
TILES = S // P
CW = 512
CHUNKS = S // CW
TPC = CW // P
QUADS = HEADS // 4
UNITS = CHUNKS * QUADS
HIDDEN, RANK = 512, 16
HT = HIDDEN // P
DI, NST, DTR, CONV = 256, 16, 64, 4
HALVES = DI // P
LR, DDIM, UDIM = 4, 100, 50
EPS = 1e-5
MASKED = -1.0e30
LOWEST = -3.0e38
ROUND = 6
SPLIT_Q = (0, 0, 1, 1, 0, 2)
SPLIT_K = (0, 1, 0, 1, 2, 0)
ROWS = ROUND * DK
PAIR = 2 * ROWS
AUG = PAIR + 3
NORMS = 8
H_BOUND = 19.99


def build(nc, a):
    ctx = ExitStack()
    with ctx:
        def sb(name, shape, dt=F32):
            return ctx.enter_context(nc.sbuf_tensor(name, shape, dt))

        def sem(name):
            return ctx.enter_context(nc.semaphore(name))

        bank = [ctx.enter_context(nc.psum_tensor(f"bank{i}", [P, CW], F32))[:, :] for i in range(8)]
        st_bank = bank[0:3]
        qk_ps = bank[3:6]
        pv_ps = bank[6]
        misc = bank[7]

        x = sb("x", [P, TILES, D])
        xn = sb("xn", [P, 2, TPC, D])
        xT = sb("xT", [P, 4 + S])
        xTc = [xT[:, 4 + CW * c:4 + CW * (c + 1)] for c in range(CHUNKS)]
        stats = sb("stats", [P, 2 * TILES, 6])
        moments = sb("moments", [P, NORMS * TILES, 2])
        lnvar = sb("lnvar", [P, NORMS * TILES])
        rstd = sb("rstd", [P, NORMS * TILES])
        nrm = sb("nrm", [P, 2, TPC, D])
        arena_q = sb("arena_q", [P, 8192])
        arena_k = sb("arena_k", [P, 8192])
        arena_v = sb("arena_v", [P, 8192])
        qs = arena_q[:, :].bitcast(BF16).rearrange("p (b h t) -> p b h t", b=2, h=HEADS)
        ks = arena_k[:, :].bitcast(BF16).rearrange("p (h t) -> p h t", h=8)
        vaug = arena_v[:, :].rearrange("p (j h e) -> p j h e", j=TILES, h=HEADS)
        parts = sb("parts", [P, 2, 2, 3, CW], BF16)
        probs = sb("probs", [P, 3, 4, CW])
        junk = sb("junk", [P, 2, CW], BF16)
        maxcol = sb("maxcol", [P, 2, TPC, 4, CHUNKS])
        rowmax = sb("rowmax", [P, 2, TPC, 4])
        maxres = sb("maxres", [P, 2, TPC, 4])
        maxparts = sb("maxparts", [P, 2, TPC, 4, 3], BF16)
        maxT = sb("maxT", [12, 2, CW], BF16)
        oT = sb("oT", [P, 2, CW])
        resid = oT
        rsum = sb("rsum", [P, 2, TPC, 4])
        attn = sb("attn", [P, 2, TPC, D])
        attnT = sb("attnT", [P, CW])
        sub = xT[:, 4:].rearrange("p (i e) -> p i e", e=D)
        xc = arena_q[:, 0:4096].rearrange("p (h t) -> p h t", h=2)
        sz = arena_q[:, 4096:8192].rearrange("p (h t) -> p h t", h=2)
        delta = arena_k[:, 0:4096].rearrange("p (h t) -> p h t", h=2)
        dxc = arena_k[:, 4096:8192].rearrange("p (h t) -> p h t", h=2)
        ring = arena_v[:, :].rearrange("p (r t) -> p r t", t=CW)
        NA, NB, NH, NC_RING = 4, 3, 3, 2
        a_ring = [ring[:, i, :] for i in range(0, 4)]
        bu_ring = [ring[:, i:i + 2, :] for i in (4, 6, 8)]
        h_ring = [ring[:, i, :] for i in range(10, 13)]
        hc_ring = [ring[:, i, :] for i in range(13, 16)]
        c_ring = [probs[:, 1, i, :] for i in range(2)]
        flat = parts[:, :, :, :, :].rearrange("p a m s t -> p (a m s t)")
        bcs = flat[0:96, 0:S]
        bc_hi = flat[0:96, S:S + CW]
        bc_mid = flat[0:96, S + CW:S + 2 * CW]
        bc_r = flat[0:96, S + 2 * CW:S + 4 * CW].bitcast(F32)
        dtl = flat[0:DTR, S + 4 * CW:S + 8 * CW].bitcast(F32).rearrange("p (a t) -> p a t", a=2)
        sp_a, sp_b = ring[:, 0:2, :], ring[:, 2:4, :]
        carry = sb("carry", [P, HALVES, NST])
        relu = probs[:, 0, :, :]
        relu2 = probs[:, 1:3, :, :]
        ident = sb("ident", [P, P])
        ident_b = sb("ident_b", [P, P], BF16)
        ones = sb("ones", [P, P])
        mask_kq = sb("mask_kq", [P, P], BF16)
        mask_qk = sb("mask_qk", [P, CW])
        pick = sb("pick", [96, 2 * NST, P], BF16)
        w_qkvo = sb("w_qkvo", [P, 4, D])
        w_fc = probs[:, 0, 0, :].rearrange("p (m e) -> p m e", m=HT)
        w_pj = probs[:, 0, 1, :]
        fb = sb("fb", [RANK, RANK])
        w_u = sb("w_u", [P, HT, RANK])
        w_v = sb("w_v", [RANK, D])
        gate = sb("gate", [P, 1])
        w_in = probs[:, 0, 2, :].rearrange("p (m e) -> p m e", m=4)
        conv_w = sb("conv_w", [P, HALVES, CONV])
        conv_b = sb("conv_b", [P, HALVES])
        w_x = probs[0:96, 0, 3, 0:DI]
        w_dt = sb("w_dt", [P, HALVES, DTR])
        b_dt = sb("b_dt", [P, HALVES])
        a_log = sb("a_log", [P, HALVES, NST])
        d_par = sb("d_par", [P, HALVES])
        w_out = probs[:, 0, 3, DI:]
        w_l = probs[:, 1, 0, 0:D]
        b_l = sb("b_l", [P, D])
        l_down = sb("l_down", [LR, DDIM])
        l_up = sb("l_up", [UDIM, LR])
        d_aux = probs[0:DDIM, 1, 0, D:2 * D]
        u_aux = probs[:, 1, 0, 2 * D:2 * D + UDIM]
        tern_fc = attn[:, 0, :, :]
        tern_pj = attn[:, 1, :, :].rearrange("p i e -> p (i e)")
        tmp_w = nrm[:, :, :, :].rearrange("p a i e -> p a (i e)")
        scl = sb("scl", [P, 3, HT + 1])
        fcT = sb("fcT", [P, HIDDEN])
        pjT = sb("pjT", [P, HT, D])
        uT = probs[0:RANK, 1, 1, :]
        fbT = probs[0:RANK, 1, 2, 0:RANK]
        q1 = probs[0:RANK, 1, 2, D:2 * D]
        w_tap = probs[:, 2, 0:2, :].rearrange("p a t -> p (a t)").rearrange("p (k h e) -> p k h e", k=CONV, h=HALVES)
        tapT = sb("tapT", [P, CONV, DI])
        zT = sb("zT", [P, DI])
        wxT = sb("wxT", [P, HALVES, 96])
        wbcT = sb("wbcT", [P, HALVES, 96])
        wdtT = sb("wdtT", [DTR, DI])
        woutT = sb("woutT", [P, HALVES, D])
        neg_a = sb("neg_a", [P, HALVES, NST])
        a_max = sb("a_max", [P, HALVES])
        ldT = probs[0:DDIM, 1, 2, 16:16 + LR]
        luT = probs[0:LR, 1, 2, 32:32 + UDIM]
        uaT = probs[0:UDIM, 1, 2, 2 * D:3 * D]
        r1 = probs[0:LR, 1, 2, 3 * D:4 * D]
        r2 = probs[0:UDIM, 1, 3, 0:D]
        wlT = sb("wlT", [P, D])
        bmax = sb("bmax", [P, CHUNKS, TPC])
        diag = ring[:, 4, :].rearrange("p (i t) -> p i t", i=TPC)
        bnd_a, bnd_b, bnd_h = ring[:, 5:7, :], ring[:, 7:9, :], ring[:, 9:11, :]
        y_a, y_b = probs[:, 0, 0:2, :], probs[:, 0, 2:4, :]
        bnd_c = sb("bnd_c", [P, HALVES])
        bnd_m = sb("bnd_m", [P, CHUNKS, HALVES])
        over = sb("over", [P, 1])
        over_i = sb("over_i", [1, 1], I32)
        eps_col = sb("eps_col", [P, 1])
        h_last, h_next = sb("h_last", [P, 1]), sb("h_next", [P, 1])

        two_ones = float(np.array([0x3F803F80], np.uint32).view(np.float32)[0])

        def q_bank(c, m):
            return bank[(1 if c % 2 == 0 else 4) + m]

        def prep_bank(n):
            return bank[6 + n % 2]

        def y_bank(c, hf):
            return bank[hf if c % 2 == 0 else 6 + hf]

        scratch = nc.dram_tensor("split_parts", (2, 3, P, S), BF16, kind="Internal").ap()

        x_in = [sem(f"x_in{c}") for c in range(CHUNKS)]
        wqkv_in, weights_in = sem("wqkv_in"), sem("weights_in")
        N_WEIGHTS = 21
        PREP_SLOTS = 11
        consts = sem("consts")
        stats_of = [sem(f"stats{k}") for k in range(8)]
        moments_of = [sem(f"moments{k}") for k in range(8)]
        lnvar_of = [sem(f"lnvar{k}") for k in range(8)]
        rstd_of = [sem(f"rstd{k}") for k in range(8)]
        dve_step = sem("dve_step")
        act_step = sem("act_step")
        xn_done = [sem(f"xn_done{k}") for k in range(4)]
        xT_ps = [sem(f"xT_ps{k}") for k in range(4)]
        xT_done = [sem(f"xT_done{k}") for k in range(4)]
        prep_dve, prep_pe, prep_act = sem("prep_dve"), sem("prep_pe"), sem("prep_act")
        qkv_ps, v_taken, parts_done = sem("qkv_ps"), sem("v_taken"), sem("parts_done")
        hi_done, resid_done, mid_done = sem("hi_done"), sem("resid_done"), sem("mid_done")
        parts_stored = [sem(f"parts_stored{c}") for c in range(CHUNKS)]
        stacked = [sem(f"stacked{c}") for c in range(CHUNKS)]
        pads = sem("pads")
        scores_ps, scores_max = sem("scores_ps"), sem("scores_max")
        max_parts, maxT_ps, maxT_done = sem("max_parts"), sem("maxT_ps"), sem("maxT_done")
        max_rows = [sem(f"max_rows{i}") for i in range(2)]
        sT_ps, exp_done, pv_done, pv_taken = sem("sT_ps"), sem("exp_done"), sem("pv_done"), sem("pv_taken")
        oT_ps, attn_done, attnT_ps, attnT_done = sem("oT_ps"), sem("attn_done"), sem("attnT_ps"), sem("attnT_done")
        wo_ps, sub_done = sem("wo_ps"), sem("sub_done")
        x1_done, x2_done, x3_done, x4_done = (sem(f"x{i}_done") for i in range(1, 5))
        fc_ps, relu_done, relu2_done, pj_ps = sem("fc_ps"), sem("relu_done"), sem("relu2_done"), sem("pj_ps")
        pre_ps, silu_done = sem("pre_ps"), sem("silu_done")
        dtl_ps, dtl_done, bc_ps, bcs_done = sem("dtl_ps"), sem("dtl_done"), sem("bc_ps"), sem("bcs_done")
        dt_ps, sp_a_done, sp_exp, sp_ln, delta_done, dxc_done = (sem(n) for n in ("dt_ps", "sp_a_done", "sp_exp", "sp_ln", "delta_done", "dxc_done"))
        bt_ps, diag_done, bm_ps, bnd_b_done, bnd_abs, bnd_exp, bnd_done = (sem(n) for n in ("bt_ps", "diag_done", "bm_ps", "bnd_b_done", "bnd_abs", "bnd_exp", "bnd_done"))
        over_done, over_ps, flag_done = sem("over_done"), sem("over_ps"), sem("flag_done")
        b_ps, c_ps, c_done, decay_done, bu_done, h_done, hc_done, hc_used = (
            sem(n) for n in ("b_ps", "c_ps", "c_done", "decay_done", "bu_done", "h_done", "hc_done", "hc_used"))
        y_done, yout_ps, fin_ps, stored = (sem(n) for n in ("y_done", "yout_ps", "fin_ps", "stored"))
        clip_done, carry_set, y_sum, y_clip = (sem(n) for n in ("clip_done", "carry_set", "y_sum", "y_clip"))
        eps_set = sem("eps_set")

        unit = [(u // QUADS, u % QUADS) for u in range(UNITS)]
        pieces = [[(i, n, g) for g in range(c + 1) for i in range(TPC) for n in range(4)] for c, _ in unit]
        steps = [TPC * (c + 1) for c, _ in unit]
        piece_base = [sum(len(p) for p in pieces[:u]) for u in range(UNITS + 1)]
        step_base = [sum(steps[:u]) for u in range(UNITS + 1)]
        FIRST = 2
        LEAD = 4
        STEPS = step_base[UNITS]
        PIECE_COST, STEP_COST = 200, 1000

        def queries(c, j):
            return CW - max(0, P * (j - TPC * c))

        def piece_keys(v, p):
            i, _, g = pieces[v][p]
            return CW if g < unit[v][0] else P * (i + 1)

        def deal_pieces():
            order = [(v, p) for v in range(FIRST, UNITS) for p in range(len(pieces[v]))]
            work = [0]
            for v, p in order:
                work.append(work[-1] + piece_keys(v, p) + PIECE_COST)
            room = [0]
            for c, n in zip([c for c, _ in unit], steps):
                for j in range(n):
                    room.append(room[-1] + queries(c, j) + STEP_COST)
            due = {max(step_base[v] - LEAD, 1): piece_base[v + 1] - piece_base[FIRST] for v in range(FIRST, UNITS)}
            at, done = [], 0
            for s in range(STEPS):
                rate = max([(work[n] - work[done]) / (room[t] - room[s]) for t, n in due.items() if t > s] + [0])
                upto = done
                while upto < len(order) and (work[upto + 1] + work[upto]) / 2 - work[done] < rate * (room[s + 1] - room[s]):
                    upto += 1
                upto = max([upto] + [n for t, n in due.items() if t == s + 1])
                at.append(order[done:upto])
                done = upto
            return at

        pieces_at = deal_pieces()
        turn_at = [[FIRST - 1]] + [[v for v in range(FIRST, UNITS) if (v, len(pieces[v]) - 1) in pieces_at[s - 1]]
                                   for s in range(1, STEPS)]
        misc_order = [("max", v) for v in range(FIRST - 1)]
        for u in range(UNITS):
            for j in range(steps[u]):
                misc_order += [("max", v) for v in turn_at[step_base[u] + j]]
                misc_order += [("out", u - 1)] * (j == 2 and u > 0)
                misc_order += [("project", u // QUADS - 1)] * (j == 3 and u > 0 and u % QUADS == 0)
        misc_order += [("out", UNITS - 1), ("project", CHUNKS - 1)]

        ROUNDS = CHUNKS + 3
        AHEAD = 3
        LAST_PIECE = max(s for s in range(STEPS) if pieces_at[s])
        EARLY = [LAST_PIECE + 5, LAST_PIECE + 9]

        def in_round(k, lag):
            return 0 <= k - lag < CHUNKS

        Y_LAG, STATS5, NORM5, NORM6, STATS7, NORM7 = 5, 12, 15, 18, 29, 31
        YOUT_AT, RSTD5_AT, RSTD6_AT, XT3_AT, TAKE3_AT, FIN_AT, RSTD7_AT = 4, 7, 8, 9, 12, 12, 15

        block = ctx.enter_context(nc.Block())

        @block.sync
        def _(sp):
            xr = a["L0_attn_x"][0].rearrange("(i p) e -> p i e", p=P)
            for c in range(CHUNKS):
                sp.dma_start(x[:, TPC * c:TPC * (c + 1), :], xr[:, TPC * c:TPC * (c + 1), :]).then_inc(x_in[c], 16)
                if c == 0:
                    for n, w in enumerate(("WQ", "WK", "WV", "WO")):
                        sp.dma_start(w_qkvo[:, n, :], a[f"L0_attn_{w}"]).then_inc(wqkv_in, 16)
            d = lambda dst, src, **k: sp.dma_start(dst, src, **k).then_inc(weights_in, 16)
            d(w_fc[:], a["L0_ffn_w_fc"].rearrange("(m p) e -> p m e", p=P))
            d(w_pj[:], a["L0_ffn_w_proj"])
            d(w_in[:], a["L1_attn_W_in"].rearrange("(m p) e -> p m e", p=P))
            d(conv_w[:], a["L1_attn_conv_w"].rearrange("(h p) o k -> p h (o k)", p=P))
            d(conv_b[:], a["L1_attn_conv_b"].rearrange("(h p) -> p h", p=P), allow_slow_non_contiguous=True)
            d(a_log[:], a["L1_attn_A_log"].rearrange("(h p) n -> p h n", p=P))
            d(w_u[:], a["L0_ffn_u"].rearrange("(m p) r -> p m r", p=P))
            d(fb[:], a["L0_ffn_fast_b"])
            d(w_v[:], a["L0_ffn_v"])
            d(gate[0:RANK, :], a["L0_ffn_gate"].to_broadcast([RANK, 1]))
            d(w_x[:], a["L1_attn_W_x"])
            d(w_dt[:], a["L1_attn_W_dt"].rearrange("(h p) r -> p h r", p=P))
            d(b_dt[:], a["L1_attn_b_dt"].rearrange("(h p) -> p h", p=P), allow_slow_non_contiguous=True)
            d(d_par[:], a["L1_attn_D_param"].rearrange("(h p) -> p h", p=P), allow_slow_non_contiguous=True)
            d(w_out[:], a["L1_attn_W_out"])
            d(w_l[:], a["L1_ffn_W"])
            d(b_l[0:1, :], a["L1_ffn_b"].rearrange("(a o) -> a o", a=1))
            d(l_down[:], a["L1_ffn_lora_down"])
            d(l_up[:], a["L1_ffn_lora_up"])
            d(d_aux[:], a["L1_ffn_down_aux"])
            d(u_aux[:], a["L1_ffn_up_aux"])


            def stack_q(c):
                for par in range(2):
                    for t in range(ROUND):
                        src = scratch[0, SPLIT_Q[t]].rearrange("(hp par d) t -> par d hp t", par=2, d=DK)[par]
                        row = ROWS * par + DK * t
                        sp.dma_start(qs[row:row + DK, c % 2, par::2, :], src[:, :, CW * c:CW * (c + 1)]).then_inc(stacked[c], 16)

            def stack_k(c):
                for par in range(2):
                    for t in range(ROUND):
                        src = scratch[1, SPLIT_K[t]].rearrange("(hp par d) t -> par d hp t", par=2, d=DK)[par]
                        row = ROWS * par + DK * t
                        sp.dma_start(ks[row:row + DK, :, CW * c:CW * (c + 1)],
                                     src[:, :, CW * c:CW * (c + 1)]).then_inc(stacked[c], 16)

            def store_parts(c):
                for m in range(2):
                    sp.wait_ge(parts_done, 2 * c + m + 1)
                    sp.dma_start(scratch[m, :, :, CW * c:CW * (c + 1)].rearrange("s p t -> p s t"),
                                 parts[:, c % 2, m, :, :]).then_inc(parts_stored[c], 16)

            store_parts(0)
            sp.wait_ge(parts_stored[0], 32)
            sp.wait_ge(pads, 2)
            stack_q(0)
            store_parts(1)
            stack_k(0)
            sp.wait_ge(parts_stored[1], 32)
            stack_q(1)
            stack_k(1)
            for u, (c, quad) in enumerate(unit):
                if u in (4, 6):
                    store_parts(u // 2)
                    sp.wait_ge(parts_stored[u // 2], 32)
                    stack_k(u // 2)
                for c2 in range(2, CHUNKS):
                    if u in next(t for t in turn_at[step_base[QUADS * (c2 - 1)]:] if t)[:1]:
                        sp.wait_ge(sT_ps, 4 * step_base[QUADS * (c2 - 1)])
                        stack_q(c2)
                sp.wait_ge(maxT_done, u + 1)
                for n in range(4):
                    sp.dma_start(qs[PAIR:AUG, c % 2, 4 * quad + n, :],
                                 maxT[3 * n:3 * n + 3, u % 2, :]).then_inc(max_rows[u % 2], 16)
            outr = a["out"][0].rearrange("(i p) e -> p i e", p=P)
            for c in range(CHUNKS):
                sp.wait_ge(x4_done, c + 1)
                sp.dma_start(outr[:, TPC * c:TPC * (c + 1), :], x[:, TPC * c:TPC * (c + 1), :]).then_inc(stored, 16)
            sp.wait_ge(stored, 16 * CHUNKS)

        @block.gpsimd
        def _(pool):
            def chained(ins, n):
                ins.then_inc(consts, 1)
                pool.wait_ge(consts, n)

            chained(nc.gpsimd.memset(ident[:], 1.0), 1)
            chained(nc.gpsimd.affine_select(out=ident[:], in_=ident[:], compare_op=ALU.is_equal, fill=0.0, base=0,
                                            pattern=[[-1, P]], channel_multiplier=1), 2)
            nc.gpsimd.memset(ones[:], 1.0).then_inc(consts, 1)
            nc.gpsimd.memset(xT[:, 0:4], 0.0).then_inc(consts, 1)
            nc.gpsimd.tensor_copy(ident_b[:], ident[:]).then_inc(consts, 1)
            nc.gpsimd.memset(mask_kq[:], 0.0).then_inc(consts, 1)
            chained(nc.gpsimd.memset(mask_qk[:], 0.0), 7)
            nc.gpsimd.affine_select(out=mask_kq[:], in_=mask_kq[:], compare_op=ALU.is_ge, fill=MASKED, base=0,
                                    pattern=[[1, P]], channel_multiplier=-1).then_inc(consts, 1)
            nc.gpsimd.affine_select(out=mask_qk[:, CW - P:], in_=mask_qk[:, CW - P:], compare_op=ALU.is_ge,
                                    fill=MASKED, base=0, pattern=[[-1, P]], channel_multiplier=1).then_inc(consts, 1)
            nc.gpsimd.memset(vaug[:, :, :, DK:], 1.0).then_inc(consts, 1)
            nc.gpsimd.memset(arena_q[:, :], 0.0).then_inc(pads, 1)
            pool.wait_ge(pads, 1)
            nc.gpsimd.memset(arena_k[PAIR:P, :], two_ones).then_inc(pads, 1)
            pool.wait_ge(pads, 2)
            chained(nc.gpsimd.memset(pick[:], 0.0), 11)
            for g in range(3):
                chained(nc.gpsimd.affine_select(out=pick[:], in_=pick[:], compare_op=ALU.not_equal, fill=1.0,
                                                base=-32 * g, pattern=[[-1, 2 * NST], [0, P]],
                                                channel_multiplier=1), 12 + g)
            for k in range(ROUNDS):
                if in_round(k, 0):
                    for m in range(HT):
                        pool.wait_ge(relu_done, HT * k + m + 1)
                        if k >= 2:
                            pool.wait_ge(pj_ps, k - 1)
                        nc.gpsimd.tensor_tensor(relu2[:, k % 2, m, :], relu[:, m, :], relu[:, m, :],
                                                ALU.mult).then_inc(relu2_done, 1)
            for m in range(CHUNKS * NST * HALVES):
                pool.wait_ge(c_done, m // 2 + 1)
                pool.wait_ge(h_done, m + 1)
                if m >= NH:
                    pool.wait_ge(hc_used, m - NH + 1)
                c, n, hf = m // (2 * NST), (m // 2) % NST, m % 2
                if m == 0:
                    pool.wait_ge(carry_set, 1)
                if c < CHUNKS - 1:
                    nc.gpsimd.tensor_copy(carry[:, hf, n:n + 1], h_ring[m % NH][:, CW - 1:CW])
                nc.gpsimd.tensor_tensor(hc_ring[m % NH], h_ring[m % NH], c_ring[(m // 2) % NC_RING],
                                        ALU.mult).then_inc(hc_done, 1)

        @block.tensor
        def _(pe):
            mm, tr = pe.matmul, pe.transpose

            def transposed_chunk(k, c, src, dst):
                for i in range(TPC):
                    ins = tr(dst[:, P * i:P * (i + 1)], src[:, c % 2, i, :], ident[:, :])
                ins.then_inc(xT_ps[k], 1)

            def qkv(c):
                pe.wait_ge(xn_done[0], c + 1)
                if c:
                    pe.wait_ge(xT_done[0], c)
                transposed_chunk(0, c, xn, bank[0])
                pe.wait_ge(xT_done[0], c + 1)
                if c == 0:
                    pe.wait_ge(wqkv_in, 64)
                else:
                    pe.wait_ge(v_taken, c)
                if c >= 2:
                    pe.wait_ge(resid_done, 2 * (c - 1))
                mm(q_bank(c, 0), w_qkvo[:, 0, :], xTc[c], start=True, stop=True).then_inc(qkv_ps, 1)
                mm(q_bank(c, 1), w_qkvo[:, 1, :], xTc[c], start=True, stop=True).then_inc(qkv_ps, 1)
                for i in range(TPC):
                    ins = mm(bank[3][:, P * i:P * (i + 1)], xTc[c][:, P * i:P * (i + 1)], w_qkvo[:, 2, :],
                             start=(i == 0), stop=(i == TPC - 1), skip_group_check=True)
                ins.then_inc(qkv_ps, 1)

            pe.wait_ge(consts, 2)
            qkv(0)
            qkv(1)

            def slot(n):
                if n >= 2:
                    pe.wait_ge(prep_act, n - 1)
                return prep_bank(n)

            pe.wait_ge(weights_in, 16 * N_WEIGHTS)
            b0 = slot(0)
            for m in range(HT):
                ins = tr(b0[0:RANK, P * m:P * (m + 1)], w_u[:, m, :], ident[:, :])
            ins.then_inc(prep_pe, 1)
            b1 = slot(1)
            tr(b1[0:RANK, 0:RANK], fb[:, :], ident[0:RANK, 0:RANK])
            tr(b1[0:DDIM, 32:32 + LR], l_down[:, :], ident[0:LR, 0:LR])
            tr(b1[0:LR, 64:64 + UDIM], l_up[:, :], ident[0:UDIM, 0:UDIM])
            tr(b1[0:UDIM, P:2 * P], u_aux[:, :], ident[:, :]).then_inc(prep_pe, 1)
            b2 = slot(2)
            for i in range(2):
                tr(b2[:, P * i:P * (i + 1)], w_in[:, 2 + i, :], ident[:, :])
            for i in range(2):
                ins = tr(b2[:, 2 * P + P * i:3 * P + P * i], w_out[:, P * i:P * (i + 1)], ident[:, :])
            ins.then_inc(prep_pe, 1)
            b3 = slot(3)
            for i in range(2):
                tr(b3[:, P * i:P * i + 96], w_x[:, P * i:P * (i + 1)], ident[0:96, 0:96])
            for i in range(2):
                ins = tr(b3[0:DTR, 2 * P + P * i:3 * P + P * i], w_dt[:, i, :], ident[:, :])
            ins.then_inc(prep_pe, 1)
            qkv(2)
            for g in range(2):
                b = slot(4 + g)
                if g == 0:
                    pe.wait_ge(prep_dve, 1)
                for k in range(2):
                    for hf in range(HALVES):
                        o = 2 * P * k + P * hf
                        ins = tr(b[:, o:o + P], w_tap[:, 2 * g + k, hf, :], ident[:, :])
                ins.then_inc(prep_pe, 1)
            qkv(3)
            b6 = slot(6)
            pe.wait_ge(prep_dve, 2)
            for m in range(HT):
                ins = tr(b6[:, P * m:P * (m + 1)], tern_pj[:, P * m:P * (m + 1)], ident[:, :])
            ins.then_inc(prep_pe, 1)
            b7 = slot(7)
            mm(b7[0:RANK, 0:D], fbT[:, :], w_v[:, :], start=True, stop=True)
            mm(b7[0:LR, P:2 * P], ldT[:, :], d_aux[:, :], start=True, stop=True,
               skip_group_check=True).then_inc(prep_pe, 1)
            b8 = slot(8)
            pe.wait_ge(prep_act, 8)
            mm(b8[0:UDIM, 0:D], luT[:, :], r1[:, :], start=True, stop=True).then_inc(prep_pe, 1)
            b9 = slot(9)
            pe.wait_ge(prep_dve, 3)
            for m in range(HT):
                mm(b9[:, P * m:P * (m + 1)], tern_fc[:, m, :], ident[:, :], start=(m == 0), stop=False,
                   skip_group_check=True)
                ins = mm(b9[:, P * m:P * (m + 1)], q1[:, :], uT[:, P * m:P * (m + 1)], start=False,
                         stop=(m == HT - 1), skip_group_check=True)
            ins.then_inc(prep_pe, 1)
            b10 = slot(10)
            pe.wait_ge(prep_act, 9)
            mm(b10[:, 0:D], w_l[:, :], ident[:, :], start=True, stop=False)
            mm(b10[:, 0:D], r2[:, :], uaT[:, :], start=False, stop=True).then_inc(prep_pe, 1)

            pe.wait_ge(xT_done[0], CHUNKS)
            pe.wait_ge(parts_done, 2 * CHUNKS)
            pe.wait_ge(v_taken, CHUNKS)
            pe.wait_ge(prep_act, PREP_SLOTS)
            pe.wait_ge(consts, 10)
            pe.wait_ge(pads, 2)

            def scores(v, p):
                c, quad = unit[v]
                i, n, g = pieces[v][p]
                h, gp = 4 * quad + n, piece_base[v] + p
                if p == 0 and quad == 0:
                    pe.wait_ge(stacked[c], 16 * 4 * ROUND)
                if gp >= 3:
                    pe.wait_ge(scores_max, gp - 2)
                w = CW if g < c else P * (i + 1)
                mm(qk_ps[gp % 3][:, 0:w], qs[0:PAIR, c % 2, h, P * i:P * (i + 1)],
                   ks[0:PAIR, h // 2, CW * g:CW * g + w], start=True, stop=True).then_inc(scores_ps, 1)

            def scores_T(u, j, n):
                c, quad = unit[u]
                g = 4 * (step_base[u] + j) + n
                if g >= 3:
                    pe.wait_ge(exp_done, g - 2)
                q0 = CW - queries(c, j)
                h = 4 * quad + n
                on_diag = j >= TPC * c
                ins = mm(st_bank[g % 3][:, q0:CW], ks[0:AUG, h // 2, P * j:P * (j + 1)],
                         qs[0:AUG, c % 2, h, q0:CW], start=True, stop=not on_diag)
                if on_diag:
                    ins = mm(st_bank[g % 3][:, q0:q0 + P], ident_b[:, :], mask_kq[:, :], start=False, stop=True)
                ins.then_inc(sT_ps, 1)

            def weigh(u, j, part):
                c, quad = unit[u]
                s = step_base[u] + j
                q0 = max(0, P * (j - TPC * c))
                cut = q0 + (CW - q0 + 1) // 2
                lo, hi = (q0, cut) if part == 0 else (cut, CW)
                if part == 0:
                    if j == 0 and u:
                        pe.wait_ge(pv_taken, u)
                    pe.wait_ge(exp_done, 4 * (s + 1))
                for n in range(4):
                    ins = mm(pv_ps[32 * n:32 * n + 32, lo:hi], vaug[:, j, 4 * quad + n, :],
                             probs[:, s % 3, n, lo:hi], start=(j == 0 and part == 0),
                             stop=(j == steps[u] - 1 and part == 1), tile_position=(0, 32 * n),
                             skip_group_check=True)
                if part == 1:
                    ins.then_inc(pv_done, 1)

            def misc_free(job):
                k = misc_order.index(job)
                if k:
                    kind, n = misc_order[k - 1]
                    pe.wait_ge({"max": maxT_done, "out": attn_done, "project": sub_done}[kind], n + 1)

            def turn_max(v):
                pe.wait_ge(max_parts, v + 1)
                misc_free(("max", v))
                m16 = misc.bitcast(BF16)
                for i in range(TPC):
                    ins = tr(m16[0:12, P * i:P * (i + 1)], maxparts[:, v % 2, i, :, :].rearrange("p n s -> p (n s)"),
                             ident_b[:, :])
                ins.then_inc(maxT_ps, 1)

            def turn_out(u):
                pe.wait_ge(pv_taken, u + 1)
                misc_free(("out", u))
                for i in range(TPC):
                    ins = tr(misc[:, P * i:P * (i + 1)], oT[:, u % 2, P * i:P * (i + 1)], ident[:, :])
                ins.then_inc(oT_ps, 1)

            def project_out(c):
                pe.wait_ge(attn_done, QUADS * (c + 1))
                misc_free(("project", c))
                for i in range(TPC):
                    ins = tr(misc[:, P * i:P * (i + 1)], attn[:, c % 2, i, :], ident[:, :])
                ins.then_inc(attnT_ps, 1)
                pe.wait_ge(attnT_done, c + 1)
                for i in range(TPC):
                    ins = mm(misc[:, P * i:P * (i + 1)], attnT[:, P * i:P * (i + 1)], w_qkvo[:, 3, :],
                             start=(i == 0), stop=(i == TPC - 1), skip_group_check=True)
                ins.then_inc(wo_ps, 1)

            for u in range(FIRST):
                for p in range(len(pieces[u])):
                    scores(u, p)
                if u < FIRST - 1:
                    turn_max(u)
            last = None
            for u in range(UNITS):
                pe.wait_ge(max_rows[u % 2], 64 * (u // 2 + 1))
                for j in range(steps[u]):
                    s_ = step_base[u] + j
                    todo = pieces_at[s_]
                    ends, done = (1, 2, 4, 5, 6, 8), 0
                    for k, end in enumerate(ends):
                        if k in (2, 5):
                            if last is not None:
                                weigh(*last, k // 3)
                        else:
                            scores_T(u, j, k if k < 2 else k - 1)
                        upto = (len(todo) * end + 4) // 8
                        for v, p in todo[done:upto]:
                            scores(v, p)
                        done = upto
                    last = (u, j)
                    for v in turn_at[s_]:
                        turn_max(v)
                    if j == 2 and u:
                        turn_out(u - 1)
                    if j == 3 and u and u % QUADS == 0:
                        project_out(u // QUADS - 1)
            weigh(*last, 0)
            weigh(*last, 1)
            turn_out(UNITS - 1)

            def up(c):
                pe.wait_ge(xn_done[1], c + 1)
                if c >= 3:
                    pe.wait_ge(xT_done[2], c - 2)
                transposed_chunk(1, c, xn, bank[0])
                pe.wait_ge(xT_done[1], c + 1)
                for m in range(HT):
                    if HT * c + m >= 2:
                        pe.wait_ge(relu_done, HT * c + m - 1)
                    mm(bank[1 + m % 2], fcT[:, P * m:P * (m + 1)], xTc[c], start=True, stop=True).then_inc(fc_ps, 1)

            def down(c):
                pe.wait_ge(relu2_done, HT * (c + 1))
                if c:
                    pe.wait_ge(x2_done, c)
                for i in range(TPC):
                    for m in range(HT):
                        ins = mm(bank[3][:, P * i:P * (i + 1)], relu2[:, c % 2, m, P * i:P * (i + 1)], pjT[:, m, :],
                                 start=(i == 0 and m == 0), stop=(m == HT - 1), skip_group_check=True)
                ins.then_inc(pj_ps, 1)

            def in_projection(c):
                pe.wait_ge(xT_done[2], c + 1)
                t0 = 4 + CW * c - (CONV - 1)
                for hf in range(HALVES):
                    if c:
                        pe.wait_ge(sp_a_done, 2 * (c - 1) + hf + 1)
                    for k in range(CONV):
                        ins = mm(bank[4 + hf], tapT[:, k, P * hf:P * (hf + 1)], xT[:, t0 + k:t0 + k + CW],
                                 start=(k == 0), stop=(k == CONV - 1))
                    ins.then_inc(pre_ps, 1)
                if c:
                    pe.wait_ge(bnd_b_done, 2 * c)
                    pe.wait_ge(bcs_done, c)
                for hf in range(HALVES):
                    mm(bank[6 + hf], zT[:, P * hf:P * (hf + 1)], xTc[c], start=True, stop=True).then_inc(pre_ps, 1)

            def mamba_transpose(c):
                pe.wait_ge(xn_done[2], c + 1)
                pe.wait_ge(xT_done[1], min(c + 3, CHUNKS))
                transposed_chunk(2, c, attn, bank[0])

            def x_projection(c):
                pe.wait_ge(silu_done, 4 * c + 3)
                for hf in range(HALVES):
                    ins = mm(bank[6][0:DTR, :], wxT[:, hf, 0:DTR], xc[:, hf, CW * c:CW * (c + 1)],
                             start=(hf == 0), stop=(hf == HALVES - 1))
                ins.then_inc(dtl_ps, 1)
                pe.wait_ge(silu_done, 4 * c + 4)
                for hf in range(HALVES):
                    ins = mm(bank[7][0:96, :], wbcT[:, hf, :], xc[:, hf, CW * c:CW * (c + 1)],
                             start=(hf == 0), stop=(hf == HALVES - 1))
                ins.then_inc(bc_ps, 1)
                pe.wait_ge(dtl_done, c + 1)
                for hf in range(HALVES):
                    mm(bank[4 + hf], wdtT[:, P * hf:P * (hf + 1)], dtl[:, c % 2, :], start=True,
                       stop=True).then_inc(dt_ps, 1)
                for i in range(TPC):
                    for hf in range(HALVES):
                        t1 = CW * c + P * i
                        ins = mm(bank[6][:, NST * i:NST * (i + 1)], xc[:, hf, t1:t1 + P], wxT[:, hf, DTR:DTR + NST],
                                 start=(i == 0 and hf == 0), stop=(hf == HALVES - 1), skip_group_check=True)
                ins.then_inc(bt_ps, 1)

            def spread_bmax(c):
                pe.wait_ge(diag_done, c + 1)
                for i in range(TPC):
                    ins = mm(bank[6][:, P * i:P * (i + 1)], ones[:, :], diag[:, i, :], start=(i == 0),
                             stop=(i == TPC - 1), skip_group_check=True)
                ins.then_inc(bm_ps, 1)

            for k in range(ROUNDS):
                if in_round(k, 0):
                    up(k)
                if k == 0:
                    project_out(CHUNKS - 1)
                if k == 2:
                    pe.wait_ge(sub_done, CHUNKS)
                if in_round(k, 3):
                    spread_bmax(k - 3)
                if in_round(k, 1):
                    down(k - 1)
                if in_round(k, 2):
                    mamba_transpose(k - 2)
                    in_projection(k - 2)
                    x_projection(k - 2)
            pe.wait_ge(over_done, 1)
            mm(bank[5][0:1, 0:1], over[:, :], ones[:, 0:1], start=True, stop=True).then_inc(over_ps, 1)

            pe.wait_ge(consts, 14)
            pe.wait_ge(bcs_done, CHUNKS)
            pe.wait_ge(bnd_b_done, 2 * CHUNKS)
            pe.wait_ge(flag_done, 1)
            pe.wait_ge(silu_done, 4 * CHUNKS)

            def spread_b(n_):
                c, n = divmod(n_, NST)
                if n_ >= 2:
                    pe.wait_ge(bu_done, n_ - 1)
                mm(bank[2 + n_ % 2], pick[:, n, :], bcs[:, CW * c:CW * (c + 1)], start=True,
                   stop=True).then_inc(b_ps, 1)

            def spread_c(n_):
                c, n = divmod(n_, NST)
                if n_ >= 2:
                    pe.wait_ge(c_done, n_ - 1)
                mm(bank[4 + n_ % 2], pick[:, NST + n, :], bcs[:, CW * c:CW * (c + 1)], start=True,
                   stop=True).then_inc(c_ps, 1)

            def out_projection(c):
                pe.wait_ge(y_done, 2 * (c + 1))
                for i in range(TPC):
                    t1 = CW * c + P * i
                    for hf in range(HALVES):
                        ins = mm(y_bank(c, 0)[:, P * i:P * (i + 1)], sz[:, hf, t1:t1 + P], woutT[:, hf, :],
                                 start=(i == 0 and hf == 0), stop=(hf == HALVES - 1), skip_group_check=True)
                ins.then_inc(yout_ps, 1)

            def last_transpose(c):
                pe.wait_ge(xn_done[3], c + 1)
                transposed_chunk(3, c, xn, y_bank(c, 1))

            def last_linear(c):
                pe.wait_ge(xT_done[3], c + 1)
                pe.wait_ge(x3_done, c + 1)
                for i in range(TPC):
                    mm(y_bank(c, 0)[:, P * i:P * (i + 1)], xTc[c][:, P * i:P * (i + 1)], wlT[:, :],
                       start=(i == 0), stop=False, skip_group_check=True)
                    ins = mm(y_bank(c, 0)[:, P * i:P * (i + 1)], ones[0:1, :], b_l[0:1, :],
                             start=False, stop=(i == TPC - 1), skip_group_check=True)
                ins.then_inc(fin_ps, 1)

            for n_ in range(AHEAD):
                spread_b(n_)
                spread_c(n_)
            for n_ in range(CHUNKS * NST):
                c, n = divmod(n_, NST)
                for hf in range(HALVES):
                    m = 2 * n_ + hf
                    if n == 0 and c >= 2:
                        pe.wait_ge(x4_done, c - 1)
                    pe.wait_ge(hc_done, m + 1)
                    mm(y_bank(c, hf), ident[:, :], hc_ring[m % NH], start=(n == 0),
                       stop=(n == NST - 1)).then_inc(hc_used, 1)
                    if n_ + AHEAD < CHUNKS * NST:
                        (spread_b if hf == 0 else spread_c)(n_ + AHEAD)
                if c and n == YOUT_AT:
                    out_projection(c - 1)
                if c and n == XT3_AT:
                    last_transpose(c - 1)
                if c and n == FIN_AT:
                    last_linear(c - 1)

            out_projection(CHUNKS - 1)
            last_transpose(CHUNKS - 1)
            last_linear(CHUNKS - 1)

        @block.scalar
        def _(act):
            f = nc.scalar.activation

            def ln_rstd(k, c):
                t = TILES * k + TPC * c
                act.wait_ge(moments_of[k], c + 1)
                f(lnvar[:, t:t + TPC], moments[:, t:t + TPC, 1], ACT.Ln, bias=eps_col[:, 0:1]).then_inc(lnvar_of[k], 1)
                act.wait_ge(lnvar_of[k], c + 1)
                f(rstd[:, t:t + TPC], lnvar[:, t:t + TPC], ACT.Exp, scale=-0.5).then_inc(rstd_of[k], 1)

            def take_xT(k, c, src):
                act.wait_ge(xT_ps[k], c + 1)
                f(xTc[c], src, ACT.Copy).then_inc(xT_done[k], 1)

            nc.scalar.preload_act_table_set("natural_log_exp_and_others")
            act.wait_ge(eps_set, 1)
            for c in range(CHUNKS):
                ln_rstd(0, c)

            def take_qkv(c):
                take_xT(0, c, bank[0])
                if c >= 2:
                    act.wait_ge(parts_stored[c - 2], 32)
                for m in range(2):
                    act.wait_ge(qkv_ps, 3 * c + m + 1)
                    f(parts[:, c % 2, m, 0, :], q_bank(c, m), ACT.Copy).then_inc(hi_done, 1)
                act.wait_ge(qkv_ps, 3 * c + 3)
                act.wait_ge(consts, 10)
                f(vaug[:, TPC * c:TPC * (c + 1), :, 0:DK],
                  bank[3].rearrange("p (i h d) -> p i h d", i=TPC, h=HEADS), ACT.Copy).then_inc(v_taken, 1)

            def middle_parts(c):
                for m in range(2):
                    act.wait_ge(resid_done, 2 * c + m + 1)
                    f(parts[:, c % 2, m, 1, :], resid[:, m, :], ACT.Copy).then_inc(mid_done, 1)

            take_qkv(0)
            take_qkv(1)
            middle_parts(0)

            def took(ins):
                ins.then_inc(prep_act, 1)

            act.wait_ge(weights_in, 16 * N_WEIGHTS)
            f(neg_a[:, :, :], a_log[:, :, :], ACT.Exp).then_inc(act_step, 1)
            act.wait_ge(prep_pe, 1)
            took(f(uT[:, :], prep_bank(0)[0:RANK, :], ACT.Copy))
            act.wait_ge(prep_pe, 2)
            b1 = prep_bank(1)
            f(fbT[:, :], b1[0:RANK, 0:RANK], ACT.Copy)
            f(ldT[:, :], b1[0:DDIM, 32:32 + LR], ACT.Copy)
            f(luT[:, :], b1[0:LR, 64:64 + UDIM], ACT.Copy)
            took(f(uaT[:, :], b1[0:UDIM, P:2 * P], ACT.Copy))
            act.wait_ge(prep_pe, 3)
            b2 = prep_bank(2)
            f(zT[:, :], b2[:, 0:2 * P], ACT.Copy)
            took(f(woutT[:, :, :].rearrange("p h e -> p (h e)"), b2[:, 2 * P:4 * P], ACT.Copy))
            act.wait_ge(prep_pe, 4)
            b3 = prep_bank(3)
            wx_ps = b3[:, 0:2 * P].rearrange("p (h e) -> p h e", h=2)
            f(wxT[:, :, :], wx_ps[:, :, 0:96], ACT.Copy)
            for g in range(3):
                f(wbcT[:, :, 32 * g:32 * (g + 1)], wx_ps[:, :, DTR:96], ACT.Copy)
            took(f(wdtT[:, :], b3[0:DTR, 2 * P:4 * P], ACT.Copy))
            take_qkv(2)
            middle_parts(1)
            for g in range(2):
                act.wait_ge(prep_pe, 5 + g)
                took(f(tapT[:, 2 * g:2 * g + 2, :].rearrange("p k d -> p (k d)"), prep_bank(4 + g), ACT.Copy))
            take_qkv(3)
            act.wait_ge(prep_pe, 7)
            took(f(pjT[:, :, :].rearrange("p m e -> p (m e)"), prep_bank(6), ACT.Copy))
            act.wait_ge(prep_pe, 8)
            f(q1[:, :], prep_bank(7)[0:RANK, 0:D], ACT.Copy, scale=gate[0:RANK, 0:1])
            took(f(r1[:, :], prep_bank(7)[0:LR, P:2 * P], ACT.Copy))
            act.wait_ge(prep_pe, 9)
            took(f(r2[:, :], prep_bank(8)[0:UDIM, 0:D], ACT.Copy))
            middle_parts(2)
            middle_parts(3)
            act.wait_ge(prep_pe, 10)
            took(f(fcT[:, :], prep_bank(9), ACT.Copy))
            act.wait_ge(prep_pe, 11)
            took(f(wlT[:, :], prep_bank(10)[:, 0:D], ACT.Copy))

            def take_max(u):
                act.wait_ge(maxT_ps, u + 1)
                if u >= 2:
                    act.wait_ge(max_rows[u % 2], 64 * (u // 2))
                f(maxT[:, u % 2, :], misc.bitcast(BF16)[0:12, 0:CW], ACT.Copy).then_inc(maxT_done, 1)

            def take_out(u):
                act.wait_ge(pv_done, step_base[u + 1])
                if u >= 2:
                    act.wait_ge(oT_ps, u - 1)
                f(oT[:, u % 2, :], pv_ps, ACT.Copy).then_inc(pv_taken, 1)

            def take_projection(c):
                act.wait_ge(attnT_ps, c + 1)
                if c:
                    act.wait_ge(wo_ps, c)
                f(attnT[:, :], misc, ACT.Copy).then_inc(attnT_done, 1)
                act.wait_ge(wo_ps, c + 1)
                f(sub[:, TPC * c:TPC * (c + 1), :].rearrange("p i e -> p (i e)"), misc,
                  ACT.Copy).then_inc(sub_done, 1)

            for u in range(FIRST - 1):
                take_max(u)
            for u, (c, _) in enumerate(unit):
                for j in range(steps[u]):
                    s_ = step_base[u] + j
                    q0 = max(0, P * (j - TPC * c))
                    for n in range(4):
                        act.wait_ge(sT_ps, 4 * s_ + n + 1)
                        if s_ >= 3:
                            act.wait_ge(pv_done, s_ - 2)
                        f(probs[:, s_ % 3, n, q0:CW], st_bank[(4 * s_ + n) % 3][:, q0:CW],
                          ACT.Exp, scale=DK ** -0.5).then_inc(exp_done, 1)
                    if j == 0 and u:
                        take_out(u - 1)
                    for v in turn_at[s_]:
                        take_max(v)
                    if j == 3 and u and u % QUADS == 0:
                        take_projection(u // QUADS - 1)
                    if s_ in EARLY:
                        for c2 in range(CHUNKS - 1):
                            ln_rstd(1 + EARLY.index(s_), c2)
            take_out(UNITS - 1)

            for k in range(ROUNDS):
                if in_round(k, 0):
                    take_xT(1, k, bank[0])
                    if k == 2:
                        ln_rstd(3, 0)
                    for m in range(HT):
                        act.wait_ge(fc_ps, HT * k + m + 1)
                        if k:
                            act.wait_ge(relu2_done, HT * (k - 1) + m + 1)
                        f(relu[:, m, :], bank[1 + m % 2], ACT.Relu).then_inc(relu_done, 1)
                        if k == 2 and m == 1:
                            ln_rstd(4, 0)
                    if k == 0:
                        take_projection(CHUNKS - 1)
                    if k == 1:
                        ln_rstd(1, CHUNKS - 1)
                        ln_rstd(2, CHUNKS - 1)
                if in_round(k, 2):
                    take_xT(2, k - 2, bank[0])
                if in_round(k, 3):
                    c = k - 3
                    for hf in range(HALVES):
                        act.wait_ge(delta_done, 2 * c + hf + 1)
                        if c:
                            act.wait_ge(bnd_done, 2 * (c - 1) + hf + 1)
                        act.wait_ge(prep_dve, 4)
                        f(bnd_a[:, hf, :], delta[:, hf, CW * c:CW * (c + 1)], ACT.Exp,
                          scale=a_max[:, hf:hf + 1]).then_inc(bnd_exp, 1)
                    for hf in range(HALVES):
                        act.wait_ge(bnd_b_done, 2 * c + hf + 1)
                        f(bnd_h[:, hf, :], bnd_b[:, hf, :], ACT.Abs).then_inc(bnd_abs, 1)
                if in_round(k, 1) and k > 1:
                    ln_rstd(3, k - 1)
                    ln_rstd(4, k - 1)
                if in_round(k, 2):
                    c = k - 2
                    t = slice(CW * c, CW * (c + 1))
                    nc.scalar.preload_act_table_set("silu_and_others")
                    for hf in range(HALVES):
                        act.wait_ge(pre_ps, 4 * c + hf + 1)
                        f(xc[:, hf, t], bank[4 + hf], ACT.Silu, bias=conv_b[:, hf:hf + 1]).then_inc(silu_done, 1)
                    for hf in range(HALVES):
                        act.wait_ge(pre_ps, 4 * c + hf + 3)
                        f(sz[:, hf, t], bank[6 + hf], ACT.Silu).then_inc(silu_done, 1)
                    nc.scalar.preload_act_table_set("natural_log_exp_and_others")
                    act.wait_ge(dtl_ps, c + 1)
                    if c >= 2:
                        act.wait_ge(dt_ps, 2 * (c - 1))
                    f(dtl[:, c % 2, :], bank[6][0:DTR, :], ACT.Copy).then_inc(dtl_done, 1)
                    for hf in range(HALVES):
                        act.wait_ge(sp_a_done, 2 * c + hf + 1)
                        f(sp_b[:, hf, :], sp_a[:, hf, :], ACT.Exp).then_inc(sp_exp, 1)
                    for hf in range(HALVES):
                        act.wait_ge(sp_exp, 2 * c + hf + 1)
                        f(sp_a[:, hf, :], sp_b[:, hf, :], ACT.Ln, bias=1.0).then_inc(sp_ln, 1)

            for n_ in range(CHUNKS * NST):
                c, n = divmod(n_, NST)
                act.wait_ge(c_ps, n_ + 1)
                if n_ >= NC_RING:
                    act.wait_ge(hc_done, 2 * (n_ - NC_RING) + 2)
                f(c_ring[n_ % NC_RING], bank[4 + n_ % 2], ACT.Copy).then_inc(c_done, 1)
                for hf in range(HALVES):
                    m = 2 * n_ + hf
                    if m >= NA:
                        act.wait_ge(h_done, m - NA + 1)
                    f(a_ring[m % NA], delta[:, hf, CW * c:CW * (c + 1)], ACT.Exp,
                      scale=neg_a[:, hf, n:n + 1]).then_inc(decay_done, 1)

                if c and n == RSTD5_AT:
                    ln_rstd(5, c - 1)
                if c and n == RSTD6_AT:
                    ln_rstd(6, c - 1)
                if c and n == TAKE3_AT:
                    take_xT(3, c - 1, y_bank(c - 1, 1))
                if c and n == RSTD7_AT:
                    ln_rstd(7, c - 1)
            ln_rstd(5, CHUNKS - 1)
            ln_rstd(6, CHUNKS - 1)
            take_xT(3, CHUNKS - 1, y_bank(CHUNKS - 1, 1))
            ln_rstd(7, CHUNKS - 1)

        @block.vector
        def _(dve):
            v = nc.vector
            step = [0]

            def chained(ins):
                ins.then_inc(dve_step, 1)
                step[0] += 1
                dve.wait_ge(dve_step, step[0])

            def ln_stats(k, c, tile_of):
                t = TILES * k + TPC * c
                for i in range(TPC):
                    ins = v.bn_stats(stats[:, t % (2 * TILES) + i, :], tile_of(i))
                ins.then_inc(stats_of[k], 1)
                dve.wait_ge(stats_of[k], c + 1)
                for i in range(TPC):
                    ins = v.bn_aggr(moments[:, t + i, :], stats[:, t % (2 * TILES) + i, :])
                ins.then_inc(moments_of[k], 1)

            def normalised(k, c, tile_of, out):
                t = TILES * k + TPC * c
                dve.wait_ge(rstd_of[k], c + 1)
                for i in range(TPC):
                    ins = v.tensor_scalar(out[:, c % 2, i, :], tile_of(i), moments[:, t + i, 0:1],
                                          rstd[:, t + i:t + i + 1], ALU.subtract, ALU.mult)
                return ins

            def x_tile(c):
                return lambda i: x[:, TPC * c + i, :]

            def ps_tile(b):
                return lambda i: b[:, P * i:P * (i + 1)]

            def pre_stats(k, c):
                ln_stats(k, c, x_tile(c))

            def pre_norm(k, j, c):
                if c >= 2:
                    dve.wait_ge(xT_ps[j], c - 1)
                normalised(k, c, x_tile(c), attn if j == 2 else xn).then_inc(xn_done[j], 1)

            def post_norm(k, c, tile_of, done):
                chained(normalised(k, c, tile_of, nrm))
                xs = x[:, TPC * c:TPC * (c + 1), :]
                v.tensor_tensor(xs, xs, nrm[:, c % 2, :, :], ALU.add).then_inc(done, 1)
                dve.wait_ge(done, c + 1)

            v.memset(eps_col[:, :], EPS).then_inc(eps_set, 1)

            def residual(c):
                if c:
                    dve.wait_ge(parts_done, 2 * c)
                for m in range(2):
                    dve.wait_ge(hi_done, 2 * c + m + 1)
                    v.tensor_tensor(resid[:, m, :], q_bank(c, m), parts[:, c % 2, m, 0, :],
                                    ALU.subtract).then_inc(resid_done, 1)

            def low_parts(c):
                for m in range(2):
                    dve.wait_ge(mid_done, 2 * c + m + 1)
                    v.tensor_tensor(parts[:, c % 2, m, 2, :], resid[:, m, :], parts[:, c % 2, m, 1, :],
                                    ALU.subtract).then_inc(parts_done, 1)

            for c in range(CHUNKS):
                dve.wait_ge(x_in[c], 16)
                pre_stats(0, c)
            pre_norm(0, 0, 0)
            pre_norm(0, 0, 1)
            residual(0)
            pre_norm(0, 0, 2)
            low_parts(0)
            residual(1)

            dve.wait_ge(weights_in, 16 * N_WEIGHTS)
            for k in range(CONV):
                for hf in range(HALVES):
                    ins = v.tensor_scalar(w_tap[:, k, hf, :], w_in[:, hf, :], conv_w[:, hf, k:k + 1], None, ALU.mult)
            ins.then_inc(prep_dve, 1)
            low_parts(1)
            pre_norm(0, 0, 3)
            v.tensor_reduce(scl[:, 0, 0:HT], w_fc[:, :, :], AX.X, ALU.add, apply_absolute_value=True)
            chained(v.tensor_reduce(scl[:, 0, HT:HT + 1], w_pj[:, :], AX.X, ALU.add, apply_absolute_value=True))
            v.tensor_scalar(scl[:, 1, 0:HT], scl[:, 0, 0:HT], 1.0 / D, EPS, ALU.mult, ALU.max)
            chained(v.tensor_scalar(scl[:, 1, HT:HT + 1], scl[:, 0, HT:HT + 1], 1.0 / HIDDEN, EPS, ALU.mult, ALU.max))
            chained(v.tensor_scalar(scl[:, 2, :], scl[:, 1, :], 0.5, None, ALU.mult))
            chained(v.tensor_scalar(scl[:, 0, :], scl[:, 1, :], -0.5, None, ALU.mult))

            def ternary(out, w, col):
                n = w.shape[1]
                chained(v.tensor_scalar(tmp_w[:, 0, 0:n], w, scl[:, 2, col:col + 1], None, ALU.is_gt))
                chained(v.scalar_tensor_tensor(tmp_w[:, 1, 0:n], w, scl[:, 0, col:col + 1], tmp_w[:, 0, 0:n],
                                               ALU.is_lt, ALU.subtract))
                chained(v.scalar_tensor_tensor(tmp_w[:, 0, 0:n], tmp_w[:, 1, 0:n], -1.0, w, ALU.mult, ALU.subtract))
                chained(v.tensor_tensor(tmp_w[:, 1, 0:n], w, tmp_w[:, 0, 0:n], ALU.add))
                return v.tensor_scalar(out, tmp_w[:, 1, 0:n], scl[:, 1, col:col + 1], None, ALU.mult)

            ternary(tern_pj[:, :], w_pj[:, :], HT).then_inc(prep_dve, 1)
            dve.wait_ge(prep_dve, 2)
            for m in range(HT):
                ins = ternary(tern_fc[:, m, :], w_fc[:, m, :], m)
                if m < HT - 1:
                    chained(ins)
            ins.then_inc(prep_dve, 1)
            dve.wait_ge(act_step, 1)
            chained(v.tensor_scalar(neg_a[:, :, :], neg_a[:, :, :], -1.0, None, ALU.mult))
            v.tensor_reduce(a_max[:, :], neg_a[:, :, :], AX.X, ALU.max).then_inc(prep_dve, 1)
            residual(2)
            low_parts(2)
            residual(3)
            low_parts(3)

            def piece_max(w_, p):
                c, _ = unit[w_]
                i, n, g = pieces[w_][p]
                gp = piece_base[w_] + p
                dve.wait_ge(scores_ps, gp + 1)
                if gp >= 2:
                    dve.wait_ge(scores_max, gp - 1)
                out = maxcol[:, w_ % 2, i, n, g:g + 1]
                src = qk_ps[gp % 3]
                if g < c:
                    v.reduce_max(out, src, AX.X).then_inc(scores_max, 1)
                else:
                    w = P * (i + 1)
                    v.tensor_tensor_reduce(junk[:, gp % 2, 0:w], src[:, 0:w], mask_qk[:, CW - w:CW], 1.0, LOWEST,
                                           ALU.add, ALU.max, out).then_inc(scores_max, 1)

            def finish_max(w_):
                b = w_ % 2
                dve.wait_ge(scores_max, piece_base[w_ + 1])
                if w_ >= 2:
                    dve.wait_ge(maxT_ps, w_ - 1)
                chained(v.tensor_reduce(rowmax[:, b, :, :], maxcol[:, b, :, :, 0:unit[w_][0] + 1], AX.X, ALU.max))
                chained(v.tensor_scalar(maxparts[:, b, :, :, 0], rowmax[:, b, :, :], -1.0, None, ALU.mult))
                chained(v.scalar_tensor_tensor(maxres[:, b, :, :], rowmax[:, b, :, :], -1.0, maxparts[:, b, :, :, 0],
                                               ALU.mult, ALU.subtract))
                chained(v.tensor_copy(maxparts[:, b, :, :, 1], maxres[:, b, :, :]))
                v.tensor_tensor(maxparts[:, b, :, :, 2], maxres[:, b, :, :], maxparts[:, b, :, :, 1],
                                ALU.subtract).then_inc(max_parts, 1)

            def take_heads(u):
                c, quad = unit[u]
                o = misc.rearrange("p (i n e) -> p i n e", i=TPC, n=4)
                dve.wait_ge(oT_ps, u + 1)
                if c >= 2:
                    dve.wait_ge(attnT_ps, c - 1)
                chained(v.reciprocal(rsum[:, u % 2, :, :], o[:, :, :, DK]))
                v.tensor_tensor(attn[:, c % 2, :, 32 * quad:32 * quad + 32].rearrange("p i (n d) -> p i n d", n=4),
                                o[:, :, :, 0:DK],
                                rsum[:, u % 2, :, :].rearrange("p i (n a) -> p i n a", a=1).to_broadcast([P, TPC, 4, DK]),
                                ALU.mult).then_inc(attn_done, 1)

            def attention_stats(c):
                dve.wait_ge(sub_done, c + 1)
                ln_stats(1, c, lambda i: sub[:, TPC * c + i, :])

            def attention_norm(c):
                post_norm(1, c, lambda i: sub[:, TPC * c + i, :], x1_done)
                pre_stats(2, c)

            dve.wait_ge(consts, 10)
            for u in range(FIRST):
                for p in range(len(pieces[u])):
                    piece_max(u, p)
                finish_max(u)
            for u in range(UNITS):
                for j in range(steps[u]):
                    for w_, p in pieces_at[step_base[u] + j]:
                        piece_max(w_, p)
                        if p == len(pieces[w_]) - 1:
                            finish_max(w_)
                    if j == 2 and u:
                        take_heads(u - 1)
                    if step_base[u] + j == EARLY[0]:
                        for c in range(CHUNKS - 1):
                            attention_stats(c)
                        for c in range(CHUNKS - 1):
                            attention_norm(c)
                    if step_base[u] + j == EARLY[1]:
                        for c in range(2):
                            pre_norm(2, 1, c)
            take_heads(UNITS - 1)

            def split_bc(c):
                t = slice(CW * c, CW * (c + 1))
                dve.wait_ge(bc_ps, c + 1)
                chained(v.tensor_copy(bc_hi[:, :], bank[7][0:96, :]))
                chained(v.tensor_tensor(bc_r[:, :], bank[7][0:96, :], bc_hi[:, :], ALU.subtract))
                chained(v.tensor_copy(bc_mid[:, :], bc_r[:, :]))
                v.tensor_copy(bcs[0:32, t], bc_hi[0:32, :])
                v.tensor_copy(bcs[32:64, t], bc_mid[32:64, :])
                v.tensor_tensor(bcs[64:96, t], bc_r[64:96, :], bc_mid[64:96, :], ALU.subtract).then_inc(bcs_done, 1)

            def largest_b(c):
                dve.wait_ge(bt_ps, c + 1)
                chained(v.tensor_reduce(bmax[:, c, :], bank[6][:, 0:TPC * NST].rearrange("p (i n) -> p i n", i=TPC),
                                        AX.X, ALU.max, apply_absolute_value=True))
                if c:
                    dve.wait_ge(bm_ps, c)
                for i in range(TPC):
                    ins = v.tensor_scalar(diag[:, i, :], ident[:, :], bmax[:, c, i:i + 1], None, ALU.mult)
                ins.then_inc(diag_done, 1)

            def take_dt(c):
                for hf in range(HALVES):
                    dve.wait_ge(dt_ps, 2 * c + hf + 1)
                    v.tensor_scalar(sp_a[:, hf, :], bank[4 + hf], b_dt[:, hf:hf + 1], 20.0, ALU.add,
                                    ALU.min).then_inc(sp_a_done, 1)

            def take_delta(c):
                for hf in range(HALVES):
                    dve.wait_ge(sp_ln, 2 * c + hf + 1)
                    v.tensor_scalar(delta[:, hf, CW * c:CW * (c + 1)], sp_a[:, hf, :], 1e-4, 10.0, ALU.add,
                                    ALU.min).then_inc(delta_done, 1)
                for hf in range(HALVES):
                    t = slice(CW * c, CW * (c + 1))
                    dve.wait_ge(delta_done, 2 * c + hf + 1)
                    v.tensor_tensor(dxc[:, hf, t], delta[:, hf, t], xc[:, hf, t], ALU.mult).then_inc(dxc_done, 1)

            def bound_input(c):
                dve.wait_ge(bm_ps, c + 1)
                for hf in range(HALVES):
                    dve.wait_ge(dxc_done, 2 * c + hf + 1)
                    v.tensor_tensor(bnd_b[:, hf, :], dxc[:, hf, CW * c:CW * (c + 1)], bank[6],
                                    ALU.mult).then_inc(bnd_b_done, 1)

            def bound_scan(c):
                for hf in range(HALVES):
                    dve.wait_ge(bnd_abs, 2 * c + hf + 1)
                    dve.wait_ge(bnd_exp, 2 * c + hf + 1)
                    ins = v.tensor_scalar(bnd_h[:, hf, :], bnd_h[:, hf, :], 10.0, None, ALU.min)
                chained(ins)
                for hf in range(HALVES):
                    ins = v.tensor_tensor_scan(bnd_b[:, hf, :], bnd_a[:, hf, :], bnd_h[:, hf, :],
                                               bnd_c[:, hf:hf + 1] if c else 0.0, ALU.mult, ALU.add)
                chained(ins)
                for hf in range(HALVES):
                    v.tensor_copy(bnd_c[:, hf:hf + 1], bnd_b[:, hf, CW - 1:CW])
                    v.reduce_max(bnd_m[:, c, hf:hf + 1], bnd_b[:, hf, :], AX.X).then_inc(bnd_done, 1)
                dve.wait_ge(bnd_done, 2 * (c + 1))

            for k in range(ROUNDS):
                if k == 0:
                    pre_norm(2, 1, 2)
                    attention_stats(CHUNKS - 1)
                    attention_norm(CHUNKS - 1)
                if k == 1:
                    pre_norm(2, 1, 3)
                if in_round(k, 3):
                    bound_input(k - 3)
                if in_round(k, 1):
                    dve.wait_ge(pj_ps, k)
                    ln_stats(3, k - 1, ps_tile(bank[3]))
                    post_norm(3, k - 1, ps_tile(bank[3]), x2_done)
                    pre_stats(4, k - 1)
                    pre_norm(4, 2, k - 1)
                if in_round(k, 3):
                    bound_scan(k - 3)
                if in_round(k, 2):
                    take_dt(k - 2)
                    largest_b(k - 2)
                    split_bc(k - 2)
                    take_delta(k - 2)
            chained(v.tensor_reduce(bmax[:, 0, 0:1], bnd_m[:, :, :], AX.XY, ALU.max))
            v.tensor_scalar(over[:, :], bmax[:, 0, 0:1], H_BOUND, None, ALU.is_le).then_inc(over_done, 1)
            dve.wait_ge(over_ps, 1)
            v.tensor_copy(over_i[:, :], bank[5][0:1, 0:1]).then_inc(flag_done, 1)
            dve.wait_ge(flag_done, 1)
            sure = dve.value_load(over_i[0:1, 0:1])

            def scan_input(n_):
                c = n_ // NST
                dve.wait_ge(b_ps, n_ + 1)
                if n_ >= NB:
                    dve.wait_ge(h_done, 2 * (n_ - NB + 1))
                v.tensor_tensor(bu_ring[n_ % NB], dxc[:, :, CW * c:CW * (c + 1)],
                                bank[2 + n_ % 2].rearrange("p (a t) -> p a t", a=1).to_broadcast([P, HALVES, CW]),
                                ALU.mult).then_inc(bu_done, 1)

            def clip_input(n_):
                b = bu_ring[n_ % NB]
                dve.wait_ge(bu_done, n_ + 1)
                v.tensor_scalar(b, b, 10.0, -10.0, ALU.min, ALU.max).then_inc(clip_done, 1)

            def ready_for_scan(m):
                dve.wait_ge(clip_done, m // 2 + 1)
                dve.wait_ge(decay_done, m + 1)
                if m >= NH:
                    dve.wait_ge(hc_done, m - NH + 1)

            def start_of(m):
                n_, hf = divmod(m, 2)
                return carry[:, hf, n_ % NST:n_ % NST + 1]

            def finish_y(c):
                t = slice(CW * c, CW * (c + 1))
                for hf in range(HALVES):
                    dve.wait_ge(hc_used, 2 * NST * (c + 1) - 1 + hf)
                    ins = v.scalar_tensor_tensor(y_a[:, hf, :], xc[:, hf, t], d_par[:, hf:hf + 1], y_bank(c, hf),
                                                 ALU.mult, ALU.add)
                    ins.then_inc(y_sum, 1)
                for hf in range(HALVES):
                    dve.wait_ge(y_sum, 2 * c + hf + 1)
                    v.tensor_scalar(y_b[:, hf, :], y_a[:, hf, :], 50.0, -50.0, ALU.min, ALU.max).then_inc(y_clip, 1)
                for hf in range(HALVES):
                    dve.wait_ge(y_clip, 2 * c + hf + 1)
                    v.tensor_tensor(sz[:, hf, t], y_b[:, hf, :], sz[:, hf, t], ALU.mult).then_inc(y_done, 1)

            def finish_chunk(c, r):
                if r == Y_LAG:
                    finish_y(c)
                if r == STATS5:
                    dve.wait_ge(yout_ps, c + 1)
                    ln_stats(5, c, ps_tile(y_bank(c, 0)))
                if r == NORM5:
                    post_norm(5, c, ps_tile(y_bank(c, 0)), x3_done)
                    pre_stats(6, c)
                if r == NORM6:
                    pre_norm(6, 3, c)
                if r == STATS7:
                    dve.wait_ge(fin_ps, c + 1)
                    ln_stats(7, c, ps_tile(y_bank(c, 0)))
                if r == NORM7:
                    post_norm(7, c, ps_tile(y_bank(c, 0)), x4_done)

            M = CHUNKS * NST * HALVES
            v.memset(carry[:, :, :], 0.0).then_inc(carry_set, 1)
            dve.wait_ge(carry_set, 1)

            def steps_of_scan(scan):
                scan_input(0)
                clip_input(0)
                for m in range(M):
                    n_, hf = divmod(m, 2)
                    if n_ + 1 < CHUNKS * NST and hf == 0:
                        scan_input(n_ + 1)
                    if n_ + 1 < CHUNKS * NST and hf == 1:
                        clip_input(n_ + 1)
                    ready_for_scan(m)
                    scan(m)
                    c, r = divmod(m, NST * HALVES)
                    if c:
                        finish_chunk(c - 1, r)
                for r in (Y_LAG, STATS5, NORM5, NORM6, STATS7, NORM7):
                    finish_chunk(CHUNKS - 1, r)

            def plain_scan(m):
                v.tensor_tensor_scan(h_ring[m % NH], a_ring[m % NA], bu_ring[m // 2 % NB][:, m % 2, :], start_of(m), ALU.mult,
                                     ALU.add).then_inc(h_done, 1)

            def clipped_scan(m):
                h, dec, bu = h_ring[m % NH], a_ring[m % NA], bu_ring[m // 2 % NB][:, m % 2, :]
                dve.drain()
                v.tensor_copy(h_last[:, :], start_of(m))
                dve.drain()
                with dve.Fori(0, CW) as i:
                    v.scalar_tensor_tensor(h_next[:, :], dec[:, bass.ds(i, 1)], h_last[:, 0:1], bu[:, bass.ds(i, 1)],
                                           ALU.mult, ALU.add)
                    dve.drain()
                    v.tensor_scalar(h_last[:, :], h_next[:, :], 20.0, -20.0, ALU.min, ALU.max)
                    dve.drain()
                    v.tensor_copy(h[:, bass.ds(i, 1)], h_last[:, :])
                dve.drain()
                v.tensor_copy(h_next[:, :], h_last[:, :]).then_inc(h_done, 1)

            before = step[0]
            with dve.If(sure == P):
                steps_of_scan(plain_scan)
            with dve.Else():
                step[0] = before
                steps_of_scan(clipped_scan)


_INS = ['L0_attn_x', 'L0_attn_WQ', 'L0_attn_WK', 'L0_attn_WV', 'L0_attn_WO', 'L0_ffn_fast_b', 'L0_ffn_w_fc',
        'L0_ffn_w_proj', 'L0_ffn_u', 'L0_ffn_v', 'L0_ffn_gate', 'L1_attn_W_in', 'L1_attn_conv_w', 'L1_attn_conv_b',
        'L1_attn_W_x', 'L1_attn_W_dt', 'L1_attn_b_dt', 'L1_attn_A_log', 'L1_attn_D_param', 'L1_attn_W_out',
        'L1_ffn_W', 'L1_ffn_b', 'L1_ffn_lora_down', 'L1_ffn_lora_up', 'L1_ffn_down_aux', 'L1_ffn_up_aux']


def kernel(**inputs):
    import numpy as np
    import concourse.bacc as bacc
    from concourse.bass_utils import run_bass_kernel_spmd as run

    nc = bacc.Bacc("TRN2", target_bir_lowering=False, num_devices=1)
    arrays, aps = {}, {}
    for name in _INS:
        arr = np.ascontiguousarray(inputs[name]).reshape(np.shape(inputs[name]) or (1, 1))
        arrays[f"in_{name}"] = arr
        aps[name] = nc.dram_tensor(f"in_{name}", arr.shape, mybir.dt.from_np(arr.dtype), kind="ExternalInput").ap()
    aps["out"] = nc.dram_tensor("out_x", (1, S, D), F32, kind="ExternalOutput").ap()
    build(nc, aps)
    return run(nc, [arrays], core_ids=[0]).results[0]["out_x"]
```
